# Optimizing a Trainium2 kernel written in Bass

```python
import numpy as np
import jax
import jax.numpy as jnp

def _softmax(x, axis=-1):
    return jax.nn.softmax(x, axis=axis)

def _gelu(x):
    return jax.nn.gelu(x, approximate=True)

def _silu(x):
    return jax.nn.silu(x)

def _sigmoid(x):
    return jax.nn.sigmoid(x)

def _layernorm(x, axis=-1, eps=1e-05):
    m = jnp.mean(x, axis=axis, keepdims=True)
    v = jnp.var(x, axis=axis, keepdims=True)
    return (x - m) / jnp.sqrt(v + eps)

def _scatter_add(tgt, idx, src, axis=0):
    return tgt.at[idx].add(src)

def _segment_sum(src, seg, n):
    return jax.ops.segment_sum(src, seg, n)
kernel_name = 'mk_gnn_ffn_d2_gnn_r8_f4d925'

def setup_inputs(seed: int=0):
    np.random.seed(seed)
    _w = jnp.asarray

    def _rec_inputs():
        import jax
        import jax.numpy as jnp
        _gk = jax.random.key(seed)
        x = -0.0001126 + 1 * jax.random.normal(jax.random.fold_in(_gk, 1), (3750, 256), jnp.float32)
        src = jax.random.randint(jax.random.fold_in(_gk, 2), (60000,), 0, 3750, jnp.int32)
        dst = jax.random.randint(jax.random.fold_in(_gk, 3), (60000,), 0, 3750, jnp.int32)
        _o = jnp.argsort(dst, stable=True)
        src = src[_o]
        dst = dst[_o]
        edge_type_3 = jax.random.randint(jax.random.fold_in(_gk, 13), (60000,), 0, 3, jnp.int32)
        edge_type_8 = jax.random.randint(jax.random.fold_in(_gk, 14), (60000,), 0, 8, jnp.int32)
        return (x, src, dst, edge_type_3, edge_type_8)
    x, src, dst, edge_type_3, edge_type_8 = _rec_inputs()

    def _L0_gnn_setup():
        import jax, jax.numpy as jnp
        import numpy as np
        N_NODES = 3750
        N_EDGES = 60000
        IN_FEAT = 256
        OUT_FEAT = 256
        N_RELS = 8
        N_HEADS = 4
        HEAD_DIM = OUT_FEAT // N_HEADS
        LEAKY_SLOPE = 0.2
        key = jax.random.key(seed)
        ks = jax.random.split(key, 8)
        inputs = jax.random.normal(ks[0], (N_NODES, IN_FEAT), dtype=jnp.float32)
        conv_weights = jax.random.normal(ks[1], (N_RELS, N_HEADS, IN_FEAT, HEAD_DIM), dtype=jnp.float32) * (1.0 / np.sqrt(IN_FEAT))
        attn_l = jax.random.normal(ks[2], (N_RELS, N_HEADS, HEAD_DIM), dtype=jnp.float32) * 0.1
        attn_r = jax.random.normal(ks[3], (N_RELS, N_HEADS, HEAD_DIM), dtype=jnp.float32) * 0.1
        h_bias = jax.random.normal(ks[4], (OUT_FEAT,), dtype=jnp.float32) * 0.02
        edge_src = jax.random.randint(ks[5], (N_EDGES,), 0, N_NODES, dtype=jnp.int32)
        edge_dst = jax.random.randint(ks[6], (N_EDGES,), 0, N_NODES, dtype=jnp.int32)
        edge_type = jax.random.randint(ks[7], (N_EDGES,), 0, N_RELS, dtype=jnp.int32)
        return {'inputs': inputs, 'conv_weights': conv_weights, 'attn_l': attn_l, 'attn_r': attn_r, 'h_bias': h_bias, 'edge_src': edge_src, 'edge_dst': edge_dst, 'edge_type': edge_type}
    _L0_gnn_all = _L0_gnn_setup()
    _L0_gnn_in = {k: v for k, v in _L0_gnn_all.items() if k in ('conv_weights', 'attn_l', 'attn_r', 'h_bias')}
    del _L0_gnn_all

    def _L0_ffn_setup():
        import jax, jax.numpy as jnp
        import numpy as np
        B, S, D = (8, 512, 256)
        H = 4 * D
        CAPACITY = 0.5
        key = jax.random.key(seed)
        ks = jax.random.split(key, 6)
        x = jax.random.normal(ks[0], (B, S, D), dtype=jnp.float32)
        attention_mask = jnp.zeros((B, 1, 1, S), dtype=jnp.float32)
        wr = jax.random.normal(ks[1], (D, 1), dtype=jnp.float32) * 0.02
        br = jnp.zeros((1,), dtype=jnp.float32)
        w1 = jax.random.normal(ks[2], (D, H), dtype=jnp.float32) * 0.02
        b1 = jnp.zeros((H,), dtype=jnp.float32)
        w2 = jax.random.normal(ks[3], (H, D), dtype=jnp.float32) * 0.02
        b2 = jnp.zeros((D,), dtype=jnp.float32)
        return {'x': x, 'attention_mask': attention_mask, 'wr': wr, 'br': br, 'w1': w1, 'b1': b1, 'w2': w2, 'b2': b2}
    _L0_ffn_all = _L0_ffn_setup()
    _L0_ffn_in = {k: v for k, v in _L0_ffn_all.items() if k in ('attention_mask', 'wr', 'br', 'w1', 'b1', 'w2', 'b2')}
    del _L0_ffn_all

    def _L1_gnn_setup():
        import jax, jax.numpy as jnp
        import numpy as np
        H = 4
        DH = 64
        HID = 256
        EPS = 1e-05
        N_NODES = 2500
        N_EDGES = 40000
        N_LAYERS = 3

        def _layer_norm(x, g, b):
            mu = jnp.mean(x, axis=-1, keepdims=True)
            var = jnp.mean((x - mu) ** 2, axis=-1, keepdims=True)
            return (x - mu) * jax.lax.rsqrt(var + EPS) * g + b

        def _message_passing(h, src, tgt, et, Wq, bq, Wk, bk, Wv, bv, Ee, Wo, bo, n_nodes):
            Q = (h @ Wq.T + bq).reshape(-1, H, DH)
            K = (h @ Wk.T + bk).reshape(-1, H, DH)
            V = (h @ Wv.T + bv).reshape(-1, H, DH)
            scores = jnp.einsum('ehd,egd->ehg', Q[src], K[tgt]) / jnp.sqrt(jnp.float32(DH))
            attn = jax.nn.softmax(scores, axis=-1)
            msg = jnp.einsum('ehg,egd->ehd', attn, V[tgt]).reshape(-1, HID)
            msg = msg + Ee[et]
            proj = msg @ Wo.T + bo
            return jax.ops.segment_sum(proj, src, num_segments=n_nodes)
        key = jax.random.key(seed)
        ks = jax.random.split(key, 16)

        def w(k, shape, s=0.05):
            return jax.random.normal(k, shape, jnp.float32) * s
        return {'x': jax.random.normal(ks[0], (N_NODES, HID), jnp.float32), 'edges': jax.random.randint(ks[1], (N_EDGES, 2), 0, N_NODES), 'edge_types': jax.random.randint(ks[2], (N_EDGES,), 0, 3), 'Win': w(ks[3], (HID, HID)), 'b_in': jnp.zeros((HID,), jnp.float32), 'Wq': w(ks[4], (N_LAYERS, HID, HID)), 'bq': jnp.zeros((N_LAYERS, HID), jnp.float32), 'Wk': w(ks[5], (N_LAYERS, HID, HID)), 'bk': jnp.zeros((N_LAYERS, HID), jnp.float32), 'Wv': w(ks[6], (N_LAYERS, HID, HID)), 'bv': jnp.zeros((N_LAYERS, HID), jnp.float32), 'Eemb': w(ks[7], (N_LAYERS, 3, HID)), 'Wo': w(ks[8], (N_LAYERS, HID, HID)), 'bo': jnp.zeros((N_LAYERS, HID), jnp.float32), 'ln_g': jnp.ones((N_LAYERS, HID), jnp.float32), 'ln_b': jnp.zeros((N_LAYERS, HID), jnp.float32), 'W1': w(ks[9], (HID, HID)), 'b1': jnp.zeros((HID,), jnp.float32), 'W2': w(ks[10], (HID, HID)), 'b2': jnp.zeros((HID,), jnp.float32)}
    _L1_gnn_all = _L1_gnn_setup()
    _L1_gnn_in = {k: v for k, v in _L1_gnn_all.items() if k in ('Win', 'b_in', 'Wq', 'bq', 'Wk', 'bk', 'Wv', 'bv', 'Eemb', 'Wo', 'bo', 'ln_g', 'ln_b', 'W1', 'b1', 'W2', 'b2')}
    del _L1_gnn_all

    def _L1_ffn_setup():
        import jax, jax.numpy as jnp
        import numpy as np
        B, A = (512, 8)
        IN, OUT = (256, 256)
        SH1, SH2 = (256, 128)
        EH1, EH2 = (128, 64)
        E, TOPK = (4, 2)

        def _shared_mlp(x, W1, b1, W2, b2, W3, b3):
            h = jax.nn.relu(x @ W1 + b1)
            h = jax.nn.relu(h @ W2 + b2)
            return h @ W3 + b3

        def _experts_mlp(x, eW1, eb1, eW2, eb2, eW3, eb3):
            h = jax.nn.relu(jnp.einsum('baf,efh->ebah', x, eW1) + eb1[:, None, None, :])
            h = jax.nn.relu(jnp.einsum('ebah,ehg->ebag', h, eW2) + eb2[:, None, None, :])
            o = jnp.einsum('ebag,ego->ebao', h, eW3) + eb3[:, None, None, :]
            return jnp.moveaxis(o, 0, -1)
        key = jax.random.key(seed)
        ks = jax.random.split(key, 16)
        s = 0.05
        return {'x': jax.random.normal(ks[0], (B, A, IN), jnp.float32), 'sW1': jax.random.normal(ks[1], (IN, SH1), jnp.float32) * s, 'sb1': jnp.zeros((SH1,), jnp.float32), 'sW2': jax.random.normal(ks[2], (SH1, SH2), jnp.float32) * s, 'sb2': jnp.zeros((SH2,), jnp.float32), 'sW3': jax.random.normal(ks[3], (SH2, OUT), jnp.float32) * s, 'sb3': jnp.zeros((OUT,), jnp.float32), 'eW1': jax.random.normal(ks[4], (E, IN, EH1), jnp.float32) * s, 'eb1': jnp.zeros((E, EH1), jnp.float32), 'eW2': jax.random.normal(ks[5], (E, EH1, EH2), jnp.float32) * s, 'eb2': jnp.zeros((E, EH2), jnp.float32), 'eW3': jax.random.normal(ks[6], (E, EH2, OUT), jnp.float32) * s, 'eb3': jnp.zeros((E, OUT), jnp.float32), 'gW': jax.random.normal(ks[7], (IN, E), jnp.float32) * s, 'gb': jnp.zeros((E,), jnp.float32)}
    _L1_ffn_all = _L1_ffn_setup()
    _L1_ffn_in = {k: v for k, v in _L1_ffn_all.items() if k in ('sW1', 'sb1', 'sW2', 'sb2', 'sW3', 'sb3', 'eW1', 'eb1', 'eW2', 'eb2', 'eW3', 'eb3', 'gW', 'gb')}
    del _L1_ffn_all
    return {'x': x, 'src': src, 'dst': dst, 'edge_type_3': edge_type_3, 'edge_type_8': edge_type_8, 'L0_gnn_conv_weights': _L0_gnn_in['conv_weights'], 'L0_gnn_attn_l': _L0_gnn_in['attn_l'], 'L0_gnn_attn_r': _L0_gnn_in['attn_r'], 'L0_gnn_h_bias': _L0_gnn_in['h_bias'], 'L0_ffn_attention_mask': _L0_ffn_in['attention_mask'], 'L0_ffn_wr': _L0_ffn_in['wr'], 'L0_ffn_br': _L0_ffn_in['br'], 'L0_ffn_w1': _L0_ffn_in['w1'], 'L0_ffn_b1': _L0_ffn_in['b1'], 'L0_ffn_w2': _L0_ffn_in['w2'], 'L0_ffn_b2': _L0_ffn_in['b2'], 'L1_gnn_Win': _L1_gnn_in['Win'], 'L1_gnn_b_in': _L1_gnn_in['b_in'], 'L1_gnn_Wq': _L1_gnn_in['Wq'], 'L1_gnn_bq': _L1_gnn_in['bq'], 'L1_gnn_Wk': _L1_gnn_in['Wk'], 'L1_gnn_bk': _L1_gnn_in['bk'], 'L1_gnn_Wv': _L1_gnn_in['Wv'], 'L1_gnn_bv': _L1_gnn_in['bv'], 'L1_gnn_Eemb': _L1_gnn_in['Eemb'], 'L1_gnn_Wo': _L1_gnn_in['Wo'], 'L1_gnn_bo': _L1_gnn_in['bo'], 'L1_gnn_ln_g': _L1_gnn_in['ln_g'], 'L1_gnn_ln_b': _L1_gnn_in['ln_b'], 'L1_gnn_W1': _L1_gnn_in['W1'], 'L1_gnn_b1': _L1_gnn_in['b1'], 'L1_gnn_W2': _L1_gnn_in['W2'], 'L1_gnn_b2': _L1_gnn_in['b2'], 'L1_ffn_sW1': _L1_ffn_in['sW1'], 'L1_ffn_sb1': _L1_ffn_in['sb1'], 'L1_ffn_sW2': _L1_ffn_in['sW2'], 'L1_ffn_sb2': _L1_ffn_in['sb2'], 'L1_ffn_sW3': _L1_ffn_in['sW3'], 'L1_ffn_sb3': _L1_ffn_in['sb3'], 'L1_ffn_eW1': _L1_ffn_in['eW1'], 'L1_ffn_eb1': _L1_ffn_in['eb1'], 'L1_ffn_eW2': _L1_ffn_in['eW2'], 'L1_ffn_eb2': _L1_ffn_in['eb2'], 'L1_ffn_eW3': _L1_ffn_in['eW3'], 'L1_ffn_eb3': _L1_ffn_in['eb3'], 'L1_ffn_gW': _L1_ffn_in['gW'], 'L1_ffn_gb': _L1_ffn_in['gb']}

def reference(x, src, dst, edge_type_3, edge_type_8, L0_gnn_conv_weights, L0_gnn_attn_l, L0_gnn_attn_r, L0_gnn_h_bias, L0_ffn_attention_mask, L0_ffn_wr, L0_ffn_br, L0_ffn_w1, L0_ffn_b1, L0_ffn_w2, L0_ffn_b2, L1_gnn_Win, L1_gnn_b_in, L1_gnn_Wq, L1_gnn_bq, L1_gnn_Wk, L1_gnn_bk, L1_gnn_Wv, L1_gnn_bv, L1_gnn_Eemb, L1_gnn_Wo, L1_gnn_bo, L1_gnn_ln_g, L1_gnn_ln_b, L1_gnn_W1, L1_gnn_b1, L1_gnn_W2, L1_gnn_b2, L1_ffn_sW1, L1_ffn_sb1, L1_ffn_sW2, L1_ffn_sb2, L1_ffn_sW3, L1_ffn_sb3, L1_ffn_eW1, L1_ffn_eb1, L1_ffn_eW2, L1_ffn_eb2, L1_ffn_eW3, L1_ffn_eb3, L1_ffn_gW, L1_ffn_gb):
    import jax
    import jax.numpy as jnp

    def _L0_gnn_ref(inputs, conv_weights, attn_l, attn_r, h_bias, edge_src, edge_dst, edge_type):
        import jax, jax.numpy as jnp
        import numpy as np
        N_NODES = 3750
        N_EDGES = 60000
        IN_FEAT = 256
        OUT_FEAT = 256
        N_RELS = 8
        N_HEADS = 4
        HEAD_DIM = OUT_FEAT // N_HEADS
        LEAKY_SLOPE = 0.2
        feat_all = jnp.einsum('ni,rhid->rnhd', inputs, conv_weights)
        feat_src_e = feat_all[edge_type, edge_src]
        feat_dst_e = feat_all[edge_type, edge_dst]
        el = jnp.sum(feat_src_e * attn_l[edge_type], axis=-1)
        er = jnp.sum(feat_dst_e * attn_r[edge_type], axis=-1)
        e = jax.nn.leaky_relu(el + er, negative_slope=LEAKY_SLOPE)
        m = jax.ops.segment_max(e, edge_dst, num_segments=N_NODES)
        ex = jnp.exp(e - m[edge_dst])
        denom = jax.ops.segment_sum(ex, edge_dst, num_segments=N_NODES)
        alpha = ex / denom[edge_dst]
        h = jax.ops.segment_sum(alpha[..., None] * feat_src_e, edge_dst, num_segments=N_NODES)
        h = h.reshape(N_NODES, OUT_FEAT) + h_bias
        return h

    def _L0_ffn_ref(x, attention_mask, wr, br, w1, b1, w2, b2):
        import jax, jax.numpy as jnp
        import numpy as np
        B, S, D = (8, 512, 256)
        H = 4 * D
        CAPACITY = 0.5
        b, s, d = x.shape
        weights = (jnp.einsum('bsd,do->bso', x, wr) + br)[..., 0]
        k = max(1, int(CAPACITY * s))
        kk = k - 1 if k > 1 else 1
        _, idx = jax.lax.top_k(weights, k)
        sel_idx = idx[:, :kk]
        sel = jnp.take_along_axis(x, sel_idx[:, :, None], axis=1)
        h = jax.nn.gelu(jnp.einsum('bkd,dh->bkh', sel, w1) + b1)
        y = jnp.einsum('bkh,hd->bkd', h, w2) + b2
        w_sel = jnp.take_along_axis(weights, sel_idx, axis=1)
        y = y * w_sel[..., None]
        batch_idx = jnp.arange(b)[:, None]
        processed = jnp.zeros_like(x).at[batch_idx, sel_idx].set(y)
        return processed + x

    def _L1_gnn_ref(x, edges, edge_types, Win, b_in, Wq, bq, Wk, bk, Wv, bv, Eemb, Wo, bo, ln_g, ln_b, W1, b1, W2, b2):
        import jax, jax.numpy as jnp
        import numpy as np
        H = 4
        DH = 64
        HID = 256
        EPS = 1e-05
        N_NODES = 2500
        N_EDGES = 40000
        N_LAYERS = 3

        def _layer_norm(x, g, b):
            mu = jnp.mean(x, axis=-1, keepdims=True)
            var = jnp.mean((x - mu) ** 2, axis=-1, keepdims=True)
            return (x - mu) * jax.lax.rsqrt(var + EPS) * g + b

        def _message_passing(h, src, tgt, et, Wq, bq, Wk, bk, Wv, bv, Ee, Wo, bo, n_nodes):
            Q = (h @ Wq.T + bq).reshape(-1, H, DH)
            K = (h @ Wk.T + bk).reshape(-1, H, DH)
            V = (h @ Wv.T + bv).reshape(-1, H, DH)
            scores = jnp.einsum('ehd,egd->ehg', Q[src], K[tgt]) / jnp.sqrt(jnp.float32(DH))
            attn = jax.nn.softmax(scores, axis=-1)
            msg = jnp.einsum('ehg,egd->ehd', attn, V[tgt]).reshape(-1, HID)
            msg = msg + Ee[et]
            proj = msg @ Wo.T + bo
            return jax.ops.segment_sum(proj, src, num_segments=n_nodes)
        n_nodes = x.shape[0]
        src, tgt = (edges[:, 0], edges[:, 1])
        hidden = x @ Win.T + b_in
        for l in range(N_LAYERS):
            m = _message_passing(hidden, src, tgt, edge_types, Wq[l], bq[l], Wk[l], bk[l], Wv[l], bv[l], Eemb[l], Wo[l], bo[l], n_nodes)
            hidden = jax.nn.relu(_layer_norm(hidden + m, ln_g[l], ln_b[l]))
        adjustment = jax.nn.relu(hidden @ W1.T + b1) @ W2.T + b2
        return x + adjustment

    def _L1_ffn_ref(x, sW1, sb1, sW2, sb2, sW3, sb3, eW1, eb1, eW2, eb2, eW3, eb3, gW, gb):
        import jax, jax.numpy as jnp
        import numpy as np
        B, A = (512, 8)
        IN, OUT = (256, 256)
        SH1, SH2 = (256, 128)
        EH1, EH2 = (128, 64)
        E, TOPK = (4, 2)

        def _shared_mlp(x, W1, b1, W2, b2, W3, b3):
            h = jax.nn.relu(x @ W1 + b1)
            h = jax.nn.relu(h @ W2 + b2)
            return h @ W3 + b3

        def _experts_mlp(x, eW1, eb1, eW2, eb2, eW3, eb3):
            h = jax.nn.relu(jnp.einsum('baf,efh->ebah', x, eW1) + eb1[:, None, None, :])
            h = jax.nn.relu(jnp.einsum('ebah,ehg->ebag', h, eW2) + eb2[:, None, None, :])
            o = jnp.einsum('ebag,ego->ebao', h, eW3) + eb3[:, None, None, :]
            return jnp.moveaxis(o, 0, -1)
        all_out = _experts_mlp(x, eW1, eb1, eW2, eb2, eW3, eb3)
        shared = _shared_mlp(x, sW1, sb1, sW2, sb2, sW3, sb3)
        gates = jax.nn.softmax(x @ gW + gb, axis=-1)
        topv, topi = jax.lax.top_k(gates, TOPK)
        topw = jax.nn.softmax(topv, axis=-1)
        sel = jnp.take_along_axis(all_out, topi[:, :, None, :], axis=-1)
        gated = jnp.sum(sel * topw[:, :, None, :], axis=-1)
        return shared + gated
    edge_index_t = jnp.stack([src, dst], axis=1)
    x = x + _L0_gnn_ref(_layernorm(x, axis=-1), L0_gnn_conv_weights, L0_gnn_attn_l, L0_gnn_attn_r, L0_gnn_h_bias, src, dst, edge_type_8)
    x = x + _L0_ffn_ref(_layernorm(x, axis=-1)[None], L0_ffn_attention_mask, L0_ffn_wr, L0_ffn_br, L0_ffn_w1, L0_ffn_b1, L0_ffn_w2, L0_ffn_b2)[0]
    x = x + _L1_gnn_ref(_layernorm(x, axis=-1), edge_index_t, edge_type_3, L1_gnn_Win, L1_gnn_b_in, L1_gnn_Wq, L1_gnn_bq, L1_gnn_Wk, L1_gnn_bk, L1_gnn_Wv, L1_gnn_bv, L1_gnn_Eemb, L1_gnn_Wo, L1_gnn_bo, L1_gnn_ln_g, L1_gnn_ln_b, L1_gnn_W1, L1_gnn_b1, L1_gnn_W2, L1_gnn_b2)
    x = x + _L1_ffn_ref(_layernorm(x, axis=-1)[None], L1_ffn_sW1, L1_ffn_sb1, L1_ffn_sW2, L1_ffn_sb2, L1_ffn_sW3, L1_ffn_sb3, L1_ffn_eW1, L1_ffn_eb1, L1_ffn_eW2, L1_ffn_eb2, L1_ffn_eW3, L1_ffn_eb3, L1_ffn_gW, L1_ffn_gb)[0]
    return x

_drawn_inputs = setup_inputs


def setup_inputs(seed=0):
    import zlib

    import numpy as np

    out = dict(_drawn_inputs(seed))
    spreads = {'L0_ffn_b1': (0.0, 0.8),
     'L0_ffn_b2': (0.0, 0.711),
     'L1_gnn_b_in': (0.0, 0.566),
     'L1_gnn_bq': (0.0, 0.8),
     'L1_gnn_bk': (0.0, 0.8),
     'L1_gnn_bv': (0.0, 0.1),
     'L1_gnn_bo': (0.0, 0.1),
     'L1_gnn_ln_g': (1.0, 0.54),
     'L1_gnn_ln_b': (0.0, 0.354),
     'L1_gnn_b1': (0.0, 0.457),
     'L1_gnn_b2': (0.0, 0.1),
     'L1_ffn_sb1': (0.0, 0.8),
     'L1_ffn_sb2': (0.0, 0.642),
     'L1_ffn_sb3': (0.0, 0.41),
     'L1_ffn_eb1': (0.0, 0.8),
     'L1_ffn_eb2': (0.0, 0.8),
     'L1_ffn_eb3': (0.0, 0.356),
     'L1_ffn_gb': (0.0, 0.8)}
    factors = {'L0_gnn_h_bias': 2.992,
     'L0_ffn_wr': 3.869,
     'L0_ffn_w1': 4.507,
     'L0_ffn_w2': 4.178,
     'L1_gnn_Win': 3.57,
     'L1_ffn_eW1': 3.922,
     'L1_ffn_eW2': 3.462,
     'L1_ffn_eW3': 2.712}
    for name, (base, spread) in spreads.items():
        noise = np.random.default_rng([zlib.crc32(name.encode()), seed]).standard_normal(out[name].shape)
        drawn = base * np.exp(spread * noise) if base else spread * noise
        out[name] = jnp.asarray(drawn.astype(out[name].dtype))
    for name, factor in factors.items():
        out[name] = (out[name] * factor).astype(out[name].dtype)
    return out
```

```python
import concourse.bass as bass
from concourse import mybir
from contextlib import ExitStack

F32 = mybir.dt.float32
BF16 = mybir.dt.bfloat16
I32 = mybir.dt.int32
U32 = mybir.dt.uint32
ALU = mybir.AluOpType
ACT = mybir.ActivationFunctionType
AX = mybir.AxisListType.X

P = 128
N_NODES, D = 3750, 256
N_EDGES = 60000
KC = D // P
NH, HD = 4, 64
NREL = 8
WIN = 30
NW = N_NODES // WIN
HW = NH * WIN
GROUP = 4
NT = -(-((N_EDGES + (P - 1) * NW) // P) // (2 * GROUP)) * 2 * GROUP
NG = NT // GROUP
SLICE = 120
NSL = N_EDGES // SLICE
SB = 4
SK = NSL // SB
CH = 20
NCH = NSL // CH
ROUND = 12582912.0
NEG = -1.0e30
FLOOR = -1.0e20
EPS = 1e-5
FROW = NREL * D
PADTGT = 0


class Ctx:

    def __init__(self, nc, stack):
        self.nc, self.stack, self.sems = nc, stack, []

    used = {}

    def own(self, name):
        n = self.used[name] = self.used.get(name, 0) + 1
        return name if n == 1 else f"{name}_{n}"

    def sb(self, name, shape, dt=F32):
        return self.stack.enter_context(self.nc.sbuf_tensor(self.own(name), shape, dt))

    def ps(self, name, shape):
        bank = self.stack.enter_context(self.nc.psum_tensor(self.own(name), [P, 512], F32))
        n = 1
        for m in shape[1:]:
            n *= m
        view = bank[0:shape[0], 0:n]
        return view if len(shape) == 2 else view.rearrange("p (a b) -> p a b", b=shape[2])

    def sem(self, name):
        if not self.sems:
            self.stack.callback(self.clear)
        self.sems.append(self.nc.alloc_semaphore(self.own(name)))
        return self.sems[-1]

    def clear(self):
        self.nc.clear_and_free_semaphores(self.sems)
        self.nc.all_engine_barrier()

    def block(self):
        return self.stack.enter_context(self.nc.Block())


def chained(eng, sem):
    count = [0]

    def link(ins):
        count[0] += 1
        ins.then_inc(sem, 1)
        eng.wait_ge(sem, count[0])

    return link


def row(ap):
    return ap.unsqueeze(0)


def spread(ap, parts, n):
    return ap.unsqueeze(0).to_broadcast([parts, n])


class Bag:
    pass


def constants(nc, K):
    with ExitStack() as stack:
        c = Ctx(nc, stack)
        s_fill, s_made, s_conv = c.sem("const_filled"), c.sem("const_made"), c.sem("const_converted")
        iota_i = c.sb("iota_i", [P, WIN], I32)
        part_i = c.sb("part_i", [P, 1], I32)
        tile_i = c.sb("tile_i", [P, NT], I32)
        block = c.block()

        @block.gpsimd
        def _(pool):
            nc.gpsimd.memset(K.ident[:, :], 1.0).then_inc(s_fill, 1)
            nc.gpsimd.memset(K.ones[:, :], 1.0).then_inc(s_fill, 1)
            nc.gpsimd.memset(K.before[:, :], 1.0).then_inc(s_fill, 1)
            nc.gpsimd.memset(K.zero_i[:, :], 0).then_inc(s_fill, 1)
            pool.wait_ge(s_fill, 4)
            nc.gpsimd.affine_select(out=K.ident[:, :], in_=K.ident[:, :], compare_op=ALU.is_equal, fill=0.0,
                                    base=0, pattern=[[-1, P]], channel_multiplier=1).then_inc(s_made, 1)
            nc.gpsimd.affine_select(out=K.before[:, :], in_=K.before[:, :], compare_op=ALU.is_gt, fill=0.0,
                                    base=0, pattern=[[1, P]], channel_multiplier=-1).then_inc(s_made, 1)
            nc.gpsimd.iota(iota_i[:, :], pattern=[[1, WIN]], base=0, channel_multiplier=0).then_inc(s_made, 1)
            nc.gpsimd.iota(part_i[:, :], pattern=[[1, 1]], base=0, channel_multiplier=1).then_inc(s_made, 1)
            nc.gpsimd.iota(tile_i[:, :], pattern=[[1, NT]], base=0, channel_multiplier=0).then_inc(s_made, 1)

        @block.vector
        def _(dve):
            dve.wait_ge(s_made, 5)
            nc.vector.tensor_copy(K.iota[:, :], iota_i[:, :]).then_inc(s_conv, 1)
            nc.vector.tensor_copy(K.part[:, :], part_i[:, :]).then_inc(s_conv, 1)
            nc.vector.tensor_copy(K.tile_no[:, :], tile_i[:, :]).then_inc(K.ready, 1)


def layernorm(nc, K, X, Y, tag):
    with ExitStack() as stack:
        c = Ctx(nc, stack)
        stats = c.sb("ln_stats_" + tag, [NW, WIN, 6])
        mv = c.sb("ln_mv_" + tag, [NW, WIN, 2])
        std = c.sb("ln_std_" + tag, [NW, WIN])
        s_stats, s_mv, s_var = c.sem("ln_stats_" + tag), c.sem("ln_mv_" + tag), c.sem("ln_var_" + tag)
        s_std, s_rstd, s_out = c.sem("ln_std_" + tag), c.sem("ln_rstd_" + tag), c.sem("ln_out_" + tag)
        block = c.block()

        @block.vector
        def _(dve):
            with dve.Fori(0, WIN) as i:
                nc.vector.bn_stats(stats[:, bass.ds(i, 1), :].rearrange("p a s -> p (a s)"),
                                   X[:, bass.ds(i, 1), :].rearrange("p a d -> p (a d)")).then_inc(s_stats, 1)
            dve.wait_ge(s_stats, WIN)
            for i in range(WIN):
                nc.vector.bn_aggr(mv[:, i, :], stats[:, i, :]).then_inc(s_mv, 1)
            dve.wait_ge(s_mv, WIN)
            nc.vector.tensor_scalar(mv[:, :, 1], mv[:, :, 1], EPS, None, ALU.add).then_inc(s_var, 1)
            dve.wait_ge(s_std, 1)
            nc.vector.reciprocal(mv[:, :, 1], std[:, :]).then_inc(s_rstd, 1)
            dve.wait_ge(s_rstd, 1)
            for i in range(WIN):
                nc.vector.tensor_scalar(Y[:, i, :], X[:, i, :], mv[:, i, 0:1], mv[:, i, 1:2],
                                        ALU.subtract, ALU.mult).then_inc(s_out, 1)

        @block.scalar
        def _(act):
            act.wait_ge(s_var, 1)
            nc.scalar.activation(std[:, :], mv[:, :, 1], ACT.Sqrt).then_inc(s_std, 1)


def transpose_nodes(nc, K, Y, YT, tag):
    with ExitStack() as stack:
        c = Ctx(nc, stack)
        pt = [c.ps(f"tn_ps{b}_" + tag, [P, 2, P]) for b in range(2)]
        s_t, s_free = c.sem("tn_transposed_" + tag), c.sem("tn_bank_free_" + tag)
        block = c.block()

        @block.tensor
        def _(pe):
            for i in range(WIN):
                pe.wait_ge(s_free, i + 1)
                for k in range(KC):
                    last = nc.tensor.transpose(pt[i % 2][:, k, 0:NW], Y[:, i, k * P:(k + 1) * P], K.ident[0:NW, 0:NW])
                last.then_inc(s_t, 1)

        @block.scalar
        def _(act):
            act.sem_inc(s_free, 2)
            with act.Fori(0, WIN // 2) as j:
                for b in range(2):
                    act.wait_ge(s_t, j * 2 + b + 1)
                    nc.scalar.activation(YT[:, :, bass.ds(j * 2 + b, 1), :].rearrange("p k a w -> p k (a w)"),
                                         pt[b][:, :, 0:NW], ACT.Copy).then_inc(s_free, 1)


def relation_features(nc, K, T, YT):
    with ExitStack() as stack:
        c = Ctx(nc, stack)
        NQ = FROW // 512
        W = c.sb("rf_w", [P, KC, FROW])
        prod = c.sb("rf_prod", [P, FROW])
        attn = [c.sb(f"rf_attn{a}", [P, FROW]) for a in range(2)]
        WA = c.sb("rf_wa", [P, KC, 2, NREL * NH])
        stage = c.sb("rf_stage", [NW, 2, FROW])
        logits = c.sb("rf_logits", [NW, 2, WIN, NREL * NH])
        bank = [c.ps(f"rf_ps{q}", [P, 512]) for q in range(NQ)]
        bank_l = [c.ps(f"rf_psl{b}", [P, 2, NREL * NH]) for b in range(2)]
        s_w, s_wa, s_prod = c.sem("rf_weights"), c.sem("rf_wa_parts"), c.sem("rf_product")
        full = [c.sem(f"rf_full{q}") for q in range(NQ)]
        copied = [c.sem(f"rf_copied{q}") for q in range(NQ)]
        full_l = [c.sem(f"rf_full_l{b}") for b in range(2)]
        copied_l = [c.sem(f"rf_copied_l{b}") for b in range(2)]
        stored = [c.sem(f"rf_stored{b}") for b in range(2)]
        s_lst = c.sem("rf_logits_stored")
        block = c.block()

        @block.sync
        def _(sp):
            for a, name in enumerate(("L0_gnn_attn_l", "L0_gnn_attn_r")):
                sp.dma_start(attn[a][:, :], spread(T[name].rearrange("r h d -> (r h d)"), P, FROW)).then_inc(stored[a], 16)
            for r in range(NREL):
                for h in range(NH):
                    q = r * NH + h
                    sp.dma_start(W[:, :, q * HD:(q + 1) * HD],
                                 T["L0_gnn_conv_weights"][r, h].rearrange("(k p) d -> p k d", p=P)).then_inc(s_w, 16)
            table = T["feat"].rearrange("(w i r) d -> w i (r d)", i=WIN, r=NREL)
            with sp.Fori(0, WIN // 2) as j:
                for b in range(2):
                    for q in range(NQ):
                        sp.wait_ge(copied[q], j * 2 + b + 2)
                    sp.dma_start(table[:, bass.ds(j * 2 + b, 1), :], stage[:, b:b + 1, :]).then_inc(stored[b], 16)
            for b in range(2):
                sp.wait_ge(copied_l[b], WIN // 2 + 1)
            for a in range(2):
                sp.dma_start(T[f"logit{a}"].rearrange("(w q) h -> w (q h)", w=NW),
                             logits[:, a, :, :].rearrange("p i q -> p (i q)")).then_inc(s_lst, 16)
            sp.wait_ge(s_lst, 32)
            for b in range(2):
                sp.wait_ge(stored[b], 16 + 16 * (WIN // 2))

        def copy_rows(eng, op, q, j, b):
            eng.wait_ge(full[q], j * 2 + b + 1)
            eng.wait_ge(stored[b], j * 16 + 16)
            op(stage[:, b, q * 512:(q + 1) * 512], bank[q][0:NW, :]).then_inc(copied[q], 1)

        @block.vector
        def _(dve):
            dve.wait_ge(s_w, 16 * NREL * NH)
            for a in range(2):
                dve.wait_ge(stored[a], 16)
            n = 0
            for k in range(KC):
                for a in range(2):
                    if n:
                        dve.wait_ge(s_wa, n)
                    n += 1
                    nc.vector.tensor_tensor(prod[:, :], W[:, k, :], attn[a][:, :], ALU.mult).then_inc(s_prod, 1)
                    dve.wait_ge(s_prod, n)
                    nc.vector.tensor_reduce(WA[:, k, a, :], prod[:, :].rearrange("p (q d) -> p q d", d=HD),
                                            AX, ALU.add).then_inc(s_wa, 1)
            dve.sem_inc(copied[0], 1)
            dve.sem_inc(copied[1], 1)
            for b in range(2):
                dve.sem_inc(copied_l[b], 1)
            with dve.Fori(0, WIN // 2) as j:
                for b in range(2):
                    for q in (0, 1):
                        copy_rows(dve, nc.vector.tensor_copy, q, j, b)
                    dve.wait_ge(full_l[b], j + 1)
                    nc.vector.tensor_copy(logits[:, :, bass.ds(j * 2 + b, 1), :].rearrange("p a i q -> p a (i q)"),
                                          bank_l[b][0:NW, :, :]).then_inc(copied_l[b], 1)

        @block.scalar
        def _(act):
            act.sem_inc(copied[2], 1)
            act.sem_inc(copied[3], 1)
            with act.Fori(0, WIN // 2) as j:
                for b in range(2):
                    for q in (2, 3):
                        copy_rows(act, nc.scalar.copy, q, j, b)

        @block.tensor
        def _(pe):
            pe.wait_ge(s_w, 16 * NREL * NH)
            pe.wait_ge(s_wa, 2 * KC)
            for i in range(WIN):
                for q in range(NQ):
                    pe.wait_ge(copied[q], i + 1)
                    for k in range(KC):
                        last = nc.tensor.matmul(bank[q][0:NW, :], YT[:, k, i, :], W[:, k, q * 512:(q + 1) * 512],
                                                start=k == 0, stop=k == KC - 1)
                    last.then_inc(full[q], 1)
                pe.wait_ge(copied_l[i % 2], i // 2 + 1)
                for k in range(KC):
                    last = nc.tensor.matmul(bank_l[i % 2][0:NW, :, :].rearrange("p a q -> p (a q)"), YT[:, k, i, :],
                                            WA[:, k, :, :].rearrange("p a q -> p (a q)"), start=k == 0, stop=k == KC - 1)
                last.then_inc(full_l[i % 2], 1)


def sort_edges(nc, K, T, key, fields, slots, bucket, tag, R):
    nf = len(fields)
    names = sorted({n for terms in fields for n, _ in terms} | {key})
    with ExitStack() as stack:
        c = Ctx(nc, stack)
        raw = {n: c.sb(f"so_raw_{n}_" + tag, [SK, SB, SLICE], I32) for n in names}
        val = {n: c.sb(f"so_val_{n}_" + tag, [SK, SB, SLICE]) for n in names}
        bk = c.sb("so_bucket_" + tag, [SK, SB, SLICE])
        bkh = c.sb("so_bucket_bf_" + tag, [SK, SB, SLICE], BF16)
        F = [c.sb(f"so_field{f}_" + tag, [SK, SB, SLICE]) for f in range(nf + 1)]
        pay = c.sb("so_pay_" + tag, [SLICE, NSL, 4])
        empty = c.sb("so_empty_" + tag, [P, NT, 4])
        keys = [c.sb(f"so_keys{b}_" + tag, [NW, CH * SLICE], BF16) for b in range(2)]
        hot = [c.sb(f"so_hot{b}_" + tag, [NW, CH * SLICE], BF16) for b in range(2)]
        scan = [c.sb(f"so_scan{b}_" + tag, [NW, CH * SLICE]) for b in range(2)]
        hit = [c.sb(f"so_hit{b}_" + tag, [NW, CH * SLICE]) for b in range(2)]
        count = c.sb("so_count_" + tag, [NW, NCH])
        total = c.sb("so_total_" + tag, [NW, 1])
        tiles = c.sb("so_tiles_" + tag, [NW, 1])
        first = c.sb("so_first_" + tag, [NW, 1])
        carry = c.sb("so_carry_" + tag, [NW, 1])
        reach = c.sb("so_reach_" + tag, [NW, NT])
        place = c.sb("so_place_" + tag, [SLICE, NSL])
        tile = c.sb("so_tile_" + tag, [SLICE, NSL])
        addr = c.sb("so_addr_" + tag, [SLICE, NSL])
        addr_i = c.sb("so_addr_i_" + tag, [SLICE, NSL], I32)
        NS = 10
        idx_s = c.sb("so_idx_stage_" + tag, [SLICE, 2, NS], I32)
        pay_s = c.sb("so_pay_stage_" + tag, [SLICE, 2, NS, 4])
        got = c.sb("so_slots_" + tag, [P, NT, 4])
        pt = [c.ps(f"so_pt{q}_" + tag, [P, 512]) for q in range(2)]
        ppos = c.ps("so_ppos_" + tag, [P, 512])
        pw = [c.ps(f"so_pw{q}_" + tag, [P, 512]) for q in range(2)]
        pf = c.ps("so_pf_" + tag, [P, 8])
        sem = lambda n: c.sem("so_" + n + "_" + tag)
        s_ld, s_ch, s_bk, s_bks, s_tr, s_pay = sem("loaded"), sem("chain"), sem("bucket"), sem("bucket_stored"), sem("transposed"), sem("pay")
        s_kin = [sem(f"keys_in{b}") for b in range(2)]
        s_kfree = [sem(f"keys_free{b}") for b in range(2)]
        s_cnt, s_first, s_tiles, s_reach, s_wb = sem("counted"), sem("first"), sem("tiles"), sem("reach"), sem("window_of_tile")
        s_hot, s_scan, s_hit, s_hfree = sem("hot"), sem("scanned"), sem("hit"), sem("hit_free")
        s_pos, s_addr, s_empty, s_estored = sem("positions"), sem("addr"), sem("empty"), sem("empty_stored")
        s_stage = [sem(f"staged{b}") for b in range(2)]
        s_sc = [sem(f"scattered{b}") for b in range(2)]
        s_got, s_end, s_win, s_done = sem("slots_loaded"), sem("end"), sem("win"), sem("done")
        s_ch2, s_ch3 = sem("chain2"), sem("chain3")
        s_sfree = [sem(f"stage_free{b}") for b in range(2)]
        s_i = [sem(f"idx_staged{b}") for b in range(2)]

        with nc.Block() as block:
            @block.sync
            def _(sp):
                for n in names:
                    sp.dma_start(raw[n][:, :, :], T[n].rearrange("(b k p) -> k b p", b=SB, p=SLICE)).then_inc(s_ld, 16)
                sp.wait_ge(s_bk, 1)
                sp.dma_start(T[bucket].rearrange("(b k p) -> k b p", b=SB, p=SLICE), bkh[:, :, :]).then_inc(s_bks, 16)
                sp.wait_ge(s_empty, 2)
                sp.dma_start(T[slots].rearrange("(s j) q -> s (j q)", s=P),
                             empty[:, :, :].rearrange("p j q -> p (j q)")).then_inc(s_estored, 16)
                sp.wait_ge(s_bks, 16)
                sp.wait_ge(s_estored, 16)

            @block.gpsimd
            def _(pool):
                nc.gpsimd.memset(empty[:, :, :], 0.0).then_inc(s_empty, 1)
                pool.wait_ge(s_empty, 1)
                nc.gpsimd.memset(empty[:, :, 2:3], -1.0).then_inc(s_empty, 1)

            @block.vector
            def _(dve):
                link = chained(dve, s_ch)
                dve.wait_ge(s_ld, 16 * len(names))
                for n in names:
                    link(nc.vector.tensor_copy(val[n][:, :, :], raw[n][:, :, :]))
                link(nc.vector.tensor_scalar(bk[:, :, :], val[key][:, :, :], -(WIN - 1) / 2, 1.0 / WIN, ALU.add, ALU.mult))
                link(nc.vector.tensor_scalar(bk[:, :, :], bk[:, :, :], ROUND, None, ALU.add))
                link(nc.vector.tensor_scalar(bk[:, :, :], bk[:, :, :], -ROUND, None, ALU.add))
                nc.vector.tensor_copy(bkh[:, :, :], bk[:, :, :]).then_inc(s_bk, 1)
                for f, terms in enumerate(fields):
                    n0, m0 = terms[0]
                    link(nc.vector.tensor_scalar(F[f][:, :, :], val[n0][:, :, :], float(m0), None, ALU.mult))
                    for n1, m1 in terms[1:]:
                        link(nc.vector.scalar_tensor_tensor(F[f][:, :, :], val[n1][:, :, :], float(m1), F[f][:, :, :],
                                                            ALU.mult, ALU.add))
                link(nc.vector.scalar_tensor_tensor(F[nf][:, :, :], bk[:, :, :], -float(WIN), val[key][:, :, :],
                                                    ALU.mult, ALU.add))
                nc.vector.memset(pay[:, :, 3:4], 0.0).then_inc(s_pay, 1)
                for f in range(nf + 1):
                    dve.wait_ge(s_tr, f + 1)
                    nc.vector.tensor_copy(pay[:, :, f:f + 1].rearrange("p s a -> p (s a)"),
                                          pt[f % 2][0:SLICE, 0:NSL]).then_inc(s_pay, 1)

            @block.tensor
            def _(pe):
                pe.wait_ge(s_ch, len(names) + 3 + sum(len(t) for t in fields) + 1)
                for f in range(nf + 1):
                    if f >= 2:
                        pe.wait_ge(s_pay, f)
                    for b in range(SB):
                        last = nc.tensor.transpose(pt[f % 2][0:SLICE, b * SK:(b + 1) * SK], F[f][:, b, :],
                                                   K.ident[0:SK, 0:SK])
                    last.then_inc(s_tr, 1)

        keys_of = lambda ch: T[bucket][bass.ds(ch * CH * SLICE, CH * SLICE)].unsqueeze(0).to_broadcast([NW, CH * SLICE])
        with nc.Block() as block:
            @block.sync
            def _(sp):
                for ch in range(NCH):
                    b = ch % 2
                    if ch >= 2:
                        sp.wait_ge(s_cnt, ch - 1)
                    sp.dma_start(keys[b][:, :], keys_of(ch)).then_inc(s_kin[b], 16)

            @block.vector
            def _(dve):
                for ch in range(NCH):
                    b = ch % 2
                    dve.wait_ge(s_kin[b], 16 * (ch // 2 + 1))
                    if ch >= 2:
                        dve.wait_ge(s_cnt, ch - 1)
                    nc.vector.tensor_scalar(hot[b][:, :], keys[b][:, :], K.part[0:NW, :], 0.0, ALU.is_equal, ALU.add,
                                            accum_out=count[:, ch:ch + 1]).then_inc(s_cnt, 1)
                dve.wait_ge(s_cnt, NCH)
                link = chained(dve, s_ch2)
                link(nc.vector.tensor_reduce(total[:, :], count[:, :], AX, ALU.add))
                link(nc.vector.tensor_scalar(tiles[:, :], total[:, :], 63.25, 1.0 / P, ALU.add, ALU.mult))
                link(nc.vector.tensor_scalar(tiles[:, :], tiles[:, :], ROUND, None, ALU.add))
                link(nc.vector.tensor_scalar(tiles[:, :], tiles[:, :], -ROUND, None, ALU.add))
                dve.wait_ge(s_first, 1)
                link(nc.vector.tensor_copy(first[:, :], pf[0:NW, 0:1]))
                link(nc.vector.tensor_scalar(carry[:, :], first[:, :], float(P), None, ALU.mult))
                link(nc.vector.tensor_scalar(reach[:, :], K.tile_no[0:NW, :], first[:, :], None, ALU.is_ge))
                for q in range(2):
                    dve.wait_ge(s_wb, q + 1)
                    nc.vector.tensor_scalar(R.window[:, q * (NT // 2):(q + 1) * (NT // 2)], pw[q][:, 0:NT // 2], -1.0, None,
                                            ALU.add).then_inc(s_win, 1)
                dve.wait_ge(s_win, 2)
                nc.vector.tensor_copy(R.window_i[:, :], R.window[0:1, :]).then_inc(s_win, 1)

            @block.tensor
            def _(pe):
                pe.wait_ge(s_ch2, 4)
                nc.tensor.matmul(pf[0:NW, 0:1], K.before[0:NW, 0:NW], tiles[:, :], start=True, stop=True).then_inc(s_first, 1)
                pe.wait_ge(s_ch2, 7)
                for q in range(2):
                    nc.tensor.matmul(pw[q][:, 0:NT // 2], K.ones[0:NW, :], reach[:, q * (NT // 2):(q + 1) * (NT // 2)],
                                     start=True, stop=True).then_inc(s_wb, 1)

        with nc.Block() as block:
            @block.sync
            def _(sp):
                for ch in range(NCH):
                    b = ch % 2
                    if ch >= 2:
                        sp.wait_ge(s_hot, ch - 1)
                    sp.dma_start(keys[b][:, :], keys_of(ch)).then_inc(s_kin[b], 16)

            @block.vector
            def _(dve):
                for ch in range(NCH):
                    b = ch % 2
                    dve.wait_ge(s_kin[b], 16 * ((NCH + 1 - b) // 2 + ch // 2 + 1))
                    if ch >= 2:
                        dve.wait_ge(s_hit, ch - 1)
                    nc.vector.tensor_scalar(hot[b][:, :], keys[b][:, :], K.part[0:NW, :], None, ALU.is_equal).then_inc(s_hot, 1)
                    dve.wait_ge(s_hot, ch + 1)
                    if ch:
                        dve.wait_ge(s_scan, ch)
                    nc.vector.tensor_tensor_scan(scan[b][:, :], hot[b][:, :], hot[b][:, :],
                                                 scan[1 - b][:, CH * SLICE - 1:CH * SLICE] if ch else carry[:, :],
                                                 ALU.add, ALU.max).then_inc(s_scan, 1)
                    dve.wait_ge(s_scan, ch + 1)
                    if ch >= 2:
                        dve.wait_ge(s_hfree, ch - 1)
                    nc.vector.tensor_tensor(hit[b][:, :], scan[b][:, :], hot[b][:, :], ALU.mult).then_inc(s_hit, 1)
                link = chained(dve, s_ch3)
                dve.wait_ge(s_hfree, NCH)
                link(nc.vector.tensor_scalar(place[:, :], ppos[0:SLICE, 0:NSL], -1.0, None, ALU.add))
                link(nc.vector.tensor_scalar(tile[:, :], place[:, :], -(P - 1) / 2, 1.0 / P, ALU.add, ALU.mult))
                link(nc.vector.tensor_scalar(tile[:, :], tile[:, :], ROUND, None, ALU.add))
                link(nc.vector.tensor_scalar(tile[:, :], tile[:, :], -ROUND, None, ALU.add))
                link(nc.vector.scalar_tensor_tensor(addr[:, :], tile[:, :], -float(P), place[:, :], ALU.mult, ALU.add))
                link(nc.vector.scalar_tensor_tensor(addr[:, :], addr[:, :], float(NT), tile[:, :], ALU.mult, ALU.add))
                link(nc.vector.tensor_copy(addr_i[:, :], addr[:, :]))

            @block.tensor
            def _(pe):
                for ch in range(NCH):
                    pe.wait_ge(s_hit, ch + 1)
                    for q in range(CH):
                        last = nc.tensor.matmul(ppos[0:SLICE, ch * CH + q:ch * CH + q + 1],
                                                hit[ch % 2][:, q * SLICE:(q + 1) * SLICE], K.ones[0:NW, 0:1], start=True, stop=True)
                    last.then_inc(s_hfree, 1)

        with nc.Block() as block:
            @block.gpsimd
            def _(pool):
                bound = nc.gpsimd.to_reg(P * NT - 1)
                with pool.Fori(1, NSL // (2 * NS) + 1) as i:
                    for b in range(2):
                        pool.wait_ge(K.ready, 1)
                        pool.wait_ge(s_stage[b], i)
                        for q in range(NS):
                            nc.gpsimd.indirect_dma_start(
                                out=T[slots][:, :], out_offset=bass.IndirectOffsetOnAxis(ap=idx_s[:, b, q:q + 1].bitcast(U32), axis=0),
                                in_=pay_s[:, b, q, :], in_offset=None, bounds_check=bound, oob_is_err=False).then_inc(s_sc[b], 16)

            @block.vector
            def _(dve):
                with dve.Fori(0, NSL // (2 * NS)) as i:
                    for b in range(2):
                        dve.wait_ge(s_sfree[b], i + 1)
                        nc.vector.tensor_copy(idx_s[:, b, :], addr_i[:, bass.ds((i * 2 + b) * NS, NS)]).then_inc(s_i[b], 1)
                        dve.wait_ge(s_i[b], i + 1)
                        nc.vector.tensor_copy(pay_s[:, b, :, :], pay[:, bass.ds((i * 2 + b) * NS, NS), :]).then_inc(s_stage[b], 1)

            @block.sync
            def _(sp):
                for b in range(2):
                    sp.sem_inc(s_sfree[b], 1)
                with sp.Fori(0, NSL // (2 * NS)) as i:
                    for b in range(2):
                        sp.wait_ge(s_sc[b], i * (16 * NS) + 16 * NS)
                        sp.sem_inc(s_sfree[b], 1)
                sp.dma_start(got[:, :, :].rearrange("p j q -> p (j q)"), T[slots].rearrange("(s j) q -> s (j q)", s=P)).then_inc(s_got, 16)

            @block.scalar
            def _(act):
                act.wait_ge(s_got, 16)
                for f in range(nf):
                    nc.scalar.copy(R.index[f][:, :], got[:, :, f]).then_inc(s_done, 1)
                nc.scalar.copy(R.node[:, :], got[:, :, nf]).then_inc(s_done, 1)


def edge_logits(nc, K, T, R):
    with ExitStack() as stack:
        c = Ctx(nc, stack)
        idx_s = [[c.sb(f"el_idx{b}{a}", [P, GROUP], I32) for a in range(2)] for b in range(2)]
        part = [[c.sb(f"el_part{b}{a}", [P, GROUP, NH]) for a in range(2)] for b in range(2)]
        miss = [c.sb(f"el_miss{b}", [P, GROUP, WIN]) for b in range(2)]
        Xm = [c.sb(f"el_x{b}", [P, GROUP, NH, WIN]) for b in range(2)]
        tmax = c.sb("el_tmax", [HW, NT])
        reset = [c.sb(f"el_reset{d}", [HW, NT]) for d in range(2)]
        run = c.sb("el_run", [HW, NT])
        bank = [c.ps(f"el_ps{b}", [HW, GROUP, P]) for b in range(2)]
        staged = [[c.sem(f"el_staged{b}{a}") for a in range(2)] for b in range(2)]
        arrived = [c.sem(f"el_arrived{b}") for b in range(2)]
        free = [c.sem(f"el_free{b}") for b in range(2)]
        s_leaky = c.sem("el_leaky")
        s_m1 = [c.sem(f"el_m1{b}") for b in range(2)]
        s_m2 = [c.sem(f"el_m2{b}") for b in range(2)]
        s_x = [c.sem(f"el_xs{b}") for b in range(2)]
        s_t = [c.sem(f"el_t{b}") for b in range(2)]
        s_red = [c.sem(f"el_red{b}") for b in range(2)]
        s_ch = c.sem("el_chain")
        with nc.Block() as block:
            @block.gpsimd
            def _(pool):
                bound = nc.gpsimd.to_reg(N_NODES * NREL - 1)
                with pool.Fori(1, NG // 2 + 1) as i:
                    for b in range(2):
                        pool.wait_ge(free[b], i)
                        for a in range(2):
                            nc.gpsimd.tensor_tensor(idx_s[b][a][:, :], R.index[a][:, bass.ds(i * (2 * GROUP) + (b - 2) * GROUP, GROUP)],
                                                    K.zero_i[:, :], ALU.add).then_inc(staged[b][a], 1)
                        pool.wait_ge(K.ready, 1)
                        for a in range(2):
                            pool.wait_ge(staged[b][a], i)
                        for a in range(2):
                            for t in range(GROUP):
                                nc.gpsimd.indirect_dma_start(
                                    out=part[b][a][:, t, :], out_offset=None, in_=T[f"logit{a}"][:, :],
                                    in_offset=bass.IndirectOffsetOnAxis(ap=idx_s[b][a][:, t:t + 1].bitcast(U32), axis=0),
                                    bounds_check=bound, oob_is_err=False).then_inc(arrived[b], 16)

            @block.vector
            def _(dve):
                for b in range(2):
                    dve.sem_inc(free[b], 1)
                with dve.Fori(0, NG // 2) as i:
                    for b in range(2):
                        dve.wait_ge(arrived[b], i * (16 * 2 * GROUP) + 16 * 2 * GROUP)
                        nc.vector.tensor_tensor(R.ev[:, bass.ds(i * (2 * GROUP) + b * GROUP, GROUP), :], part[b][0][:, :, :],
                                                part[b][1][:, :, :], ALU.add).then_inc(free[b], 1)
                for b in range(2):
                    dve.wait_ge(free[b], NG // 2 + 1)
                ev = R.ev[:, :, :].rearrange("p j h -> p (j h)")
                nc.vector.scalar_tensor_tensor(ev, ev, 0.2, ev, ALU.mult, ALU.max).then_inc(s_leaky, 1)

        with nc.Block() as block:
            @block.vector
            def _(dve):
                dve.wait_ge(s_leaky, 1)
                for b in range(2):
                    dve.sem_inc(s_red[b], 1)
                with dve.Fori(0, NG // 2) as i:
                    for b in range(2):
                        masked_logits(nc, dve, K, R, i, b, miss, Xm, s_m1, s_m2, s_x)
                    for b in range(2):
                        dve.wait_ge(s_t[b], i + 1)
                        nc.vector.tensor_reduce(tmax[:, bass.ds(i * (2 * GROUP) + b * GROUP, GROUP)], bank[b][:, :, :],
                                                AX, ALU.max).then_inc(s_red[b], 1)
                for b in range(2):
                    dve.wait_ge(s_red[b], NG // 2 + 1)
                link = chained(dve, s_ch)
                link(nc.vector.memset(reset[0][:, :], 0.0))
                link(nc.vector.memset(reset[1][:, :], 0.0))
                link(nc.vector.tensor_tensor(reset[0][:, 1:NT], R.window[0:HW, 1:NT], R.window[0:HW, 0:NT - 1], ALU.not_equal))
                link(nc.vector.tensor_copy(reset[1][:, 0:NT - 1], reset[0][:, 1:NT]))
                for d in range(2):
                    link(nc.vector.tensor_scalar(reset[d][:, :], reset[d][:, :], NEG, None, ALU.mult))
                link(nc.vector.tensor_tensor_scan(run[:, :], reset[0][:, :], tmax[:, :], NEG, ALU.add, ALU.max))
                link(nc.vector.tensor_tensor_scan(tmax[:, ::-1], reset[1][:, ::-1], run[:, ::-1], NEG, ALU.add, ALU.max))
                link(nc.vector.tensor_scalar(R.negmax[:, :], tmax[:, :], FLOOR, -1.0, ALU.max, ALU.mult))

            @block.tensor
            def _(pe):
                with pe.Fori(0, NG // 2) as i:
                    for b in range(2):
                        pe.wait_ge(s_x[b], i + 1)
                        pe.wait_ge(s_red[b], i + 1)
                        for t in range(GROUP):
                            last = nc.tensor.transpose(bank[b][:, t, :], Xm[b][:, t, :, :].rearrange("p h n -> p (h n)"), K.ident[:, :])
                        last.then_inc(s_t[b], 1)


def masked_logits(nc, dve, K, R, i, b, miss, Xm, s_m1, s_m2, s_x):
    j0 = i * (2 * GROUP) + b * GROUP
    nc.vector.tensor_tensor(miss[b][:, :, :], R.node[:, bass.ds(j0, GROUP)].unsqueeze(2).to_broadcast([P, GROUP, WIN]),
                            K.iota[:, :].unsqueeze(1).to_broadcast([P, GROUP, WIN]), ALU.not_equal).then_inc(s_m1[b], 1)
    dve.wait_ge(s_m1[b], i + 1)
    nc.vector.tensor_scalar(miss[b][:, :, :], miss[b][:, :, :], NEG, None, ALU.mult).then_inc(s_m2[b], 1)
    dve.wait_ge(s_m2[b], i + 1)
    nc.vector.tensor_tensor(Xm[b][:, :, :, :], miss[b][:, :, :].unsqueeze(2).to_broadcast([P, GROUP, NH, WIN]),
                            R.ev[:, bass.ds(j0, GROUP), :].unsqueeze(3).to_broadcast([P, GROUP, NH, WIN]),
                            ALU.add).then_inc(s_x[b], 1)


def skewed(eng, passes, body):
    body(0, True, False)
    with eng.Fori(1, passes - 1) as i:
        body(i, False, False)
    body(passes - 1, False, True)


def relation_attention(nc, K, T, R, X):
    with ExitStack() as stack:
        c = Ctx(nc, stack)
        acc = c.sb("ra_acc", [HD, NW, 2 * HW])
        idx_s = [c.sb(f"ra_idx{b}", [P, GROUP], I32) for b in range(2)]
        feat = [c.sb(f"ra_feat{b}", [P, GROUP, D]) for b in range(2)]
        miss = [c.sb(f"ra_miss{b}", [P, GROUP, WIN]) for b in range(2)]
        Xm = [c.sb(f"ra_x{b}", [P, GROUP, NH, WIN]) for b in range(2)]
        prob = [c.sb(f"ra_prob{b}", [HW, GROUP, P]) for b in range(2)]
        A = [c.sb(f"ra_a{b}", [P, GROUP, HW]) for b in range(2)]
        bias = c.sb("ra_bias", [NW, D])
        sems = lambda n: [c.sem(f"ra_{n}{b}") for b in range(2)]
        staged, arrived = sems("staged"), [[c.sem(f"ra_arrived{b}{t}") for t in range(GROUP)] for b in range(2)]
        s_m1, s_m2, s_x, s_t = sems("m1"), sems("m2"), sems("x"), sems("t")
        s_exp = sems("exp")
        s_a, s_ac = sems("a"), sems("ac")
        s_ag = sems("ag")
        s_acc, s_bias, s_ch = c.sem("ra_acc"), c.sem("ra_bias"), c.sem("ra_ch")
        NP = NG // 2
        with ExitStack() as banks, nc.Block() as block:
            cb = Ctx(nc, banks)
            pt = [cb.ps(f"ra_pt{b}", [HW, GROUP, P]) for b in range(2)]
            pa = [cb.ps(f"ra_pa{b}", [P, 512]) for b in range(2)]
            pg = [[cb.ps(f"ra_pg{b}{q}", [HD, 2, 2 * HW]) for q in range(2)] for b in range(2)]

            @block.sync
            def _(sp):
                sp.dma_start(bias[:, :], spread(T["L0_gnn_h_bias"], NW, D)).then_inc(s_bias, 16)
                sp.wait_ge(s_bias, 16)

            @block.gpsimd
            def _(pool):
                bound = nc.gpsimd.to_reg(N_NODES * NREL - 1)
                with pool.Fori(1, NP + 1) as i:
                    for b in range(2):
                        pool.wait_ge(s_ag[b], i)
                        nc.gpsimd.tensor_tensor(idx_s[b][:, :], R.index[0][:, bass.ds(i * (2 * GROUP) + (b - 2) * GROUP, GROUP)],
                                                K.zero_i[:, :], ALU.add).then_inc(staged[b], 1)
                        pool.wait_ge(K.ready, 1)
                        pool.wait_ge(staged[b], i)
                        for t in range(GROUP):
                            nc.gpsimd.indirect_dma_start(
                                out=feat[b][:, t, :], out_offset=None, in_=T["feat"][:, :],
                                in_offset=bass.IndirectOffsetOnAxis(ap=idx_s[b][:, t:t + 1].bitcast(U32), axis=0),
                                bounds_check=bound, oob_is_err=False).then_inc(arrived[b][t], 16)

            @block.tensor
            def _(pe):
                def turn(b, i):
                    pe.wait_ge(s_x[b], i + 1)
                    pe.wait_ge(s_exp[b], i + 1)
                    for t in range(GROUP):
                        last = nc.tensor.transpose(pt[b][:, t, :], Xm[b][:, t, :, :].rearrange("p h n -> p (h n)"), K.ident[:, :])
                    last.then_inc(s_t[b], 1)

                def back(b, i):
                    pe.wait_ge(s_exp[b], i + 2)
                    pe.wait_ge(s_ac[b], i + 1)
                    for t in range(GROUP):
                        last = nc.tensor.matmul(pa[b][:, t * HW:(t + 1) * HW], prob[b][:, t, :], K.ident[0:HW, 0:HW],
                                                start=True, stop=True)
                    last.then_inc(s_a[b], 1)

                def gather(b, i):
                    pe.wait_ge(s_ac[b], i + 2)
                    pe.wait_ge(s_acc, i * (2 * GROUP) + b * GROUP + 1)
                    for t in range(GROUP):
                        pe.wait_ge(arrived[b][t], i * 16 + 16)
                        o = pg[b][t // 2][:, t % 2, :]
                        for h in range(NH):
                            nc.tensor.matmul(o[:, h * WIN:(h + 1) * WIN], feat[b][:, t, h * HD:(h + 1) * HD],
                                             A[b][:, t, h * WIN:(h + 1) * WIN], start=True, stop=True)
                        last = nc.tensor.matmul(o[:, HW:2 * HW], K.ones[:, 0:HD], A[b][:, t, :], start=True, stop=True)
                    last.then_inc(s_ag[b], 1)

                def body(i, first, last):
                    turn(1, i)
                    back(0, i)
                    if not first:
                        gather(1, i - 1)
                    if not last:
                        turn(0, i + 1)
                    back(1, i)
                    gather(0, i)

                turn(0, 0)
                skewed(pe, NP, body)
                gather(1, NP - 1)

            @block.scalar
            def _(act):
                for b in range(2):
                    act.sem_inc(s_exp[b], 1)
                with act.Fori(0, NP) as i:
                    for b in range(2):
                        act.wait_ge(s_t[b], i + 1)
                        act.wait_ge(s_ac[b], i + 1)
                        for t in range(GROUP):
                            last = nc.scalar.activation(prob[b][:, t, :], pt[b][:, t, :], ACT.Exp,
                                                        bias=R.negmax[:, bass.ds(i * (2 * GROUP) + b * GROUP + t, 1)])
                        last.then_inc(s_exp[b], 1)

            @block.vector
            def _(dve):
                nc.vector.memset(acc[:, :, :], 0.0).then_inc(s_acc, 1)
                for b in range(2):
                    dve.sem_inc(s_ac[b], 1)
                    dve.sem_inc(s_ag[b], 1)
                dve.sem_inc(s_acc, GROUP)

                def mask(b, i):
                    masked_logits(nc, dve, K, R, i, b, miss, Xm, s_m1, s_m2, s_x)

                def copy_a(b, i):
                    dve.wait_ge(s_a[b], i + 1)
                    nc.vector.tensor_copy(A[b][:, :, :].rearrange("p t q -> p (t q)"), pa[b][:, 0:GROUP * HW]).then_inc(s_ac[b], 1)

                def add(b, i):
                    dve.wait_ge(s_ag[b], i + 2)
                    for t in range(GROUP):
                        n = i * (2 * GROUP) + b * GROUP + t
                        w = dve.value_load(R.window_i[0:1, bass.ds(n, 1)], min_val=0, max_val=NW - 1)
                        dve.wait_ge(s_acc, n + GROUP + 1)
                        a = acc[:, bass.ds(w, 1), :]
                        nc.vector.tensor_tensor(a, a, pg[b][t // 2][:, t % 2:t % 2 + 1, :], ALU.add).then_inc(s_acc, 1)

                def body(i, first, last):
                    mask(1, i)
                    copy_a(0, i)
                    if not first:
                        add(1, i - 1)
                    if not last:
                        mask(0, i + 1)
                    copy_a(1, i)
                    add(0, i)

                mask(0, 0)
                skewed(dve, NP, body)
                add(1, NP - 1)
                dve.wait_ge(s_acc, NT + GROUP + 1)
                link = chained(dve, s_ch)
                link(nc.vector.tensor_scalar(acc[:, :, HW:2 * HW], acc[:, :, HW:2 * HW], 1e-30, None, ALU.max))
                link(nc.vector.reciprocal(acc[:, :, HW:2 * HW], acc[:, :, HW:2 * HW]))
                link(nc.vector.tensor_tensor(acc[:, :, 0:HW], acc[:, :, 0:HW], acc[:, :, HW:2 * HW], ALU.mult))

        with ExitStack() as banks, nc.Block() as block:
            cb = Ctx(nc, banks)
            pb = [cb.ps(f"ra_pb{b}", [NW, D]) for b in range(2)]
            s_tb, s_add, s_b = cb.sem("ra_tb"), cb.sem("ra_add"), cb.sem("ra_b")

            @block.tensor
            def _(pe):
                for i in range(WIN):
                    if i >= 2:
                        pe.wait_ge(s_add, i - 1)
                    for h in range(NH):
                        last = nc.tensor.transpose(pb[i % 2][:, h * HD:(h + 1) * HD], acc[:, :, h * WIN + i], K.ident[0:HD, 0:HD])
                    last.then_inc(s_tb, 1)

            @block.vector
            def _(dve):
                nc.vector.tensor_tensor(X[:, :, :], X[:, :, :], bias[:, :].unsqueeze(1).to_broadcast([NW, WIN, D]),
                                        ALU.add).then_inc(s_b, 1)
                dve.wait_ge(s_b, 1)
                for i in range(WIN):
                    dve.wait_ge(s_tb, i + 1)
                    nc.vector.tensor_tensor(X[:, i, :], X[:, i, :], pb[i % 2][:, :], ALU.add).then_inc(s_add, 1)


N_SEL = N_NODES // 2 - 1
HID = 1024
NCK = 3
NCHK = WIN // NCK


def token_weights(nc, K, T, Y, R):
    with ExitStack() as stack:
        c = Ctx(nc, stack)
        wr = c.sb("tw_wr", [NW, D])
        br = c.sb("tw_br", [NW, 1])
        prod = c.sb("tw_prod", [NW, WIN, D])
        w = c.sb("tw_w", [NW, WIN])
        every = c.sb("tw_every", [NW, N_NODES])
        larger = c.sb("tw_larger", [NW, 2, N_NODES], BF16)
        above = c.sb("tw_above", [NW, WIN])
        inside = c.sb("tw_inside", [NW, WIN])
        cand = c.sb("tw_cand", [NW, WIN])
        peak = c.sb("tw_peak", [NW, 1])
        peakT = c.sb("tw_peakT", [1, P])
        top = c.sb("tw_top", [1, 1])
        edge = c.sb("tw_edge", [NW, 1])
        tie = c.sb("tw_tie", [NW, WIN])
        order = c.sb("tw_order", [NW, WIN])
        ties = c.sb("tw_ties", [NW, 1])
        before = c.sb("tw_before", [NW, 1])
        room = c.sb("tw_room", [NW, 1])
        p1, p2, p3 = c.ps("tw_p1", [P, 512]), c.ps("tw_p2", [P, 512]), c.ps("tw_p3", [P, 512])
        s_in, s_ch, s_w, s_ws, s_all = c.sem("tw_in"), c.sem("tw_ch"), c.sem("tw_ws"), c.sem("tw_stored"), c.sem("tw_all")
        s_gt, s_peak, s_pt, s_top, s_edge, s_ties, s_bef = [c.sem("tw_s" + n) for n in ("gt", "peak", "pt", "top", "edge", "ties", "bef")]
        with nc.Block() as block:
            @block.sync
            def _(sp):
                sp.dma_start(wr[:, :], spread(T["L0_ffn_wr"].rearrange("d a -> (d a)"), NW, D)).then_inc(s_in, 16)
                sp.dma_start(br[:, :], spread(T["L0_ffn_br"], NW, 1)).then_inc(s_in, 16)
                sp.wait_ge(s_w, 1)
                sp.dma_start(T["order"].rearrange("(w i) -> w i", i=WIN), w[:, :]).then_inc(s_ws, 16)
                sp.wait_ge(s_ws, 16)
                sp.dma_start(every[:, :], spread(T["order"], NW, N_NODES)).then_inc(s_all, 16)

            @block.vector
            def _(dve):
                link = chained(dve, s_ch)
                dve.wait_ge(s_in, 32)
                link(nc.vector.tensor_tensor(prod[:, :, :], Y[:, :, :], wr[:, :].unsqueeze(1).to_broadcast([NW, WIN, D]), ALU.mult))
                link(nc.vector.tensor_reduce(w[:, :], prod[:, :, :], AX, ALU.add))
                nc.vector.tensor_scalar(w[:, :], w[:, :], br[:, :], None, ALU.add).then_inc(s_w, 1)
                dve.wait_ge(s_w, 1)
                dve.wait_ge(s_all, 16)
                for i in range(WIN):
                    if i >= 2:
                        dve.wait_ge(s_gt, i - 1)
                    nc.vector.tensor_scalar(larger[:, i % 2, :], every[:, :], w[:, i:i + 1], 0.0, ALU.is_gt, ALU.add,
                                            accum_out=above[:, i:i + 1]).then_inc(s_gt, 1)
                dve.wait_ge(s_gt, WIN)
                link(nc.vector.tensor_scalar(inside[:, :], above[:, :], float(N_SEL), None, ALU.is_lt))
                link(nc.vector.tensor_scalar(cand[:, :], above[:, :], 1.0, None, ALU.add))
                link(nc.vector.tensor_tensor(cand[:, :], cand[:, :], inside[:, :], ALU.mult))
                nc.vector.tensor_reduce(peak[:, :], cand[:, :], AX, ALU.max).then_inc(s_peak, 1)
                dve.wait_ge(s_pt, 1)
                link(nc.vector.tensor_copy(peakT[:, 0:NW], p1[0:1, 0:NW]))
                nc.vector.tensor_reduce(top[:, :], peakT[:, 0:NW], AX, ALU.max).then_inc(s_top, 1)
                dve.wait_ge(s_edge, 1)
                link(nc.vector.tensor_scalar(edge[:, :], p2[0:NW, 0:1], -1.0, None, ALU.add))
                link(nc.vector.tensor_scalar(tie[:, :], above[:, :], edge[:, :], None, ALU.is_equal))
                nc.vector.tensor_reduce(ties[:, :], tie[:, :], AX, ALU.add).then_inc(s_ties, 1)
                dve.wait_ge(s_bef, 1)
                link(nc.vector.tensor_copy(before[:, :], p3[0:NW, 0:1]))
                link(nc.vector.tensor_tensor_scan(order[:, :], tie[:, :], tie[:, :], before[:, :], ALU.add, ALU.max))
                link(nc.vector.tensor_scalar(room[:, :], edge[:, :], -1.0, float(N_SEL), ALU.mult, ALU.add))
                link(nc.vector.tensor_scalar(order[:, :], order[:, :], room[:, :], None, ALU.is_le))
                link(nc.vector.tensor_tensor(order[:, :], order[:, :], tie[:, :], ALU.mult))
                link(nc.vector.tensor_scalar(inside[:, :], above[:, :], edge[:, :], None, ALU.is_lt))
                link(nc.vector.tensor_tensor(inside[:, :], inside[:, :], order[:, :], ALU.add))
                link(nc.vector.tensor_tensor(R.gate[:, :], inside[:, :], w[:, :], ALU.mult))

            @block.tensor
            def _(pe):
                pe.wait_ge(s_peak, 1)
                nc.tensor.transpose(p1[0:1, 0:NW], peak[:, :], K.ident[0:NW, 0:NW]).then_inc(s_pt, 1)
                pe.wait_ge(s_top, 1)
                nc.tensor.matmul(p2[0:NW, 0:1], K.ones[0:1, 0:NW], top[:, :], start=True, stop=True).then_inc(s_edge, 1)
                pe.wait_ge(s_ties, 1)
                nc.tensor.matmul(p3[0:NW, 0:1], K.before[0:NW, 0:NW], ties[:, :], start=True, stop=True).then_inc(s_bef, 1)


def routed_ffn(nc, K, T, X, Y, YT, R):
    with ExitStack() as stack:
        c = Ctx(nc, stack)
        NH1 = HID // P
        w1 = c.sb("rt_w1", [P, KC, HID])
        w2 = c.sb("rt_w2", [P, NH1, D])
        b1 = c.sb("rt_b1", [P, NH1])
        b2 = c.sb("rt_b2", [NW, D])
        H = [c.sb(f"rt_h{b}", [P, NH1, NCK * NW]) for b in range(2)]
        y = [c.sb(f"rt_y{b}", [NW, D]) for b in range(2)]
        pu = [c.ps(f"rt_pu{b}", [P, 512]) for b in range(3)]
        pd = [c.ps(f"rt_pd{b}", [P, 512]) for b in range(2)]
        s_in, s_u, s_h, s_d, s_y, s_x, s_res, s_hb = [c.sem("rt_s" + n) for n in ("in", "u", "h", "d", "y", "x", "res", "hb")]
        with nc.Block() as block:
            @block.sync
            def _(sp):
                sp.dma_start(w1[:, :, :], T["L0_ffn_w1"].rearrange("(k p) n -> p k n", p=P)).then_inc(s_in, 16)
                sp.dma_start(w2[:, :, :], T["L0_ffn_w2"].rearrange("(k p) n -> p k n", p=P)).then_inc(s_in, 16)
                sp.dma_start(b1[:, :], T["L0_ffn_b1"].rearrange("(k p) -> p k", p=P)).then_inc(s_in, 16)
                sp.dma_start(b2[:, :], spread(T["L0_ffn_b2"], NW, D)).then_inc(s_in, 16)

            @block.tensor
            def _(pe):
                pe.wait_ge(s_in, 64)

                def up(ck):
                    for m in range(NH1):
                        n = ck * NH1 + m
                        if n >= 3:
                            pe.wait_ge(s_h, n - 2)
                        for k in range(KC):
                            last = nc.tensor.matmul(pu[n % 3][:, 0:NCK * NW], w1[:, k, m * P:(m + 1) * P],
                                                    YT[:, k, ck * NCK:(ck + 1) * NCK, :].rearrange("p a w -> p (a w)"),
                                                    start=k == 0, stop=k == KC - 1)
                        last.then_inc(s_u, 1)

                def down(ck):
                    pe.wait_ge(s_h, (ck + 1) * NH1)
                    for a in range(NCK):
                        i = ck * NCK + a
                        if i >= 2:
                            pe.wait_ge(s_y, i - 1)
                        for m in range(NH1):
                            last = nc.tensor.matmul(pd[i % 2][0:NW, 0:D], H[ck % 2][:, m, a * NW:(a + 1) * NW], w2[:, m, :],
                                                    start=m == 0, stop=m == NH1 - 1)
                        last.then_inc(s_d, 1)

                up(0)
                for ck in range(1, NCHK):
                    up(ck)
                    down(ck - 1)
                down(NCHK - 1)

            @block.scalar
            def _(act):
                act.wait_ge(s_in, 64)
                for n in range(NCHK * NH1):
                    ck, m = divmod(n, NH1)
                    act.wait_ge(s_u, n + 1)
                    if m == 0 and ck >= 2:
                        act.wait_ge(s_d, (ck - 1) * NCK)
                    nc.scalar.activation(H[ck % 2][:, m, :], pu[n % 3][:, 0:NCK * NW], ACT.Gelu_apprx_tanh,
                                         bias=b1[:, m:m + 1]).then_inc(s_h, 1)

            @block.vector
            def _(dve):
                dve.wait_ge(s_in, 64)
                nc.vector.tensor_tensor(X[:, :, :], X[:, :, :], Y[:, :, :], ALU.add).then_inc(s_res, 1)
                dve.wait_ge(s_res, 1)
                for i in range(WIN):
                    dve.wait_ge(s_d, i + 1)
                    if i >= 2:
                        dve.wait_ge(s_x, i - 1)
                    nc.vector.tensor_tensor(y[i % 2][:, :], pd[i % 2][0:NW, 0:D], b2[:, :], ALU.add).then_inc(s_y, 1)
                    dve.wait_ge(s_y, i + 1)
                    nc.vector.scalar_tensor_tensor(X[:, i, :], y[i % 2][:, :], R.gate[:, i:i + 1], X[:, i, :],
                                                   ALU.mult, ALU.add).then_inc(s_x, 1)


HO = 2 * D


def load_transposed(nc, K, T, c, tag, items):
    with ExitStack() as stack, nc.Block() as block:
        s = Ctx(nc, stack)
        raw = [s.sb(f"lt_raw{q}_{tag}", [P, KC, D]) for q in range(len(items))]
        bank = [s.ps(f"lt_ps{b}_{tag}", [P, P]) for b in range(2)]
        s_in, s_t, s_c = s.sem(f"lt_in_{tag}"), s.sem(f"lt_t_{tag}"), s.sem(f"lt_c_{tag}")
        pieces = [(q, k, o) for q, (_, _, wide) in enumerate(items) for k in range(D // wide) for o in range(KC)]

        @block.sync
        def _(sp):
            for q, (src, _, _) in enumerate(items):
                sp.dma_start(raw[q][:, :, :], src.rearrange("(o p) n -> p o n", p=P)).then_inc(s_in, 16)

        @block.tensor
        def _(pe):
            pe.wait_ge(s_in, 16 * len(items))
            for n, (q, k, o) in enumerate(pieces):
                wide = items[q][2]
                if n >= 2:
                    pe.wait_ge(s_c, n - 1)
                nc.tensor.transpose(bank[n % 2][0:wide, :], raw[q][:, o, k * wide:(k + 1) * wide], K.ident[:, :]).then_inc(s_t, 1)

        @block.vector
        def _(dve):
            for n, (q, k, o) in enumerate(pieces):
                _, dst, wide = items[q]
                dve.wait_ge(s_t, n + 1)
                nc.vector.tensor_copy(dst[0:wide, k, o * P:(o + 1) * P], bank[n % 2][0:wide, :]).then_inc(s_c, 1)


def node_linear(nc, K, HT, W, bias, dst, tag, func=None, add=None):
    with ExitStack() as stack, nc.Block() as block:
        c = Ctx(nc, stack)
        bank = [c.ps(f"nl_ps{b}_{tag}", [P, 512]) for b in range(2)]
        s_m, s_v, s_r = c.sem(f"nl_m_{tag}"), c.sem(f"nl_v_{tag}"), c.sem(f"nl_r_{tag}")

        @block.tensor
        def _(pe):
            for i in range(WIN):
                if i >= 2:
                    pe.wait_ge(s_v, i - 1)
                for k in range(KC):
                    last = nc.tensor.matmul(bank[i % 2][0:NW, 0:D], HT[:, k, i, :], W[:, k, :], start=k == 0, stop=k == KC - 1)
                last.then_inc(s_m, 1)

        @block.vector
        def _(dve):
            for i in range(WIN):
                dve.wait_ge(s_m, i + 1)
                nc.vector.tensor_tensor(dst[:, i, :], bank[i % 2][0:NW, 0:D], bias[:, :], ALU.add).then_inc(s_v, 1)
            if func == "relu":
                dve.wait_ge(s_v, WIN)
                nc.vector.tensor_scalar(dst[:, :, :], dst[:, :, :], 0.0, None, ALU.max).then_inc(s_r, 1)
            if add is not None:
                dve.wait_ge(s_v, WIN)
                nc.vector.tensor_tensor(add[:, :, :], add[:, :, :], dst[:, :, :], ALU.add).then_inc(s_r, 1)


def load_rows(nc, T, tag, items):
    with ExitStack() as stack, nc.Block() as block:
        s_in = Ctx(nc, stack).sem(f"lr_in_{tag}")

        @block.sync
        def _(sp):
            for dst, src in items:
                sp.dma_start(dst, src).then_inc(s_in, 16)
            sp.wait_ge(s_in, 16 * len(items))


def project_qkv(nc, K, T, HT, QT, Wq, Wkv, bq, bkv):
    with ExitStack() as stack, nc.Block() as block:
        c = Ctx(nc, stack)
        rows = c.sb("pq_rows", [NW, 2, HO])
        bank = [c.ps(f"pq_ps{b}", [P, 512]) for b in range(2)]
        bq_ps = [c.ps(f"pq_q{b}", [P, 512]) for b in range(2)]
        s_kv, s_row, s_q, s_qc = c.sem("pq_kv"), c.sem("pq_row"), c.sem("pq_sq"), c.sem("pq_qc")
        s_st = [c.sem(f"pq_st{b}") for b in range(2)]
        qs = [(h, ck) for h in range(NH) for ck in range(NCHK)]

        @block.tensor
        def _(pe):
            for n in range(max(WIN, len(qs))):
                if n < WIN:
                    if n >= 2:
                        pe.wait_ge(s_row, n - 1)
                    for k in range(KC):
                        last = nc.tensor.matmul(bank[n % 2][0:NW, :], HT[:, k, n, :], Wkv[:, k, :], start=k == 0, stop=k == KC - 1)
                    last.then_inc(s_kv, 1)
                if n < len(qs):
                    h, ck = qs[n]
                    if n >= 2:
                        pe.wait_ge(s_qc, n - 1)
                    for k in range(KC):
                        last = nc.tensor.matmul(bq_ps[n % 2][0:HD, 0:NCK * NW], Wq[:, k, h * HD:(h + 1) * HD],
                                                HT[:, k, ck * NCK:(ck + 1) * NCK, :].rearrange("p a w -> p (a w)"),
                                                start=k == 0, stop=k == KC - 1)
                    last.then_inc(s_q, 1)

        @block.vector
        def _(dve):
            for i in range(WIN):
                dve.wait_ge(s_kv, i + 1)
                if i >= 2:
                    dve.wait_ge(s_st[i % 2], 16 * (i // 2))
                nc.vector.tensor_tensor(rows[:, i % 2, :], bank[i % 2][0:NW, :], bkv[:, :], ALU.add).then_inc(s_row, 1)

        @block.scalar
        def _(act):
            for n, (h, ck) in enumerate(qs):
                act.wait_ge(s_q, n + 1)
                nc.scalar.activation(QT[:, :, h, ck * NCK:(ck + 1) * NCK].rearrange("p w i -> p i w"),
                                     bq_ps[n % 2][0:HD, 0:NCK * NW].rearrange("p (i w) -> p i w", w=NW), ACT.Identity,
                                     bias=bq[:, h:h + 1]).then_inc(s_qc, 1)

        @block.sync
        def _(sp):
            table = T["kv"].rearrange("(w i) d -> w i d", i=WIN)
            for i in range(WIN):
                sp.wait_ge(s_row, i + 1)
                sp.dma_start(table[:, i, :], rows[:, i % 2, :]).then_inc(s_st[i % 2], 16)
            for b in range(2):
                sp.wait_ge(s_st[b], 16 * (WIN // 2))


NTY = 3
AR = HD + NTY


def head_attention(nc, K, T, R, QT, acc):
    with ExitStack() as stack, nc.Block() as block:
        c = Ctx(nc, stack)
        S16 = NH * NH
        idx_s = [c.sb(f"ha_idx{b}", [P, GROUP], I32) for b in range(2)]
        kv = [c.sb(f"ha_kv{b}", [P, GROUP, HO]) for b in range(2)]
        kT = [c.sb(f"ha_kt{t}", [HD, NH, P]) for t in range(GROUP)]
        hot = [c.sb(f"ha_hot{b}", [P, GROUP, WIN], BF16) for b in range(2)]
        typ = [c.sb(f"ha_typ{b}", [P, GROUP, AR], BF16) for b in range(2)]
        none = c.sb("ha_none", [P, AR], BF16)
        M = [c.sb(f"ha_m{b}", [P, S16, WIN]) for b in range(2)]
        s16 = [c.sb(f"ha_s{b}", [P, GROUP, S16]) for b in range(2)]
        mx = [c.sb(f"ha_mx{b}", [P, GROUP, NH]) for b in range(2)]
        A = [c.sb(f"ha_a{b}", [P, GROUP, S16, WIN]) for b in range(2)]
        pk = [c.ps(f"ha_pk{q}", [P, 2, P]) for q in range(2)]
        pS = [c.ps(f"ha_ps{t}", [P, 512]) for t in range(GROUP)]
        pg = [c.ps(f"ha_pg{b}", [AR, GROUP, HW]) for b in range(2)]
        sems = lambda n: [c.sem(f"ha_{n}{b}") for b in range(2)]
        staged, arrived = sems("staged"), [[c.sem(f"ha_arr{b}{t}") for t in range(GROUP)] for b in range(2)]
        s_kt = c.sem("ha_turned")
        s_kc = c.sem("ha_kcopied")
        s_sc = c.sem("ha_scores")
        s_sel = c.sem("ha_selected")
        s_red = c.sem("ha_reduced")
        s_hot, s_typ, s_mx, s_sub, s_exp = sems("hoted"), sems("typed"), sems("max"), sems("sub"), sems("exp")
        s_sum, s_rec, s_nrm, s_A = sems("sum"), sems("rec"), sems("norm"), sems("As")
        s_ag = sems("ag")
        s_acc = c.sem("ha_acc")
        s_z = c.sem("ha_zero")
        NP = NG // 2
        T2 = 2 * GROUP

        @block.gpsimd
        def _(pool):
            bound = nc.gpsimd.to_reg(N_NODES - 1)
            with pool.Fori(1, NP + 1) as i:
                for b in range(2):
                    pool.wait_ge(s_ag[b], i)
                    nc.gpsimd.tensor_tensor(idx_s[b][:, :], R.index[0][:, bass.ds(i * T2 + (b - 2) * GROUP, GROUP)],
                                            K.zero_i[:, :], ALU.add).then_inc(staged[b], 1)
                    pool.wait_ge(K.ready, 1)
                    pool.wait_ge(staged[b], i)
                    for t in range(GROUP):
                        nc.gpsimd.indirect_dma_start(
                            out=kv[b][:, t, :], out_offset=None, in_=T["kv"][:, :],
                            in_offset=bass.IndirectOffsetOnAxis(ap=idx_s[b][:, t:t + 1].bitcast(U32), axis=0),
                            bounds_check=bound, oob_is_err=False).then_inc(arrived[b][t], 16)

        @block.tensor
        def _(pe):
            def turn(b, i, t):
                n = i * T2 + b * GROUP + t
                pe.wait_ge(arrived[b][t], i * 16 + 16)
                pe.wait_ge(s_kc, n + 1)
                for k in range(2):
                    last = nc.tensor.transpose(pk[t % 2][:, k, :], kv[b][:, t, k * P:(k + 1) * P], K.ident[:, :])
                last.then_inc(s_kt, 1)

            def score(b, i, t):
                n = i * T2 + b * GROUP + t
                pe.wait_ge(s_kc, n + 3)
                pe.wait_ge(s_sel, n + 1)
                w = pe.value_load(R.window_i[0:1, bass.ds(n, 1)], min_val=0, max_val=NW - 1)
                for g in range(NH):
                    last = nc.tensor.matmul(pS[t][:, g * HW:(g + 1) * HW], kT[t][:, g, :],
                                            QT[:, bass.ds(w, 1), :, :].rearrange("p a h n -> p (a h n)"),
                                            start=True, stop=True)
                last.then_inc(s_sc, 1)

            def gather(b, i):
                pe.wait_ge(s_A[b], i * GROUP + GROUP)
                pe.wait_ge(s_typ[b], i + 1)
                pe.wait_ge(s_acc, i * T2 + b * GROUP + 1)
                for t in range(GROUP):
                    o = pg[b][:, t, :]
                    at_node = hot[b][:, t, :].unsqueeze(1).to_broadcast([P, NH, WIN])
                    nc.tensor.matmul(o, typ[b][:, t, :], at_node, start=True, stop=False)
                    for g in range(NH):
                        nc.tensor.matmul(o[0:HD, :], kv[b][:, t, D + g * HD:D + (g + 1) * HD],
                                         A[b][:, t, g * NH:(g + 1) * NH, :].rearrange("p h n -> p (h n)"),
                                         start=False, stop=False)
                    last = nc.tensor.matmul(o, none[:, :], at_node, start=False, stop=True)
                last.then_inc(s_ag[b], 1)

            def scores(b, i):
                turn(b, i, 0)
                for t in range(GROUP):
                    if t + 1 < GROUP:
                        turn(b, i, t + 1)
                    score(b, i, t)

            def body(i, first, last):
                scores(0, i)
                if not first:
                    gather(1, i - 1)
                scores(1, i)
                gather(0, i)

            skewed(pe, NP, body)
            gather(1, NP - 1)

        @block.scalar
        def _(act):
            act.sem_inc(s_kc, 2)
            act.sem_inc(s_sc, GROUP)

            def body(i, first, last):
                for b in range(2):
                    for t in range(GROUP):
                        n = i * T2 + b * GROUP + t
                        act.wait_ge(s_kt, n + 1)
                        act.wait_ge(s_sc, n + 1)
                        nc.scalar.copy(kT[t][:, 0::2, :], pk[t % 2][0:HD, :, :])
                        nc.scalar.copy(kT[t][:, 1::2, :], pk[t % 2][HD:P, :, :]).then_inc(s_kc, 1)
                        if t == 1:
                            if b == 1:
                                exps(0, i)
                            elif not first:
                                exps(1, i - 1)

            def exps(b, i):
                act.wait_ge(s_sub[b], i + 1)
                nc.scalar.activation(s16[b][:, :, :], s16[b][:, :, :], ACT.Exp, scale=HD ** -0.5).then_inc(s_exp[b], 1)

            skewed(act, NP, body)
            exps(1, NP - 1)

        @block.vector
        def _(dve):
            nc.vector.memset(acc[:, :, :], 0.0).then_inc(s_acc, 1)
            nc.vector.memset(none[:, :], 0.0).then_inc(s_z, 1)
            for b in range(2):
                nc.vector.memset(typ[b][:, :, :], 0.0).then_inc(s_z, 1)
                dve.sem_inc(s_ag[b], 1)
            dve.sem_inc(s_acc, GROUP)
            dve.sem_inc(s_sel, GROUP)
            dve.wait_ge(s_z, 3)

            def select(b, i):
                j0 = i * T2 + b * GROUP
                dve.wait_ge(s_ag[b], i + 1)
                nc.vector.tensor_tensor(hot[b][:, :, :], R.node[:, bass.ds(j0, GROUP)].unsqueeze(2).to_broadcast([P, GROUP, WIN]),
                                        K.iota[:, :].unsqueeze(1).to_broadcast([P, GROUP, WIN]), ALU.is_equal).then_inc(s_hot[b], 1)
                nc.vector.tensor_tensor(typ[b][:, :, HD:AR], R.type[:, bass.ds(j0, GROUP)].unsqueeze(2).to_broadcast([P, GROUP, NTY]),
                                        K.iota[:, 0:NTY].unsqueeze(1).to_broadcast([P, GROUP, NTY]), ALU.is_equal).then_inc(s_typ[b], 1)
                dve.wait_ge(s_hot[b], i + 1)
                for t in range(GROUP):
                    n = j0 + t
                    dve.wait_ge(s_sc, n + GROUP + 1)
                    dve.wait_ge(s_red, n) if not (isinstance(n, int) and n == 0) else None
                    nc.vector.tensor_tensor(M[t % 2][:, :, :], pS[t][:, 0:S16 * WIN].rearrange("p (q n) -> p q n", n=WIN),
                                            hot[b][:, t, :].unsqueeze(1).to_broadcast([P, S16, WIN]), ALU.mult).then_inc(s_sel, 1)
                    dve.wait_ge(s_sel, n + GROUP + 1)
                    nc.vector.tensor_reduce(s16[b][:, t, :], M[t % 2][:, :, :], AX, ALU.add).then_inc(s_red, 1)
                dve.wait_ge(s_red, j0 + GROUP)
                nc.vector.tensor_reduce(mx[b][:, :, :], s16[b][:, :, :].rearrange("p t (g h) -> p t h g", h=NH), AX, ALU.max).then_inc(s_mx[b], 1)
                dve.wait_ge(s_mx[b], i + 1)
                q = s16[b][:, :, :].rearrange("p t (g h) -> p t g h", h=NH)
                nc.vector.tensor_tensor(q, q, mx[b][:, :, :].unsqueeze(2).to_broadcast([P, GROUP, NH, NH]), ALU.subtract).then_inc(s_sub[b], 1)

            def spread_out(b, i):
                dve.wait_ge(s_exp[b], i + 1)
                nc.vector.tensor_reduce(mx[b][:, :, :], s16[b][:, :, :].rearrange("p t (g h) -> p t h g", h=NH), AX, ALU.add).then_inc(s_sum[b], 1)
                dve.wait_ge(s_sum[b], i + 1)
                nc.vector.reciprocal(mx[b][:, :, :], mx[b][:, :, :]).then_inc(s_rec[b], 1)
                dve.wait_ge(s_rec[b], i + 1)
                q = s16[b][:, :, :].rearrange("p t (g h) -> p t g h", h=NH)
                nc.vector.tensor_tensor(q, q, mx[b][:, :, :].unsqueeze(2).to_broadcast([P, GROUP, NH, NH]), ALU.mult).then_inc(s_nrm[b], 1)
                dve.wait_ge(s_nrm[b], i + 1)
                for t in range(GROUP):
                    nc.vector.tensor_tensor(A[b][:, t, :, :], s16[b][:, t, :].unsqueeze(2).to_broadcast([P, S16, WIN]),
                                            hot[b][:, t, :].unsqueeze(1).to_broadcast([P, S16, WIN]), ALU.mult).then_inc(s_A[b], 1)

            def add(b, i):
                dve.wait_ge(s_ag[b], i + 2)
                ws = []
                for t in range(GROUP):
                    ws.append(dve.value_load(R.window_i[0:1, bass.ds(i * T2 + b * GROUP + t, 1)], min_val=0, max_val=NW - 1))
                for t in range(GROUP):
                    n = i * T2 + b * GROUP + t
                    dve.wait_ge(s_acc, n + GROUP + 1)
                    a = acc[:, bass.ds(ws[t], 1), :]
                    nc.vector.tensor_tensor(a, a, pg[b][:, t:t + 1, :], ALU.add).then_inc(s_acc, 1)

            def body(i, first, last):
                select(0, i)
                if not first:
                    spread_out(1, i - 1)
                    add(0, i - 1)
                select(1, i)
                spread_out(0, i)
                if not first:
                    add(1, i - 1)

            skewed(dve, NP, body)
            spread_out(1, NP - 1)
            add(0, NP - 1)
            add(1, NP - 1)
            dve.wait_ge(s_acc, NT + GROUP + 1)


def node_update(nc, K, acc, Wo, H, tag):
    with ExitStack() as stack, nc.Block() as block:
        c = Ctx(nc, stack)
        bank = [c.ps(f"nu_ps{b}_{tag}", [P, 512]) for b in range(2)]
        s_m, s_v = c.sem(f"nu_m_{tag}"), c.sem(f"nu_v_{tag}")

        @block.tensor
        def _(pe):
            for i in range(WIN):
                if i >= 2:
                    pe.wait_ge(s_v, i - 1)
                for h in range(NH):
                    rows = AR if h == 0 else HD
                    last = nc.tensor.matmul(bank[i % 2][0:NW, 0:D], acc[0:rows, :, h * WIN + i], Wo[0:rows, h, :],
                                            start=h == 0, stop=h == NH - 1)
                last.then_inc(s_m, 1)

        @block.vector
        def _(dve):
            for i in range(WIN):
                dve.wait_ge(s_m, i + 1)
                nc.vector.tensor_tensor(H[:, i, :], H[:, i, :], bank[i % 2][0:NW, 0:D], ALU.add).then_inc(s_v, 1)


def edge_type_rows(nc, K, T, l, Wo, tag):
    with ExitStack() as stack, nc.Block() as block:
        c = Ctx(nc, stack)
        E = c.sb("et_e_" + tag, [NTY, D])
        bo = c.sb("et_bo_" + tag, [NTY, D])
        ET = c.sb("et_et_" + tag, [HD, NH, NTY])
        ew = c.sb("et_ew_" + tag, [NTY, D])
        pe_t = c.ps("et_pt_" + tag, [HD, NH, NTY])
        pe_o = c.ps("et_po_" + tag, [NTY, D])
        s_in, s_t, s_c, s_m, s_o, s_w = [c.sem(f"et_{n}_{tag}") for n in ("in", "t", "c", "m", "o", "w")]

        @block.sync
        def _(sp):
            sp.dma_start(E[:, :], T["L1_gnn_Eemb"][l]).then_inc(s_in, 16)
            sp.dma_start(bo[:, :], spread(T["L1_gnn_bo"][l], NTY, D)).then_inc(s_in, 16)
            sp.wait_ge(s_o, 1)
            sp.dma_start(Wo[HD:AR, 0, :], ew[:, :]).then_inc(s_w, 16)
            sp.wait_ge(s_w, 16)

        @block.tensor
        def _(pe):
            pe.wait_ge(s_in, 32)
            for h in range(NH):
                last = nc.tensor.transpose(pe_t[:, h, :], E[:, h * HD:(h + 1) * HD], K.ident[0:NTY, 0:NTY])
            last.then_inc(s_t, 1)
            pe.wait_ge(s_c, 1)
            for h in range(NH):
                last = nc.tensor.matmul(pe_o[:, :], ET[:, h, :], Wo[0:HD, h, :], start=h == 0, stop=h == NH - 1)
            last.then_inc(s_m, 1)

        @block.vector
        def _(dve):
            dve.wait_ge(s_t, 1)
            nc.vector.tensor_copy(ET[:, :, :], pe_t[:, :, :]).then_inc(s_c, 1)
            dve.wait_ge(s_m, 1)
            nc.vector.tensor_tensor(ew[:, :], pe_o[:, :], bo[:, :], ALU.add).then_inc(s_o, 1)


def scale_relu(nc, H, g, b, tag):
    with ExitStack() as stack, nc.Block() as block:
        s_ch = Ctx(nc, stack).sem("sr_ch_" + tag)

        @block.vector
        def _(dve):
            link = chained(dve, s_ch)
            link(nc.vector.tensor_tensor(H[:, :, :], H[:, :, :], g[:, :].unsqueeze(1).to_broadcast([NW, WIN, D]), ALU.mult))
            link(nc.vector.tensor_tensor(H[:, :, :], H[:, :, :], b[:, :].unsqueeze(1).to_broadcast([NW, WIN, D]), ALU.add))
            link(nc.vector.tensor_scalar(H[:, :, :], H[:, :, :], 0.0, None, ALU.max))


def message_layers(nc, K, T, R, H):
    for l in range(3):
        tag = f"l{l}"
        with ExitStack() as stack:
            c = Ctx(nc, stack)
            QT = c.sb("qt_" + tag, [HD, NW, NH, WIN])
            Wo = c.sb("wo_" + tag, [AR, NH, D])
            with ExitStack() as inner:
                ci = Ctx(nc, inner)
                HT = ci.sb("ht_" + tag, [P, KC, WIN, NW])
                Wq = ci.sb("wq_" + tag, [P, KC, D])
                Wkv = ci.sb("wkv_" + tag, [P, KC, HO])
                bq = ci.sb("bq_" + tag, [HD, NH])
                bkv = ci.sb("bkv_" + tag, [NW, HO])
                load_rows(nc, T, tag, [(bkv[:, 0:D], spread(T["L1_gnn_bk"][l], NW, D)), (bkv[:, D:HO], spread(T["L1_gnn_bv"][l], NW, D)),
                                       (bq[:, :], T["L1_gnn_bq"][l].rearrange("(h d) -> d h", h=NH))])
                load_transposed(nc, K, T, ci, tag, [(T["L1_gnn_Wq"][l], Wq, P), (T["L1_gnn_Wk"][l], Wkv[:, :, 0:D], P),
                                                    (T["L1_gnn_Wv"][l], Wkv[:, :, D:HO], P), (T["L1_gnn_Wo"][l], Wo, HD)])
                edge_type_rows(nc, K, T, l, Wo, tag)
                transpose_nodes(nc, K, H, HT, tag)
                project_qkv(nc, K, T, HT, QT, Wq, Wkv, bq, bkv)
            acc = c.sb("acc_" + tag, [AR, NW, HW])
            head_attention(nc, K, T, R, QT, acc)
            node_update(nc, K, acc, Wo, H, tag)
        layernorm(nc, K, H, H, tag)
        with ExitStack() as stack:
            c = Ctx(nc, stack)
            g, b = c.sb("ln_gain_" + tag, [NW, D]), c.sb("ln_bias_" + tag, [NW, D])
            load_rows(nc, T, tag + "b", [(g[:, :], spread(T["L1_gnn_ln_g"][l], NW, D)), (b[:, :], spread(T["L1_gnn_ln_b"][l], NW, D))])
            scale_relu(nc, H, g, b, tag)


NE = 4
EH1, EH2 = 128, 64


def expert_gates(nc, K, T, YT, R):
    with ExitStack() as stack, nc.Block() as block:
        c = Ctx(nc, stack)
        gW, gb = c.sb("eg_w", [P, KC, NE]), c.sb("eg_b", [NW, NE])
        G, cmp = c.sb("eg_g", [NW, WIN, NE]), c.sb("eg_cmp", [NW, WIN, NE])
        rank, red = c.sb("eg_rank", [NW, WIN, NE]), c.sb("eg_red", [NW, WIN])
        pg = c.ps("eg_ps", [NW, WIN, NE])
        s_in, s_m, s_ch, s_e, s_x = [c.sem("eg_s" + n) for n in ("in", "m", "ch", "e", "x")]
        wide = red[:, :].unsqueeze(2).to_broadcast([NW, WIN, NE])

        @block.sync
        def _(sp):
            sp.dma_start(gW[:, :, :], T["L1_ffn_gW"].rearrange("(k p) e -> p k e", p=P)).then_inc(s_in, 16)
            sp.dma_start(gb[:, :], spread(T["L1_ffn_gb"], NW, NE)).then_inc(s_in, 16)

        @block.tensor
        def _(pe):
            pe.wait_ge(s_in, 32)
            for i in range(WIN):
                for k in range(KC):
                    last = nc.tensor.matmul(pg[:, i, :], YT[:, k, i, :], gW[:, k, :], start=k == 0, stop=k == KC - 1)
            last.then_inc(s_m, 1)

        @block.vector
        def _(dve):
            link = chained(dve, s_ch)
            dve.wait_ge(s_in, 32)
            dve.wait_ge(s_m, 1)
            link(nc.vector.tensor_tensor(G[:, :, :], pg[:, :, :], gb[:, :].unsqueeze(1).to_broadcast([NW, WIN, NE]), ALU.add))
            link(nc.vector.tensor_reduce(red[:, :], G[:, :, :], AX, ALU.max))
            nc.vector.tensor_tensor(G[:, :, :], G[:, :, :], wide, ALU.subtract).then_inc(s_x, 1)
            dve.wait_ge(s_e, 1)
            link(nc.vector.tensor_reduce(red[:, :], G[:, :, :], AX, ALU.add))
            link(nc.vector.reciprocal(red[:, :], red[:, :]))
            link(nc.vector.tensor_tensor(G[:, :, :], G[:, :, :], wide, ALU.mult))
            for e in range(NE):
                own = G[:, :, e:e + 1]
                if e:
                    link(nc.vector.tensor_tensor(cmp[:, :, 0:e], G[:, :, 0:e], own.to_broadcast([NW, WIN, e]), ALU.is_ge))
                link(nc.vector.tensor_tensor(cmp[:, :, e:NE], G[:, :, e:NE], own.to_broadcast([NW, WIN, NE - e]), ALU.is_gt))
                link(nc.vector.tensor_reduce(rank[:, :, e], cmp[:, :, :], AX, ALU.add))
            link(nc.vector.tensor_scalar(rank[:, :, :], rank[:, :, :], 2.0, None, ALU.is_lt))
            link(nc.vector.tensor_reduce(red[:, :], G[:, :, :], AX, ALU.max))
            nc.vector.tensor_tensor(G[:, :, :], G[:, :, :], wide, ALU.subtract).then_inc(s_x, 1)
            dve.wait_ge(s_e, 2)
            link(nc.vector.tensor_tensor(G[:, :, :], G[:, :, :], rank[:, :, :], ALU.mult))
            link(nc.vector.tensor_reduce(red[:, :], G[:, :, :], AX, ALU.add))
            link(nc.vector.reciprocal(red[:, :], red[:, :]))
            link(nc.vector.tensor_tensor(R.share[:, :, :], G[:, :, :], wide, ALU.mult))

        @block.scalar
        def _(act):
            for n in range(2):
                act.wait_ge(s_x, n + 1)
                nc.scalar.activation(G[:, :, :], G[:, :, :], ACT.Exp).then_inc(s_e, 1)


def expert_ffn(nc, K, T, X, YT, R):
    with ExitStack() as stack, nc.Block() as block:
        c = Ctx(nc, stack)
        sW1, sW2, sW3 = c.sb("ef_s1", [P, KC, D]), c.sb("ef_s2", [P, KC, P]), c.sb("ef_s3", [P, D])
        sb1, sb2, sb3 = c.sb("ef_sb1", [P, KC]), c.sb("ef_sb2", [P, 1]), c.sb("ef_sb3", [NW, D])
        eW1, eW2 = c.sb("ef_e1", [P, NE, KC, EH1]), c.sb("ef_e2", [P, NE, EH2])
        eW3 = c.sb("ef_e3", [EH2 + 1, NE, D])
        eb1, eb2 = c.sb("ef_eb1", [P, NE]), c.sb("ef_eb2", [EH2, NE])
        NN = NCK * NW
        h1 = [c.sb(f"ef_h1{b}", [P, KC + NE, NN]) for b in range(2)]
        h2 = [c.sb(f"ef_h2{b}", [P, NN]) for b in range(2)]
        e2 = [c.sb(f"ef_g2{b}", [EH2 + 1, NE, NN]) for b in range(2)]
        pu = [c.ps(f"ef_pu{b}", [P, 512]) for b in range(4)]
        po = [c.ps(f"ef_po{b}", [P, 512]) for b in range(3)]
        s_in, s_u, s_a, s_o, s_x, s_one, s_b = [c.sem("ef_s" + n) for n in ("in", "u", "a", "o", "x", "one", "b")]
        s_1, s_2 = c.sem("ef_l1"), c.sem("ef_l2")
        loads = [(sW1[:, :, :], T["L1_ffn_sW1"].rearrange("(k p) n -> p k n", p=P)),
                 (sW2[:, :, :], T["L1_ffn_sW2"].rearrange("(k p) n -> p k n", p=P)), (sW3[:, :], T["L1_ffn_sW3"]),
                 (sb1[:, :], T["L1_ffn_sb1"].rearrange("(k p) -> p k", p=P)), (sb2[:, :], T["L1_ffn_sb2"].unsqueeze(1)),
                 (sb3[:, :], spread(T["L1_ffn_sb3"], NW, D)),
                 (eW2[:, :, :], T["L1_ffn_eW2"].rearrange("e p n -> p e n")),
                 (eW3[0:EH2, :, :], T["L1_ffn_eW3"].rearrange("e p n -> p e n")),
                 (eW3[EH2:EH2 + 1, :, :], T["L1_ffn_eb3"].unsqueeze(0)),
                 (eb1[:, :], T["L1_ffn_eb1"].rearrange("e p -> p e")), (eb2[:, :], T["L1_ffn_eb2"].rearrange("e p -> p e"))]
        loads += [(eW1[:, e, :, :], T["L1_ffn_eW1"][e].rearrange("(k p) n -> p k n", p=P)) for e in range(NE)]
        L1, L2 = KC + NE, 1 + NE
        NU = L1 + L2

        @block.sync
        def _(sp):
            for dst, src in loads:
                sp.dma_start(dst, src).then_inc(s_in, 16)
            sp.wait_ge(s_in, 16 * len(loads))

        @block.tensor
        def _(pe):
            pe.wait_ge(s_in, 16 * len(loads))
            pe.wait_ge(s_one, 2)

            def unit(ck, u):
                n = ck * NU + u
                if n >= 4:
                    pe.wait_ge(s_a, n - 3)
                bank = pu[n % 4]
                cols = YT[:, :, ck * NCK:(ck + 1) * NCK, :].rearrange("p k a w -> p k (a w)")
                if u < L1:
                    for k in range(KC):
                        w = sW1[:, k, u * P:(u + 1) * P] if u < KC else eW1[:, u - KC, k, :]
                        last = nc.tensor.matmul(bank[:, 0:NN], w, cols[:, k, :], start=k == 0, stop=k == KC - 1)
                elif u == L1:
                    pe.wait_ge(s_a, ck * NU + L1)
                    for k in range(KC):
                        last = nc.tensor.matmul(bank[:, 0:NN], sW2[:, k, :], h1[ck % 2][:, k, :], start=k == 0, stop=k == KC - 1)
                else:
                    e = u - L1 - 1
                    last = nc.tensor.matmul(bank[0:EH2, 0:NN], eW2[:, e, :], h1[ck % 2][:, KC + e, :], start=True, stop=True)
                last.then_inc(s_u, 1)

            def outputs(ck):
                pe.wait_ge(s_a, (ck + 1) * NU)
                for a in range(NCK):
                    for v in range(1 + NE):
                        n = (ck * NCK + a) * (1 + NE) + v
                        if n >= 3:
                            pe.wait_ge(s_x, n - 2)
                        part = slice(a * NW, (a + 1) * NW)
                        o = po[n % 3][0:NW, 0:D]
                        if v == 0:
                            nc.tensor.matmul(o, h2[ck % 2][:, part], sW3[:, :], start=True, stop=True).then_inc(s_o, 1)
                        else:
                            nc.tensor.matmul(o, e2[ck % 2][:, v - 1, part], eW3[:, v - 1, :], start=True, stop=True).then_inc(s_o, 1)

            for ck in range(NCHK):
                for u in range(NU):
                    unit(ck, u)
                if ck:
                    outputs(ck - 1)
            outputs(NCHK - 1)

        @block.scalar
        def _(act):
            act.wait_ge(s_in, 16 * len(loads))
            for ck in range(NCHK):
                for u in range(NU):
                    n = ck * NU + u
                    act.wait_ge(s_u, n + 1)
                    if u == 0 and ck >= 2:
                        act.wait_ge(s_o, (ck - 1) * NCK * (1 + NE))
                    if u < L1:
                        dst, src = h1[ck % 2][:, u, :], pu[n % 4][:, 0:NN]
                        bias = sb1[:, u:u + 1] if u < KC else eb1[:, u - KC:u - KC + 1]
                    elif u == L1:
                        dst, src, bias = h2[ck % 2][:, :], pu[n % 4][:, 0:NN], sb2[:, :]
                    else:
                        e = u - L1 - 1
                        dst, src, bias = e2[ck % 2][0:EH2, e, :], pu[n % 4][0:EH2, 0:NN], eb2[:, e:e + 1]
                    nc.scalar.activation(dst, src, ACT.Relu, bias=bias).then_inc(s_a, 1)

        @block.gpsimd
        def _(pool):
            for b in range(2):
                nc.gpsimd.memset(e2[b][EH2:EH2 + 1, :, :], 1.0).then_inc(s_one, 1)

        @block.vector
        def _(dve):
            dve.wait_ge(s_in, 16 * len(loads))
            nc.vector.tensor_tensor(X[:, :, :], X[:, :, :], sb3[:, :].unsqueeze(1).to_broadcast([NW, WIN, D]), ALU.add).then_inc(s_b, 1)
            dve.wait_ge(s_b, 1)
            for i in range(WIN):
                for v in range(1 + NE):
                    n = i * (1 + NE) + v
                    dve.wait_ge(s_o, n + 1)
                    if n:
                        dve.wait_ge(s_x, n)
                    if v == 0:
                        nc.vector.tensor_tensor(X[:, i, :], X[:, i, :], po[n % 3][0:NW, 0:D], ALU.add).then_inc(s_x, 1)
                    else:
                        nc.vector.scalar_tensor_tensor(X[:, i, :], po[n % 3][0:NW, 0:D], R.share[:, i, v - 1:v], X[:, i, :],
                                                       ALU.mult, ALU.add).then_inc(s_x, 1)


def node_rows(ap):
    return ap.rearrange("(w i) d -> w i d", i=WIN)


def build(nc, T, out):
    Ctx.used.clear()
    with ExitStack() as stack:
        stack.enter_context(nc.allow_non_contiguous_dma(reason="biases of a few hundred elements, one per partition"))
        c = Ctx(nc, stack)
        K = Bag()
        K.ident = c.sb("identity", [P, P])
        K.ones = c.sb("ones", [P, P])
        K.before = c.sb("before", [P, P])
        K.iota = c.sb("iota_window", [P, WIN], BF16)
        K.part = c.sb("iota_partition", [P, 1])
        K.tile_no = c.sb("iota_tile", [P, NT])
        K.zero_i = c.sb("zero_i", [P, GROUP], I32)
        K.ready = c.sem("constants_ready")
        X = c.sb("x", [NW, WIN, D])
        constants(nc, K)

        load_rows(nc, T, "x", [(X[:, :, :], node_rows(T["x"]))])
        with ExitStack() as st:
            c1 = Ctx(nc, st)
            Y, YT = c1.sb("y0", [NW, WIN, D]), c1.sb("yt0", [P, KC, WIN, NW])
            layernorm(nc, K, X, Y, "a")
            transpose_nodes(nc, K, Y, YT, "a")
            relation_features(nc, K, T, YT)
        with ExitStack() as st:
            c1 = Ctx(nc, st)
            R = Bag()
            R.window, R.window_i = c1.sb("win0", [P, NT]), c1.sb("wini0", [1, NT], I32)
            R.index = [c1.sb(f"idx0{f}", [P, NT], I32) for f in range(2)]
            R.node = c1.sb("node0", [P, NT], BF16)
            sort_edges(nc, K, T, "dst", [[("src", NREL), ("edge_type_8", 1)], [("dst", NREL), ("edge_type_8", 1)]],
                       "slots0", "bucket0", "s0", R)
            R.ev, R.negmax = c1.sb("ev", [P, NT, NH]), c1.sb("negmax", [HW, NT])
            edge_logits(nc, K, T, R)
            relation_attention(nc, K, T, R, X)

        with ExitStack() as st:
            c1 = Ctx(nc, st)
            R = Bag()
            Y, YT, R.gate = c1.sb("y1", [NW, WIN, D]), c1.sb("yt1", [P, KC, WIN, NW]), c1.sb("gate", [NW, WIN])
            layernorm(nc, K, X, Y, "b")
            token_weights(nc, K, T, Y, R)
            transpose_nodes(nc, K, Y, YT, "b")
            routed_ffn(nc, K, T, X, Y, YT, R)

        with ExitStack() as st:
            c1 = Ctx(nc, st)
            Y, YT = c1.sb("y2", [NW, WIN, D]), c1.sb("yt2", [P, KC, WIN, NW])
            WinT, b_in = c1.sb("win_t", [P, KC, D]), c1.sb("b_in", [NW, D])
            layernorm(nc, K, X, Y, "c")
            s_sum, s_park = c1.sem("residual"), c1.sem("parked")
            with nc.Block() as block:
                @block.vector
                def _(dve):
                    nc.vector.tensor_tensor(X[:, :, :], X[:, :, :], Y[:, :, :], ALU.add).then_inc(s_sum, 1)

                @block.sync
                def _(sp):
                    sp.wait_ge(s_sum, 1)
                    sp.dma_start(node_rows(T["park"]), X[:, :, :]).then_inc(s_park, 16)
                    sp.wait_ge(s_park, 16)
            load_rows(nc, T, "win", [(b_in[:, :], spread(T["L1_gnn_b_in"], NW, D))])
            load_transposed(nc, K, T, c1, "win", [(T["L1_gnn_Win"], WinT, P)])
            transpose_nodes(nc, K, Y, YT, "c")
            node_linear(nc, K, YT, WinT, b_in, X, "win")
        H = X
        with ExitStack() as st:
            c1 = Ctx(nc, st)
            R = Bag()
            R.window_i, R.node, R.type = c1.sb("wini1", [1, NT], I32), c1.sb("node1", [P, NT], BF16), c1.sb("type1", [P, NT], BF16)
            R.index = [c1.sb("idx10", [P, NT], I32), R.type]
            with ExitStack() as st2:
                R.window = Ctx(nc, st2).sb("win1", [P, NT])
                sort_edges(nc, K, T, "src", [[("dst", 1)], [("edge_type_3", 1)]], "slots1", "bucket1", "s1", R)
            message_layers(nc, K, T, R, H)
        with ExitStack() as st:
            c1 = Ctx(nc, st)
            HT, B = c1.sb("ht_adj", [P, KC, WIN, NW]), c1.sb("adj", [NW, WIN, D])
            W1T, W2T = c1.sb("w1_t", [P, KC, D]), c1.sb("w2_t", [P, KC, D])
            b1, b2 = c1.sb("b1_adj", [NW, D]), c1.sb("b2_adj", [NW, D])
            load_rows(nc, T, "adj", [(b1[:, :], spread(T["L1_gnn_b1"], NW, D)), (b2[:, :], spread(T["L1_gnn_b2"], NW, D))])
            load_transposed(nc, K, T, c1, "adj", [(T["L1_gnn_W1"], W1T, P), (T["L1_gnn_W2"], W2T, P)])
            transpose_nodes(nc, K, H, HT, "adj1")
            node_linear(nc, K, HT, W1T, b1, B, "adj1", func="relu")
            load_rows(nc, T, "park", [(X[:, :, :], node_rows(T["park"]))])
            transpose_nodes(nc, K, B, HT, "adj2")
            node_linear(nc, K, HT, W2T, b2, B, "adj2", add=X)

        with ExitStack() as st:
            c1 = Ctx(nc, st)
            R = Bag()
            Y, YT, R.share = c1.sb("y3", [NW, WIN, D]), c1.sb("yt3", [P, KC, WIN, NW]), c1.sb("share", [NW, WIN, NE])
            layernorm(nc, K, X, Y, "d")
            transpose_nodes(nc, K, Y, YT, "d")
            expert_gates(nc, K, T, YT, R)
            expert_ffn(nc, K, T, X, YT, R)
        stored = c.sem("output_stored")
        with nc.Block() as block:
            @block.sync
            def _(sp):
                sp.dma_start(node_rows(out), X[:, :, :]).then_inc(stored, 16)
                sp.wait_ge(stored, 16)


SCRATCH = [("feat", (N_NODES * NREL, D), F32), ("logit0", (N_NODES * NREL, NH), F32), ("logit1", (N_NODES * NREL, NH), F32),
           ("bucket0", (N_EDGES,), BF16), ("bucket1", (N_EDGES,), BF16), ("slots0", (P * NT, 4), F32), ("slots1", (P * NT, 4), F32),
           ("order", (N_NODES,), F32), ("park", (N_NODES, D), F32), ("kv", (N_NODES, 2 * D), F32)]


def kernel(**inputs):
    import numpy as _np
    import concourse.bacc as _bacc
    from concourse import mybir as _mybir
    from concourse.bass_utils import run_bass_kernel_spmd as _run
    nc = _bacc.Bacc("TRN2", target_bir_lowering=False, num_devices=1)
    arrays, T = {}, {}
    for name, value in inputs.items():
        a = _np.ascontiguousarray(value)
        arrays[f"in_{name}"] = a
        T[name] = nc.dram_tensor(f"in_{name}", a.shape, _mybir.dt.from_np(a.dtype), kind="ExternalInput").ap()
    for name, shape, dt in SCRATCH:
        T[name] = nc.dram_tensor(f"scratch_{name}", shape, dt).ap()
    out = nc.dram_tensor("out_x", (N_NODES, D), F32, kind="ExternalOutput").ap()
    build(nc, T, out)
    r = _run(nc, [arrays], core_ids=[0])
    return r.results[0]["out_x"]
```

```python
import concourse.bass as bass
from concourse import mybir
from contextlib import ExitStack

F32 = mybir.dt.float32
BF16 = mybir.dt.bfloat16
I32 = mybir.dt.int32
U32 = mybir.dt.uint32
ALU = mybir.AluOpType
ACT = mybir.ActivationFunctionType
AX = mybir.AxisListType.X

P = 128
N_NODES, D = 3750, 256
N_EDGES = 60000
KC = D // P
NH, HD = 4, 64
NREL = 8
WIN = 30
NW = N_NODES // WIN
HW = NH * WIN
GROUP = 4
NT = -(-((N_EDGES + (P - 1) * NW) // P) // (6 * GROUP)) * 6 * GROUP
NG = NT // GROUP
SLICE = 120
NSL = N_EDGES // SLICE
SB = 4
SK = NSL // SB
CH = 20
NCH = NSL // CH
ROUND = 12582912.0
NEG = -1.0e30
FLOOR = -1.0e20
EPS = 1e-5
FROW = NREL * D
PADTGT = 0


class Ctx:

    def __init__(self, nc, stack):
        self.nc, self.stack, self.sems = nc, stack, []

    used = {}

    def own(self, name):
        n = self.used[name] = self.used.get(name, 0) + 1
        return name if n == 1 else f"{name}_{n}"

    def sb(self, name, shape, dt=F32):
        return self.stack.enter_context(self.nc.sbuf_tensor(self.own(name), shape, dt))

    def ps(self, name, shape):
        bank = self.stack.enter_context(self.nc.psum_tensor(self.own(name), [P, 512], F32))
        n = 1
        for m in shape[1:]:
            n *= m
        view = bank[0:shape[0], 0:n]
        return view if len(shape) == 2 else view.rearrange("p (a b) -> p a b", b=shape[2])

    def sem(self, name):
        if not self.sems:
            self.stack.callback(self.clear)
        self.sems.append(self.nc.alloc_semaphore(self.own(name)))
        return self.sems[-1]

    def clear(self):
        self.nc.clear_and_free_semaphores(self.sems)
        self.nc.all_engine_barrier()

    def block(self):
        return self.stack.enter_context(self.nc.Block())


def chained(eng, sem):
    count = [0]

    def link(ins):
        count[0] += 1
        ins.then_inc(sem, 1)
        eng.wait_ge(sem, count[0])

    return link


def row(ap):
    return ap.unsqueeze(0)


def spread(ap, parts, n):
    return ap.unsqueeze(0).to_broadcast([parts, n])


class Bag:
    pass


def constants(nc, K):
    with ExitStack() as stack:
        c = Ctx(nc, stack)
        s_fill, s_made, s_conv = c.sem("const_filled"), c.sem("const_made"), c.sem("const_converted")
        iota_i = c.sb("iota_i", [P, WIN], I32)
        part_i = c.sb("part_i", [P, 1], I32)
        tile_i = c.sb("tile_i", [P, NT], I32)
        block = c.block()

        @block.gpsimd
        def _(pool):
            nc.gpsimd.memset(K.ident[:, :], 1.0).then_inc(s_fill, 1)
            nc.gpsimd.memset(K.ones[:, :], 1.0).then_inc(s_fill, 1)
            nc.gpsimd.memset(K.before[:, :], 1.0).then_inc(s_fill, 1)
            nc.gpsimd.memset(K.zero_i[:, :], 0).then_inc(s_fill, 1)
            pool.wait_ge(s_fill, 4)
            nc.gpsimd.affine_select(out=K.ident[:, :], in_=K.ident[:, :], compare_op=ALU.is_equal, fill=0.0,
                                    base=0, pattern=[[-1, P]], channel_multiplier=1).then_inc(s_made, 1)
            nc.gpsimd.affine_select(out=K.before[:, :], in_=K.before[:, :], compare_op=ALU.is_gt, fill=0.0,
                                    base=0, pattern=[[1, P]], channel_multiplier=-1).then_inc(s_made, 1)
            nc.gpsimd.iota(iota_i[:, :], pattern=[[1, WIN]], base=0, channel_multiplier=0).then_inc(s_made, 1)
            nc.gpsimd.iota(part_i[:, :], pattern=[[1, 1]], base=0, channel_multiplier=1).then_inc(s_made, 1)
            nc.gpsimd.iota(tile_i[:, :], pattern=[[1, NT]], base=0, channel_multiplier=0).then_inc(s_made, 1)

        @block.vector
        def _(dve):
            dve.wait_ge(s_made, 5)
            nc.vector.tensor_copy(K.iota[:, :], iota_i[:, :]).then_inc(s_conv, 1)
            nc.vector.tensor_copy(K.part[:, :], part_i[:, :]).then_inc(s_conv, 1)
            nc.vector.tensor_copy(K.tile_no[:, :], tile_i[:, :]).then_inc(K.ready, 1)


def layernorm(nc, K, X, Y, tag):
    with ExitStack() as stack:
        c = Ctx(nc, stack)
        stats = c.sb("ln_stats_" + tag, [NW, WIN, 6])
        mv = c.sb("ln_mv_" + tag, [NW, WIN, 2])
        std = c.sb("ln_std_" + tag, [NW, WIN])
        s_stats, s_mv, s_var = c.sem("ln_stats_" + tag), c.sem("ln_mv_" + tag), c.sem("ln_var_" + tag)
        s_std, s_rstd, s_out = c.sem("ln_std_" + tag), c.sem("ln_rstd_" + tag), c.sem("ln_out_" + tag)
        block = c.block()

        @block.vector
        def _(dve):
            with dve.Fori(0, WIN) as i:
                nc.vector.bn_stats(stats[:, bass.ds(i, 1), :].rearrange("p a s -> p (a s)"),
                                   X[:, bass.ds(i, 1), :].rearrange("p a d -> p (a d)")).then_inc(s_stats, 1)
            dve.wait_ge(s_stats, WIN)
            for i in range(WIN):
                nc.vector.bn_aggr(mv[:, i, :], stats[:, i, :]).then_inc(s_mv, 1)
            dve.wait_ge(s_mv, WIN)
            nc.vector.tensor_scalar(mv[:, :, 1], mv[:, :, 1], EPS, None, ALU.add).then_inc(s_var, 1)
            dve.wait_ge(s_std, 1)
            nc.vector.reciprocal(mv[:, :, 1], std[:, :]).then_inc(s_rstd, 1)
            dve.wait_ge(s_rstd, 1)
            for i in range(WIN):
                nc.vector.tensor_scalar(Y[:, i, :], X[:, i, :], mv[:, i, 0:1], mv[:, i, 1:2],
                                        ALU.subtract, ALU.mult).then_inc(s_out, 1)

        @block.scalar
        def _(act):
            act.wait_ge(s_var, 1)
            nc.scalar.activation(std[:, :], mv[:, :, 1], ACT.Sqrt).then_inc(s_std, 1)


def transpose_nodes(nc, K, Y, YT, tag):
    with ExitStack() as stack:
        c = Ctx(nc, stack)
        pt = [c.ps(f"tn_ps{b}_" + tag, [P, 2, P]) for b in range(2)]
        s_t, s_free = c.sem("tn_transposed_" + tag), c.sem("tn_bank_free_" + tag)
        block = c.block()

        @block.tensor
        def _(pe):
            for i in range(WIN):
                pe.wait_ge(s_free, i + 1)
                for k in range(KC):
                    last = nc.tensor.transpose(pt[i % 2][:, k, 0:NW], Y[:, i, k * P:(k + 1) * P], K.ident[0:NW, 0:NW])
                last.then_inc(s_t, 1)

        @block.scalar
        def _(act):
            act.sem_inc(s_free, 2)
            with act.Fori(0, WIN // 2) as j:
                for b in range(2):
                    act.wait_ge(s_t, j * 2 + b + 1)
                    nc.scalar.activation(YT[:, :, bass.ds(j * 2 + b, 1), :].rearrange("p k a w -> p k (a w)"),
                                         pt[b][:, :, 0:NW], ACT.Copy).then_inc(s_free, 1)


def relation_features(nc, K, T, YT):
    with ExitStack() as stack:
        c = Ctx(nc, stack)
        NQ = FROW // 512
        W = c.sb("rf_w", [P, KC, FROW])
        prod = c.sb("rf_prod", [P, FROW])
        attn = [c.sb(f"rf_attn{a}", [P, FROW]) for a in range(2)]
        WA = c.sb("rf_wa", [P, KC, 2, NREL * NH])
        stage = c.sb("rf_stage", [NW, 2, FROW])
        logits = c.sb("rf_logits", [NW, 2, WIN, NREL * NH])
        bank = [c.ps(f"rf_ps{q}", [P, 512]) for q in range(NQ)]
        bank_l = [c.ps(f"rf_psl{b}", [P, 2, NREL * NH]) for b in range(2)]
        s_w, s_wa, s_prod = c.sem("rf_weights"), c.sem("rf_wa_parts"), c.sem("rf_product")
        full = [c.sem(f"rf_full{q}") for q in range(NQ)]
        copied = [c.sem(f"rf_copied{q}") for q in range(NQ)]
        full_l = [c.sem(f"rf_full_l{b}") for b in range(2)]
        copied_l = [c.sem(f"rf_copied_l{b}") for b in range(2)]
        stored = [c.sem(f"rf_stored{b}") for b in range(2)]
        s_lst = c.sem("rf_logits_stored")
        block = c.block()

        @block.sync
        def _(sp):
            for a, name in enumerate(("L0_gnn_attn_l", "L0_gnn_attn_r")):
                sp.dma_start(attn[a][:, :], spread(T[name].rearrange("r h d -> (r h d)"), P, FROW)).then_inc(stored[a], 16)
            for r in range(NREL):
                for h in range(NH):
                    q = r * NH + h
                    sp.dma_start(W[:, :, q * HD:(q + 1) * HD],
                                 T["L0_gnn_conv_weights"][r, h].rearrange("(k p) d -> p k d", p=P)).then_inc(s_w, 16)
            table = T["feat"].rearrange("(w i r) d -> w i (r d)", i=WIN, r=NREL)
            with sp.Fori(0, WIN // 2) as j:
                for b in range(2):
                    for q in range(NQ):
                        sp.wait_ge(copied[q], j * 2 + b + 2)
                    sp.dma_start(table[:, bass.ds(j * 2 + b, 1), :], stage[:, b:b + 1, :]).then_inc(stored[b], 16)
            for b in range(2):
                sp.wait_ge(copied_l[b], WIN // 2 + 1)
            for a in range(2):
                sp.dma_start(T[f"logit{a}"].rearrange("(w q) h -> w (q h)", w=NW),
                             logits[:, a, :, :].rearrange("p i q -> p (i q)")).then_inc(s_lst, 16)
            sp.wait_ge(s_lst, 32)
            for b in range(2):
                sp.wait_ge(stored[b], 16 + 16 * (WIN // 2))

        def copy_rows(eng, op, q, j, b):
            eng.wait_ge(full[q], j * 2 + b + 1)
            eng.wait_ge(stored[b], j * 16 + 16)
            op(stage[:, b, q * 512:(q + 1) * 512], bank[q][0:NW, :]).then_inc(copied[q], 1)

        @block.vector
        def _(dve):
            dve.wait_ge(s_w, 16 * NREL * NH)
            for a in range(2):
                dve.wait_ge(stored[a], 16)
            n = 0
            for k in range(KC):
                for a in range(2):
                    if n:
                        dve.wait_ge(s_wa, n)
                    n += 1
                    nc.vector.tensor_tensor(prod[:, :], W[:, k, :], attn[a][:, :], ALU.mult).then_inc(s_prod, 1)
                    dve.wait_ge(s_prod, n)
                    nc.vector.tensor_reduce(WA[:, k, a, :], prod[:, :].rearrange("p (q d) -> p q d", d=HD),
                                            AX, ALU.add).then_inc(s_wa, 1)
            dve.sem_inc(copied[0], 1)
            dve.sem_inc(copied[1], 1)
            for b in range(2):
                dve.sem_inc(copied_l[b], 1)
            with dve.Fori(0, WIN // 2) as j:
                for b in range(2):
                    for q in (0, 1):
                        copy_rows(dve, nc.vector.tensor_copy, q, j, b)
                    dve.wait_ge(full_l[b], j + 1)
                    nc.vector.tensor_copy(logits[:, :, bass.ds(j * 2 + b, 1), :].rearrange("p a i q -> p a (i q)"),
                                          bank_l[b][0:NW, :, :]).then_inc(copied_l[b], 1)

        @block.scalar
        def _(act):
            act.sem_inc(copied[2], 1)
            act.sem_inc(copied[3], 1)
            with act.Fori(0, WIN // 2) as j:
                for b in range(2):
                    for q in (2, 3):
                        copy_rows(act, nc.scalar.copy, q, j, b)

        @block.tensor
        def _(pe):
            pe.wait_ge(s_w, 16 * NREL * NH)
            pe.wait_ge(s_wa, 2 * KC)
            for i in range(WIN):
                for q in range(NQ):
                    pe.wait_ge(copied[q], i + 1)
                    for k in range(KC):
                        last = nc.tensor.matmul(bank[q][0:NW, :], YT[:, k, i, :], W[:, k, q * 512:(q + 1) * 512],
                                                start=k == 0, stop=k == KC - 1)
                    last.then_inc(full[q], 1)
                pe.wait_ge(copied_l[i % 2], i // 2 + 1)
                for k in range(KC):
                    last = nc.tensor.matmul(bank_l[i % 2][0:NW, :, :].rearrange("p a q -> p (a q)"), YT[:, k, i, :],
                                            WA[:, k, :, :].rearrange("p a q -> p (a q)"), start=k == 0, stop=k == KC - 1)
                last.then_inc(full_l[i % 2], 1)


def sort_edges(nc, K, T, key, fields, slots, bucket, tag, R):
    nf = len(fields)
    names = sorted({n for terms in fields for n, _ in terms} | {key})
    with ExitStack() as stack:
        c = Ctx(nc, stack)
        raw = {n: c.sb(f"so_raw_{n}_" + tag, [SK, SB, SLICE], I32) for n in names}
        val = {n: c.sb(f"so_val_{n}_" + tag, [SK, SB, SLICE]) for n in names}
        bk = c.sb("so_bucket_" + tag, [SK, SB, SLICE])
        bkh = c.sb("so_bucket_bf_" + tag, [SK, SB, SLICE], BF16)
        F = [c.sb(f"so_field{f}_" + tag, [SK, SB, SLICE]) for f in range(nf + 1)]
        pay = c.sb("so_pay_" + tag, [SLICE, NSL, 4])
        empty = c.sb("so_empty_" + tag, [P, NT, 4])
        keys = [c.sb(f"so_keys{b}_" + tag, [NW, CH * SLICE], BF16) for b in range(2)]
        hot = [c.sb(f"so_hot{b}_" + tag, [NW, CH * SLICE], BF16) for b in range(2)]
        scan = [c.sb(f"so_scan{b}_" + tag, [NW, CH * SLICE]) for b in range(2)]
        hit = [c.sb(f"so_hit{b}_" + tag, [NW, CH * SLICE]) for b in range(2)]
        count = c.sb("so_count_" + tag, [NW, NCH])
        total = c.sb("so_total_" + tag, [NW, 1])
        tiles = c.sb("so_tiles_" + tag, [NW, 1])
        first = c.sb("so_first_" + tag, [NW, 1])
        carry = c.sb("so_carry_" + tag, [NW, 1])
        reach = c.sb("so_reach_" + tag, [NW, NT])
        place = c.sb("so_place_" + tag, [SLICE, NSL])
        tile = c.sb("so_tile_" + tag, [SLICE, NSL])
        addr = c.sb("so_addr_" + tag, [SLICE, NSL])
        addr_i = c.sb("so_addr_i_" + tag, [SLICE, NSL], I32)
        NS = 10
        idx_s = c.sb("so_idx_stage_" + tag, [SLICE, 2, NS], I32)
        pay_s = c.sb("so_pay_stage_" + tag, [SLICE, 2, NS, 4])
        got = c.sb("so_slots_" + tag, [P, NT, 4])
        pt = [c.ps(f"so_pt{q}_" + tag, [P, 512]) for q in range(2)]
        ppos = c.ps("so_ppos_" + tag, [P, 512])
        pw = [c.ps(f"so_pw{q}_" + tag, [P, 512]) for q in range(2)]
        pf = c.ps("so_pf_" + tag, [P, 8])
        sem = lambda n: c.sem("so_" + n + "_" + tag)
        s_ld, s_ch, s_bk, s_bks, s_tr, s_pay = sem("loaded"), sem("chain"), sem("bucket"), sem("bucket_stored"), sem("transposed"), sem("pay")
        s_kin = [sem(f"keys_in{b}") for b in range(2)]
        s_kfree = [sem(f"keys_free{b}") for b in range(2)]
        s_cnt, s_first, s_tiles, s_reach, s_wb = sem("counted"), sem("first"), sem("tiles"), sem("reach"), sem("window_of_tile")
        s_hot, s_scan, s_hit, s_hfree = sem("hot"), sem("scanned"), sem("hit"), sem("hit_free")
        s_pos, s_addr, s_empty, s_estored = sem("positions"), sem("addr"), sem("empty"), sem("empty_stored")
        s_stage = [sem(f"staged{b}") for b in range(2)]
        s_sc = [sem(f"scattered{b}") for b in range(2)]
        s_got, s_end, s_win, s_done = sem("slots_loaded"), sem("end"), sem("win"), sem("done")
        s_ch2, s_ch3 = sem("chain2"), sem("chain3")
        s_sfree = [sem(f"stage_free{b}") for b in range(2)]
        s_i = [sem(f"idx_staged{b}") for b in range(2)]

        with nc.Block() as block:
            @block.sync
            def _(sp):
                for n in names:
                    sp.dma_start(raw[n][:, :, :], T[n].rearrange("(b k p) -> k b p", b=SB, p=SLICE)).then_inc(s_ld, 16)
                sp.wait_ge(s_bk, 1)
                sp.dma_start(T[bucket].rearrange("(b k p) -> k b p", b=SB, p=SLICE), bkh[:, :, :]).then_inc(s_bks, 16)
                sp.wait_ge(s_empty, 2)
                sp.dma_start(T[slots].rearrange("(s j) q -> s (j q)", s=P),
                             empty[:, :, :].rearrange("p j q -> p (j q)")).then_inc(s_estored, 16)
                sp.wait_ge(s_bks, 16)
                sp.wait_ge(s_estored, 16)

            @block.gpsimd
            def _(pool):
                nc.gpsimd.memset(empty[:, :, :], 0.0).then_inc(s_empty, 1)
                pool.wait_ge(s_empty, 1)
                nc.gpsimd.memset(empty[:, :, 2:3], -1.0).then_inc(s_empty, 1)

            @block.vector
            def _(dve):
                link = chained(dve, s_ch)
                dve.wait_ge(s_ld, 16 * len(names))
                for n in names:
                    link(nc.vector.tensor_copy(val[n][:, :, :], raw[n][:, :, :]))
                link(nc.vector.tensor_scalar(bk[:, :, :], val[key][:, :, :], -(WIN - 1) / 2, 1.0 / WIN, ALU.add, ALU.mult))
                link(nc.vector.tensor_scalar(bk[:, :, :], bk[:, :, :], ROUND, None, ALU.add))
                link(nc.vector.tensor_scalar(bk[:, :, :], bk[:, :, :], -ROUND, None, ALU.add))
                nc.vector.tensor_copy(bkh[:, :, :], bk[:, :, :]).then_inc(s_bk, 1)
                for f, terms in enumerate(fields):
                    n0, m0 = terms[0]
                    link(nc.vector.tensor_scalar(F[f][:, :, :], val[n0][:, :, :], float(m0), None, ALU.mult))
                    for n1, m1 in terms[1:]:
                        link(nc.vector.scalar_tensor_tensor(F[f][:, :, :], val[n1][:, :, :], float(m1), F[f][:, :, :],
                                                            ALU.mult, ALU.add))
                link(nc.vector.scalar_tensor_tensor(F[nf][:, :, :], bk[:, :, :], -float(WIN), val[key][:, :, :],
                                                    ALU.mult, ALU.add))
                nc.vector.memset(pay[:, :, 3:4], 0.0).then_inc(s_pay, 1)
                for f in range(nf + 1):
                    dve.wait_ge(s_tr, f + 1)
                    nc.vector.tensor_copy(pay[:, :, f:f + 1].rearrange("p s a -> p (s a)"),
                                          pt[f % 2][0:SLICE, 0:NSL]).then_inc(s_pay, 1)

            @block.tensor
            def _(pe):
                pe.wait_ge(s_ch, len(names) + 3 + sum(len(t) for t in fields) + 1)
                for f in range(nf + 1):
                    if f >= 2:
                        pe.wait_ge(s_pay, f)
                    for b in range(SB):
                        last = nc.tensor.transpose(pt[f % 2][0:SLICE, b * SK:(b + 1) * SK], F[f][:, b, :],
                                                   K.ident[0:SK, 0:SK])
                    last.then_inc(s_tr, 1)

        keys_of = lambda ch: T[bucket][bass.ds(ch * CH * SLICE, CH * SLICE)].unsqueeze(0).to_broadcast([NW, CH * SLICE])
        with nc.Block() as block:
            @block.sync
            def _(sp):
                for ch in range(NCH):
                    b = ch % 2
                    if ch >= 2:
                        sp.wait_ge(s_cnt, ch - 1)
                    sp.dma_start(keys[b][:, :], keys_of(ch)).then_inc(s_kin[b], 16)

            @block.vector
            def _(dve):
                for ch in range(NCH):
                    b = ch % 2
                    dve.wait_ge(s_kin[b], 16 * (ch // 2 + 1))
                    if ch >= 2:
                        dve.wait_ge(s_cnt, ch - 1)
                    nc.vector.tensor_scalar(hot[b][:, :], keys[b][:, :], K.part[0:NW, :], 0.0, ALU.is_equal, ALU.add,
                                            accum_out=count[:, ch:ch + 1]).then_inc(s_cnt, 1)
                dve.wait_ge(s_cnt, NCH)
                link = chained(dve, s_ch2)
                link(nc.vector.tensor_reduce(total[:, :], count[:, :], AX, ALU.add))
                link(nc.vector.tensor_scalar(tiles[:, :], total[:, :], 63.25, 1.0 / P, ALU.add, ALU.mult))
                link(nc.vector.tensor_scalar(tiles[:, :], tiles[:, :], ROUND, None, ALU.add))
                link(nc.vector.tensor_scalar(tiles[:, :], tiles[:, :], -ROUND, None, ALU.add))
                dve.wait_ge(s_first, 1)
                link(nc.vector.tensor_copy(first[:, :], pf[0:NW, 0:1]))
                link(nc.vector.tensor_scalar(carry[:, :], first[:, :], float(P), None, ALU.mult))
                link(nc.vector.tensor_scalar(reach[:, :], K.tile_no[0:NW, :], first[:, :], None, ALU.is_ge))
                for q in range(2):
                    dve.wait_ge(s_wb, q + 1)
                    nc.vector.tensor_scalar(R.window[:, q * (NT // 2):(q + 1) * (NT // 2)], pw[q][:, 0:NT // 2], -1.0, None,
                                            ALU.add).then_inc(s_win, 1)
                dve.wait_ge(s_win, 2)
                nc.vector.tensor_copy(R.window_i[:, :], R.window[0:1, :]).then_inc(s_win, 1)

            @block.tensor
            def _(pe):
                pe.wait_ge(s_ch2, 4)
                nc.tensor.matmul(pf[0:NW, 0:1], K.before[0:NW, 0:NW], tiles[:, :], start=True, stop=True).then_inc(s_first, 1)
                pe.wait_ge(s_ch2, 7)
                for q in range(2):
                    nc.tensor.matmul(pw[q][:, 0:NT // 2], K.ones[0:NW, :], reach[:, q * (NT // 2):(q + 1) * (NT // 2)],
                                     start=True, stop=True).then_inc(s_wb, 1)

        with nc.Block() as block:
            @block.sync
            def _(sp):
                for ch in range(NCH):
                    b = ch % 2
                    if ch >= 2:
                        sp.wait_ge(s_hot, ch - 1)
                    sp.dma_start(keys[b][:, :], keys_of(ch)).then_inc(s_kin[b], 16)

            @block.vector
            def _(dve):
                for ch in range(NCH):
                    b = ch % 2
                    dve.wait_ge(s_kin[b], 16 * ((NCH + 1 - b) // 2 + ch // 2 + 1))
                    if ch >= 2:
                        dve.wait_ge(s_hit, ch - 1)
                    nc.vector.tensor_scalar(hot[b][:, :], keys[b][:, :], K.part[0:NW, :], None, ALU.is_equal).then_inc(s_hot, 1)
                    dve.wait_ge(s_hot, ch + 1)
                    if ch:
                        dve.wait_ge(s_scan, ch)
                    nc.vector.tensor_tensor_scan(scan[b][:, :], hot[b][:, :], hot[b][:, :],
                                                 scan[1 - b][:, CH * SLICE - 1:CH * SLICE] if ch else carry[:, :],
                                                 ALU.add, ALU.max).then_inc(s_scan, 1)
                    dve.wait_ge(s_scan, ch + 1)
                    if ch >= 2:
                        dve.wait_ge(s_hfree, ch - 1)
                    nc.vector.tensor_tensor(hit[b][:, :], scan[b][:, :], hot[b][:, :], ALU.mult).then_inc(s_hit, 1)
                link = chained(dve, s_ch3)
                dve.wait_ge(s_hfree, NCH)
                link(nc.vector.tensor_scalar(place[:, :], ppos[0:SLICE, 0:NSL], -1.0, None, ALU.add))
                link(nc.vector.tensor_scalar(tile[:, :], place[:, :], -(P - 1) / 2, 1.0 / P, ALU.add, ALU.mult))
                link(nc.vector.tensor_scalar(tile[:, :], tile[:, :], ROUND, None, ALU.add))
                link(nc.vector.tensor_scalar(tile[:, :], tile[:, :], -ROUND, None, ALU.add))
                link(nc.vector.scalar_tensor_tensor(addr[:, :], tile[:, :], -float(P), place[:, :], ALU.mult, ALU.add))
                link(nc.vector.scalar_tensor_tensor(addr[:, :], addr[:, :], float(NT), tile[:, :], ALU.mult, ALU.add))
                link(nc.vector.tensor_copy(addr_i[:, :], addr[:, :]))

            @block.tensor
            def _(pe):
                for ch in range(NCH):
                    pe.wait_ge(s_hit, ch + 1)
                    for q in range(CH):
                        last = nc.tensor.matmul(ppos[0:SLICE, ch * CH + q:ch * CH + q + 1],
                                                hit[ch % 2][:, q * SLICE:(q + 1) * SLICE], K.ones[0:NW, 0:1], start=True, stop=True)
                    last.then_inc(s_hfree, 1)

        with nc.Block() as block:
            @block.gpsimd
            def _(pool):
                bound = nc.gpsimd.to_reg(P * NT - 1)
                with pool.Fori(1, NSL // (2 * NS) + 1) as i:
                    for b in range(2):
                        pool.wait_ge(K.ready, 1)
                        pool.wait_ge(s_stage[b], i)
                        for q in range(NS):
                            nc.gpsimd.indirect_dma_start(
                                out=T[slots][:, :], out_offset=bass.IndirectOffsetOnAxis(ap=idx_s[:, b, q:q + 1].bitcast(U32), axis=0),
                                in_=pay_s[:, b, q, :], in_offset=None, bounds_check=bound, oob_is_err=False).then_inc(s_sc[b], 16)

            @block.vector
            def _(dve):
                with dve.Fori(0, NSL // (2 * NS)) as i:
                    for b in range(2):
                        dve.wait_ge(s_sfree[b], i + 1)
                        nc.vector.tensor_copy(idx_s[:, b, :], addr_i[:, bass.ds((i * 2 + b) * NS, NS)]).then_inc(s_i[b], 1)
                        dve.wait_ge(s_i[b], i + 1)
                        nc.vector.tensor_copy(pay_s[:, b, :, :], pay[:, bass.ds((i * 2 + b) * NS, NS), :]).then_inc(s_stage[b], 1)

            @block.sync
            def _(sp):
                for b in range(2):
                    sp.sem_inc(s_sfree[b], 1)
                with sp.Fori(0, NSL // (2 * NS)) as i:
                    for b in range(2):
                        sp.wait_ge(s_sc[b], i * (16 * NS) + 16 * NS)
                        sp.sem_inc(s_sfree[b], 1)
                sp.dma_start(got[:, :, :].rearrange("p j q -> p (j q)"), T[slots].rearrange("(s j) q -> s (j q)", s=P)).then_inc(s_got, 16)

            @block.scalar
            def _(act):
                act.wait_ge(s_got, 16)
                for f in range(nf):
                    nc.scalar.copy(R.index[f][:, :], got[:, :, f]).then_inc(s_done, 1)
                nc.scalar.copy(R.node[:, :], got[:, :, nf]).then_inc(s_done, 1)


def edge_logits(nc, K, T, R):
    with ExitStack() as stack:
        c = Ctx(nc, stack)
        idx_s = [[c.sb(f"el_idx{b}{a}", [P, GROUP], I32) for a in range(2)] for b in range(2)]
        part = [[c.sb(f"el_part{b}{a}", [P, GROUP, NH]) for a in range(2)] for b in range(2)]
        miss = [c.sb(f"el_miss{b}", [P, GROUP, WIN]) for b in range(2)]
        Xm = [c.sb(f"el_x{b}", [P, GROUP, NH, WIN]) for b in range(2)]
        tmax = c.sb("el_tmax", [HW, NT])
        reset = [c.sb(f"el_reset{d}", [HW, NT]) for d in range(2)]
        run = c.sb("el_run", [HW, NT])
        bank = [c.ps(f"el_ps{b}", [HW, GROUP, P]) for b in range(2)]
        staged = [[c.sem(f"el_staged{b}{a}") for a in range(2)] for b in range(2)]
        arrived = [c.sem(f"el_arrived{b}") for b in range(2)]
        free = [c.sem(f"el_free{b}") for b in range(2)]
        s_leaky = c.sem("el_leaky")
        s_m1 = [c.sem(f"el_m1{b}") for b in range(2)]
        s_m2 = [c.sem(f"el_m2{b}") for b in range(2)]
        s_x = [c.sem(f"el_xs{b}") for b in range(2)]
        s_t = [c.sem(f"el_t{b}") for b in range(2)]
        s_red = [c.sem(f"el_red{b}") for b in range(2)]
        s_ch = c.sem("el_chain")
        with nc.Block() as block:
            @block.gpsimd
            def _(pool):
                bound = nc.gpsimd.to_reg(N_NODES * NREL - 1)
                with pool.Fori(1, NG // 2 + 1) as i:
                    for b in range(2):
                        pool.wait_ge(free[b], i)
                        for a in range(2):
                            nc.gpsimd.tensor_tensor(idx_s[b][a][:, :], R.index[a][:, bass.ds(i * (2 * GROUP) + (b - 2) * GROUP, GROUP)],
                                                    K.zero_i[:, :], ALU.add).then_inc(staged[b][a], 1)
                        pool.wait_ge(K.ready, 1)
                        for a in range(2):
                            pool.wait_ge(staged[b][a], i)
                        for a in range(2):
                            for t in range(GROUP):
                                nc.gpsimd.indirect_dma_start(
                                    out=part[b][a][:, t, :], out_offset=None, in_=T[f"logit{a}"][:, :],
                                    in_offset=bass.IndirectOffsetOnAxis(ap=idx_s[b][a][:, t:t + 1].bitcast(U32), axis=0),
                                    bounds_check=bound, oob_is_err=False).then_inc(arrived[b], 16)

            @block.vector
            def _(dve):
                for b in range(2):
                    dve.sem_inc(free[b], 1)
                with dve.Fori(0, NG // 2) as i:
                    for b in range(2):
                        dve.wait_ge(arrived[b], i * (16 * 2 * GROUP) + 16 * 2 * GROUP)
                        nc.vector.tensor_tensor(R.ev[:, bass.ds(i * (2 * GROUP) + b * GROUP, GROUP), :], part[b][0][:, :, :],
                                                part[b][1][:, :, :], ALU.add).then_inc(free[b], 1)
                for b in range(2):
                    dve.wait_ge(free[b], NG // 2 + 1)
                ev = R.ev[:, :, :].rearrange("p j h -> p (j h)")
                nc.vector.scalar_tensor_tensor(ev, ev, 0.2, ev, ALU.mult, ALU.max).then_inc(s_leaky, 1)

        with nc.Block() as block:
            @block.vector
            def _(dve):
                dve.wait_ge(s_leaky, 1)
                for b in range(2):
                    dve.sem_inc(s_red[b], 1)
                with dve.Fori(0, NG // 2) as i:
                    for b in range(2):
                        masked_logits(nc, dve, K, R, i, b, miss, Xm, s_m1, s_m2, s_x)
                    for b in range(2):
                        dve.wait_ge(s_t[b], i + 1)
                        nc.vector.tensor_reduce(tmax[:, bass.ds(i * (2 * GROUP) + b * GROUP, GROUP)], bank[b][:, :, :],
                                                AX, ALU.max).then_inc(s_red[b], 1)
                for b in range(2):
                    dve.wait_ge(s_red[b], NG // 2 + 1)
                link = chained(dve, s_ch)
                link(nc.vector.memset(reset[0][:, :], 0.0))
                link(nc.vector.memset(reset[1][:, :], 0.0))
                link(nc.vector.tensor_tensor(reset[0][:, 1:NT], R.window[0:HW, 1:NT], R.window[0:HW, 0:NT - 1], ALU.not_equal))
                link(nc.vector.tensor_copy(reset[1][:, 0:NT - 1], reset[0][:, 1:NT]))
                for d in range(2):
                    link(nc.vector.tensor_scalar(reset[d][:, :], reset[d][:, :], NEG, None, ALU.mult))
                link(nc.vector.tensor_tensor_scan(run[:, :], reset[0][:, :], tmax[:, :], NEG, ALU.add, ALU.max))
                link(nc.vector.tensor_tensor_scan(tmax[:, ::-1], reset[1][:, ::-1], run[:, ::-1], NEG, ALU.add, ALU.max))
                link(nc.vector.tensor_scalar(R.negmax[:, :], tmax[:, :], FLOOR, -1.0, ALU.max, ALU.mult))

            @block.tensor
            def _(pe):
                with pe.Fori(0, NG // 2) as i:
                    for b in range(2):
                        pe.wait_ge(s_x[b], i + 1)
                        pe.wait_ge(s_red[b], i + 1)
                        for t in range(GROUP):
                            last = nc.tensor.transpose(bank[b][:, t, :], Xm[b][:, t, :, :].rearrange("p h n -> p (h n)"), K.ident[:, :])
                        last.then_inc(s_t[b], 1)


def masked_logits(nc, dve, K, R, i, b, miss, Xm, s_m1, s_m2, s_x, turned=None):
    j0 = i * (2 * GROUP) + b * GROUP
    nc.vector.tensor_tensor(miss[b][:, :, :], R.node[:, bass.ds(j0, GROUP)].unsqueeze(2).to_broadcast([P, GROUP, WIN]),
                            K.iota[:, :].unsqueeze(1).to_broadcast([P, GROUP, WIN]), ALU.not_equal).then_inc(s_m1[b], 1)
    dve.wait_ge(s_m1[b], i + 1)
    nc.vector.tensor_scalar(miss[b][:, :, :], miss[b][:, :, :], NEG, None, ALU.mult).then_inc(s_m2[b], 1)
    dve.wait_ge(s_m2[b], i + 1)
    if turned:
        dve.wait_ge(turned[b], i + 1)
    nc.vector.tensor_tensor(Xm[b][:, :, :, :], miss[b][:, :, :].unsqueeze(2).to_broadcast([P, GROUP, NH, WIN]),
                            R.ev[:, bass.ds(j0, GROUP), :].unsqueeze(3).to_broadcast([P, GROUP, NH, WIN]),
                            ALU.add).then_inc(s_x[b], 1)


def earlier(b, i, k, n=2):
    return (b - k) % n, i + (b - k) // n


def live(b, i, k, n=2):
    return not isinstance(i, int) or 0 <= n * i + b - k < NG


def pipeline(eng, step, n=2, ahead=0):
    def one_pass(i):
        for b in range(n):
            step(b, i)

    passes, peeled = NG // n, -(-3 // n)
    for i in range(peeled):
        one_pass(i)
    with eng.Fori(peeled, passes - ahead) as i:
        one_pass(i)
    for i in range(passes - ahead, passes + peeled):
        one_pass(i)


def relation_attention(nc, K, T, R, X):
    with ExitStack() as stack:
        c = Ctx(nc, stack)
        acc = c.sb("ra_acc", [HD, NW, 2 * HW])
        idx_s = [c.sb(f"ra_idx{b}", [P, GROUP], I32) for b in range(2)]
        feat = [c.sb(f"ra_feat{b}", [P, GROUP, D]) for b in range(2)]
        miss = [c.sb(f"ra_miss{b}", [P, GROUP, WIN]) for b in range(2)]
        Xm = [c.sb(f"ra_x{b}", [P, GROUP, NH, WIN]) for b in range(2)]
        prob = [c.sb(f"ra_prob{b}", [HW, GROUP, P]) for b in range(2)]
        A = [c.sb(f"ra_a{b}", [P, GROUP, HW]) for b in range(2)]
        bias = c.sb("ra_bias", [NW, D])
        sems = lambda n: [c.sem(f"ra_{n}{b}") for b in range(2)]
        staged, arrived = sems("staged"), [[c.sem(f"ra_arrived{b}{t}") for t in range(GROUP)] for b in range(2)]
        s_m1, s_m2, s_x, s_t = sems("m1"), sems("m2"), sems("x"), sems("t")
        s_exp = sems("exp")
        s_a, s_ac = sems("a"), sems("ac")
        s_gat = [[c.sem(f"ra_gat{b}{t}") for t in range(GROUP)] for b in range(2)]
        s_acc, s_bias, s_ch = c.sem("ra_acc"), c.sem("ra_bias"), c.sem("ra_ch")
        NP = NG // 2
        with ExitStack() as banks, nc.Block() as block:
            cb = Ctx(nc, banks)
            pt = [cb.ps(f"ra_pt{b}", [HW, GROUP, P]) for b in range(2)]
            pa = [cb.ps(f"ra_pa{b}", [P, 512]) for b in range(2)]
            pg = [[cb.ps(f"ra_pg{b}{q}", [HD, 2, 2 * HW]) for q in range(2)] for b in range(2)]

            @block.sync
            def _(sp):
                sp.dma_start(bias[:, :], spread(T["L0_gnn_h_bias"], NW, D)).then_inc(s_bias, 16)
                sp.wait_ge(s_bias, 16)

            @block.gpsimd
            def _(pool):
                bound = nc.gpsimd.to_reg(N_NODES * NREL - 1)
                with pool.Fori(1, NP + 1) as i:
                    for b in range(2):
                        pool.wait_ge(s_gat[b][GROUP - 1], i)
                        nc.gpsimd.tensor_tensor(idx_s[b][:, :], R.index[0][:, bass.ds(i * (2 * GROUP) + (b - 2) * GROUP, GROUP)],
                                                K.zero_i[:, :], ALU.add).then_inc(staged[b], 1)
                        for t in range(GROUP):
                            pool.wait_ge(K.ready, 1)
                            if t == 0:
                                pool.wait_ge(staged[b], i)
                            nc.gpsimd.indirect_dma_start(
                                out=feat[b][:, t, :], out_offset=None, in_=T["feat"][:, :],
                                in_offset=bass.IndirectOffsetOnAxis(ap=idx_s[b][:, t:t + 1].bitcast(U32), axis=0),
                                bounds_check=bound, oob_is_err=False).then_inc(arrived[b][t], 16)

            @block.tensor
            def _(pe):
                def turn(b, i):
                    pe.wait_ge(s_x[b], i + 1)
                    pe.wait_ge(s_exp[b], i + 1)
                    for t in range(GROUP):
                        last = nc.tensor.transpose(pt[b][:, t, :], Xm[b][:, t, :, :].rearrange("p h n -> p (h n)"), K.ident[:, :])
                    last.then_inc(s_t[b], 1)

                def back(b, i):
                    pe.wait_ge(s_exp[b], i + 2)
                    pe.wait_ge(s_ac[b], i + 1)
                    for t in range(GROUP):
                        last = nc.tensor.matmul(pa[b][:, t * HW:(t + 1) * HW], prob[b][:, t, :], K.ident[0:HW, 0:HW],
                                                start=True, stop=True)
                    last.then_inc(s_a[b], 1)

                def gather(b, i):
                    pe.wait_ge(s_ac[b], i + 2)
                    pe.wait_ge(s_acc, i * (2 * GROUP) + b * GROUP + 1)
                    for t in range(GROUP):
                        pe.wait_ge(arrived[b][t], i * 16 + 16)
                        o = pg[b][t // 2][:, t % 2, :]
                        for h in range(NH):
                            nc.tensor.matmul(o[:, h * WIN:(h + 1) * WIN], feat[b][:, t, h * HD:(h + 1) * HD],
                                             A[b][:, t, h * WIN:(h + 1) * WIN], start=True, stop=True)
                        nc.tensor.matmul(o[:, HW:2 * HW], K.ones[:, 0:HD], A[b][:, t, :], start=True, stop=True).then_inc(s_gat[b][t], 1)

                def step(b, i):
                    if live(b, i, 0):
                        turn(b, i)
                    if live(b, i, 1):
                        back(*earlier(b, i, 1))
                    if live(b, i, 2):
                        gather(*earlier(b, i, 2))

                for b in range(2):
                    pe.sem_inc(s_t[b], 1)
                    for t in range(GROUP):
                        pe.sem_inc(s_gat[b][t], 1)
                pipeline(pe, step)

            @block.scalar
            def _(act):
                for b in range(2):
                    act.sem_inc(s_exp[b], 1)
                    act.sem_inc(s_ac[b], 1)

                def exps(b, i):
                    act.wait_ge(s_t[b], i + 2)
                    for t in range(GROUP):
                        last = nc.scalar.activation(prob[b][:, t, :], pt[b][:, t, :], ACT.Exp,
                                                    bias=R.negmax[:, bass.ds(i * (2 * GROUP) + b * GROUP + t, 1)])
                    last.then_inc(s_exp[b], 1)

                def copy_a(b, i):
                    act.wait_ge(s_a[b], i + 1)
                    act.wait_ge(s_gat[b][GROUP - 1], i + 1)
                    nc.scalar.copy(A[b][:, :, :].rearrange("p t q -> p (t q)"), pa[b][:, 0:GROUP * HW]).then_inc(s_ac[b], 1)

                def step(b, i):
                    if live(b, i, 1):
                        copy_a(*earlier(b, i, 1))
                    if live(b, i, 0):
                        exps(b, i)

                pipeline(act, step)

            @block.vector
            def _(dve):
                nc.vector.memset(acc[:, :, :], 0.0).then_inc(s_acc, 1)
                dve.sem_inc(s_acc, GROUP)

                def windows(b, i):
                    return [dve.value_load(R.window_i[0:1, bass.ds(i * (2 * GROUP) + b * GROUP + t, 1)], min_val=0, max_val=NW - 1)
                            for t in range(GROUP)]

                def add(b, i, t, w):
                    dve.wait_ge(s_gat[b][t | 1], i + 2)
                    n = i * (2 * GROUP) + b * GROUP + t
                    dve.wait_ge(s_acc, n + GROUP + 1)
                    a = acc[:, bass.ds(w, 1), :]
                    nc.vector.tensor_tensor(a, a, pg[b][t // 2][:, t % 2:t % 2 + 1, :], ALU.add).then_inc(s_acc, 1)

                def mask(b, i):
                    masked_logits(nc, dve, K, R, i, b, miss, Xm, s_m1, s_m2, s_x, turned=s_t)

                def step(b, i):
                    if live(b, i, -1):
                        mask(*earlier(b, i, -1))
                    if live(b, i, 3):
                        w = windows(*earlier(b, i, 3))
                        for t in range(GROUP):
                            add(*earlier(b, i, 3), t, w[t])

                mask(0, 0)
                pipeline(dve, step, ahead=1)
                dve.wait_ge(s_acc, NT + GROUP + 1)
                link = chained(dve, s_ch)
                link(nc.vector.tensor_scalar(acc[:, :, HW:2 * HW], acc[:, :, HW:2 * HW], 1e-30, None, ALU.max))
                link(nc.vector.reciprocal(acc[:, :, HW:2 * HW], acc[:, :, HW:2 * HW]))
                link(nc.vector.tensor_tensor(acc[:, :, 0:HW], acc[:, :, 0:HW], acc[:, :, HW:2 * HW], ALU.mult))

        with ExitStack() as banks, nc.Block() as block:
            cb = Ctx(nc, banks)
            pb = [cb.ps(f"ra_pb{b}", [NW, D]) for b in range(2)]
            s_tb, s_add, s_b = cb.sem("ra_tb"), cb.sem("ra_add"), cb.sem("ra_b")

            @block.tensor
            def _(pe):
                for i in range(WIN):
                    if i >= 2:
                        pe.wait_ge(s_add, i - 1)
                    for h in range(NH):
                        last = nc.tensor.transpose(pb[i % 2][:, h * HD:(h + 1) * HD], acc[:, :, h * WIN + i], K.ident[0:HD, 0:HD])
                    last.then_inc(s_tb, 1)

            @block.vector
            def _(dve):
                nc.vector.tensor_tensor(X[:, :, :], X[:, :, :], bias[:, :].unsqueeze(1).to_broadcast([NW, WIN, D]),
                                        ALU.add).then_inc(s_b, 1)
                dve.wait_ge(s_b, 1)
                for i in range(WIN):
                    dve.wait_ge(s_tb, i + 1)
                    nc.vector.tensor_tensor(X[:, i, :], X[:, i, :], pb[i % 2][:, :], ALU.add).then_inc(s_add, 1)


N_SEL = N_NODES // 2 - 1
HID = 1024
NCK = 3
NCHK = WIN // NCK


def token_weights(nc, K, T, Y, R):
    with ExitStack() as stack:
        c = Ctx(nc, stack)
        wr = c.sb("tw_wr", [NW, D])
        br = c.sb("tw_br", [NW, 1])
        prod = c.sb("tw_prod", [NW, WIN, D])
        w = c.sb("tw_w", [NW, WIN])
        every = c.sb("tw_every", [NW, N_NODES])
        larger = c.sb("tw_larger", [NW, 2, N_NODES], BF16)
        above = c.sb("tw_above", [NW, WIN])
        inside = c.sb("tw_inside", [NW, WIN])
        cand = c.sb("tw_cand", [NW, WIN])
        peak = c.sb("tw_peak", [NW, 1])
        peakT = c.sb("tw_peakT", [1, P])
        top = c.sb("tw_top", [1, 1])
        edge = c.sb("tw_edge", [NW, 1])
        tie = c.sb("tw_tie", [NW, WIN])
        order = c.sb("tw_order", [NW, WIN])
        ties = c.sb("tw_ties", [NW, 1])
        before = c.sb("tw_before", [NW, 1])
        room = c.sb("tw_room", [NW, 1])
        p1, p2, p3 = c.ps("tw_p1", [P, 512]), c.ps("tw_p2", [P, 512]), c.ps("tw_p3", [P, 512])
        s_in, s_ch, s_w, s_ws, s_all = c.sem("tw_in"), c.sem("tw_ch"), c.sem("tw_ws"), c.sem("tw_stored"), c.sem("tw_all")
        s_gt, s_peak, s_pt, s_top, s_edge, s_ties, s_bef = [c.sem("tw_s" + n) for n in ("gt", "peak", "pt", "top", "edge", "ties", "bef")]
        with nc.Block() as block:
            @block.sync
            def _(sp):
                sp.dma_start(wr[:, :], spread(T["L0_ffn_wr"].rearrange("d a -> (d a)"), NW, D)).then_inc(s_in, 16)
                sp.dma_start(br[:, :], spread(T["L0_ffn_br"], NW, 1)).then_inc(s_in, 16)
                sp.wait_ge(s_w, 1)
                sp.dma_start(T["order"].rearrange("(w i) -> w i", i=WIN), w[:, :]).then_inc(s_ws, 16)
                sp.wait_ge(s_ws, 16)
                sp.dma_start(every[:, :], spread(T["order"], NW, N_NODES)).then_inc(s_all, 16)

            @block.vector
            def _(dve):
                link = chained(dve, s_ch)
                dve.wait_ge(s_in, 32)
                link(nc.vector.tensor_tensor(prod[:, :, :], Y[:, :, :], wr[:, :].unsqueeze(1).to_broadcast([NW, WIN, D]), ALU.mult))
                link(nc.vector.tensor_reduce(w[:, :], prod[:, :, :], AX, ALU.add))
                nc.vector.tensor_scalar(w[:, :], w[:, :], br[:, :], None, ALU.add).then_inc(s_w, 1)
                dve.wait_ge(s_w, 1)
                dve.wait_ge(s_all, 16)
                for i in range(WIN):
                    if i >= 2:
                        dve.wait_ge(s_gt, i - 1)
                    nc.vector.tensor_scalar(larger[:, i % 2, :], every[:, :], w[:, i:i + 1], 0.0, ALU.is_gt, ALU.add,
                                            accum_out=above[:, i:i + 1]).then_inc(s_gt, 1)
                dve.wait_ge(s_gt, WIN)
                link(nc.vector.tensor_scalar(inside[:, :], above[:, :], float(N_SEL), None, ALU.is_lt))
                link(nc.vector.tensor_scalar(cand[:, :], above[:, :], 1.0, None, ALU.add))
                link(nc.vector.tensor_tensor(cand[:, :], cand[:, :], inside[:, :], ALU.mult))
                nc.vector.tensor_reduce(peak[:, :], cand[:, :], AX, ALU.max).then_inc(s_peak, 1)
                dve.wait_ge(s_pt, 1)
                link(nc.vector.tensor_copy(peakT[:, 0:NW], p1[0:1, 0:NW]))
                nc.vector.tensor_reduce(top[:, :], peakT[:, 0:NW], AX, ALU.max).then_inc(s_top, 1)
                dve.wait_ge(s_edge, 1)
                link(nc.vector.tensor_scalar(edge[:, :], p2[0:NW, 0:1], -1.0, None, ALU.add))
                link(nc.vector.tensor_scalar(tie[:, :], above[:, :], edge[:, :], None, ALU.is_equal))
                nc.vector.tensor_reduce(ties[:, :], tie[:, :], AX, ALU.add).then_inc(s_ties, 1)
                dve.wait_ge(s_bef, 1)
                link(nc.vector.tensor_copy(before[:, :], p3[0:NW, 0:1]))
                link(nc.vector.tensor_tensor_scan(order[:, :], tie[:, :], tie[:, :], before[:, :], ALU.add, ALU.max))
                link(nc.vector.tensor_scalar(room[:, :], edge[:, :], -1.0, float(N_SEL), ALU.mult, ALU.add))
                link(nc.vector.tensor_scalar(order[:, :], order[:, :], room[:, :], None, ALU.is_le))
                link(nc.vector.tensor_tensor(order[:, :], order[:, :], tie[:, :], ALU.mult))
                link(nc.vector.tensor_scalar(inside[:, :], above[:, :], edge[:, :], None, ALU.is_lt))
                link(nc.vector.tensor_tensor(inside[:, :], inside[:, :], order[:, :], ALU.add))
                link(nc.vector.tensor_tensor(R.gate[:, :], inside[:, :], w[:, :], ALU.mult))

            @block.tensor
            def _(pe):
                pe.wait_ge(s_peak, 1)
                nc.tensor.transpose(p1[0:1, 0:NW], peak[:, :], K.ident[0:NW, 0:NW]).then_inc(s_pt, 1)
                pe.wait_ge(s_top, 1)
                nc.tensor.matmul(p2[0:NW, 0:1], K.ones[0:1, 0:NW], top[:, :], start=True, stop=True).then_inc(s_edge, 1)
                pe.wait_ge(s_ties, 1)
                nc.tensor.matmul(p3[0:NW, 0:1], K.before[0:NW, 0:NW], ties[:, :], start=True, stop=True).then_inc(s_bef, 1)


def routed_ffn(nc, K, T, X, Y, YT, R):
    with ExitStack() as stack:
        c = Ctx(nc, stack)
        NH1 = HID // P
        w1 = c.sb("rt_w1", [P, KC, HID])
        w2 = c.sb("rt_w2", [P, NH1, D])
        b1 = c.sb("rt_b1", [P, NH1])
        b2 = c.sb("rt_b2", [NW, D])
        H = [c.sb(f"rt_h{b}", [P, NH1, NCK * NW]) for b in range(2)]
        y = [c.sb(f"rt_y{b}", [NW, D]) for b in range(2)]
        pu = [c.ps(f"rt_pu{b}", [P, 512]) for b in range(3)]
        pd = [c.ps(f"rt_pd{b}", [P, 512]) for b in range(2)]
        s_in, s_u, s_h, s_d, s_y, s_x, s_res, s_hb = [c.sem("rt_s" + n) for n in ("in", "u", "h", "d", "y", "x", "res", "hb")]
        with nc.Block() as block:
            @block.sync
            def _(sp):
                sp.dma_start(w1[:, :, :], T["L0_ffn_w1"].rearrange("(k p) n -> p k n", p=P)).then_inc(s_in, 16)
                sp.dma_start(w2[:, :, :], T["L0_ffn_w2"].rearrange("(k p) n -> p k n", p=P)).then_inc(s_in, 16)
                sp.dma_start(b1[:, :], T["L0_ffn_b1"].rearrange("(k p) -> p k", p=P)).then_inc(s_in, 16)
                sp.dma_start(b2[:, :], spread(T["L0_ffn_b2"], NW, D)).then_inc(s_in, 16)

            @block.tensor
            def _(pe):
                pe.wait_ge(s_in, 64)

                def up(ck):
                    for m in range(NH1):
                        n = ck * NH1 + m
                        if n >= 3:
                            pe.wait_ge(s_h, n - 2)
                        for k in range(KC):
                            last = nc.tensor.matmul(pu[n % 3][:, 0:NCK * NW], w1[:, k, m * P:(m + 1) * P],
                                                    YT[:, k, ck * NCK:(ck + 1) * NCK, :].rearrange("p a w -> p (a w)"),
                                                    start=k == 0, stop=k == KC - 1)
                        last.then_inc(s_u, 1)

                def down(ck):
                    pe.wait_ge(s_h, (ck + 1) * NH1)
                    for a in range(NCK):
                        i = ck * NCK + a
                        if i >= 2:
                            pe.wait_ge(s_y, i - 1)
                        for m in range(NH1):
                            last = nc.tensor.matmul(pd[i % 2][0:NW, 0:D], H[ck % 2][:, m, a * NW:(a + 1) * NW], w2[:, m, :],
                                                    start=m == 0, stop=m == NH1 - 1)
                        last.then_inc(s_d, 1)

                up(0)
                for ck in range(1, NCHK):
                    up(ck)
                    down(ck - 1)
                down(NCHK - 1)

            @block.scalar
            def _(act):
                act.wait_ge(s_in, 64)
                for n in range(NCHK * NH1):
                    ck, m = divmod(n, NH1)
                    act.wait_ge(s_u, n + 1)
                    if m == 0 and ck >= 2:
                        act.wait_ge(s_d, (ck - 1) * NCK)
                    nc.scalar.activation(H[ck % 2][:, m, :], pu[n % 3][:, 0:NCK * NW], ACT.Gelu_apprx_tanh,
                                         bias=b1[:, m:m + 1]).then_inc(s_h, 1)

            @block.vector
            def _(dve):
                dve.wait_ge(s_in, 64)
                nc.vector.tensor_tensor(X[:, :, :], X[:, :, :], Y[:, :, :], ALU.add).then_inc(s_res, 1)
                dve.wait_ge(s_res, 1)
                for i in range(WIN):
                    dve.wait_ge(s_d, i + 1)
                    if i >= 2:
                        dve.wait_ge(s_x, i - 1)
                    nc.vector.tensor_tensor(y[i % 2][:, :], pd[i % 2][0:NW, 0:D], b2[:, :], ALU.add).then_inc(s_y, 1)
                    dve.wait_ge(s_y, i + 1)
                    nc.vector.scalar_tensor_tensor(X[:, i, :], y[i % 2][:, :], R.gate[:, i:i + 1], X[:, i, :],
                                                   ALU.mult, ALU.add).then_inc(s_x, 1)


HO = 2 * D


def load_transposed(nc, K, T, c, tag, items):
    with ExitStack() as stack, nc.Block() as block:
        s = Ctx(nc, stack)
        raw = [s.sb(f"lt_raw{q}_{tag}", [P, KC, D]) for q in range(len(items))]
        bank = [s.ps(f"lt_ps{b}_{tag}", [P, P]) for b in range(2)]
        s_in, s_t, s_c = s.sem(f"lt_in_{tag}"), s.sem(f"lt_t_{tag}"), s.sem(f"lt_c_{tag}")
        pieces = [(q, k, o) for q, (_, _, wide) in enumerate(items) for k in range(D // wide) for o in range(KC)]

        @block.sync
        def _(sp):
            for q, (src, _, _) in enumerate(items):
                sp.dma_start(raw[q][:, :, :], src.rearrange("(o p) n -> p o n", p=P)).then_inc(s_in, 16)

        @block.tensor
        def _(pe):
            pe.wait_ge(s_in, 16 * len(items))
            for n, (q, k, o) in enumerate(pieces):
                wide = items[q][2]
                if n >= 2:
                    pe.wait_ge(s_c, n - 1)
                nc.tensor.transpose(bank[n % 2][0:wide, :], raw[q][:, o, k * wide:(k + 1) * wide], K.ident[:, :]).then_inc(s_t, 1)

        @block.vector
        def _(dve):
            for n, (q, k, o) in enumerate(pieces):
                _, dst, wide = items[q]
                dve.wait_ge(s_t, n + 1)
                nc.vector.tensor_copy(dst[0:wide, k, o * P:(o + 1) * P], bank[n % 2][0:wide, :]).then_inc(s_c, 1)


def node_linear(nc, K, HT, W, bias, dst, tag, func=None, add=None):
    with ExitStack() as stack, nc.Block() as block:
        c = Ctx(nc, stack)
        bank = [c.ps(f"nl_ps{b}_{tag}", [P, 512]) for b in range(2)]
        s_m, s_v, s_r = c.sem(f"nl_m_{tag}"), c.sem(f"nl_v_{tag}"), c.sem(f"nl_r_{tag}")

        @block.tensor
        def _(pe):
            for i in range(WIN):
                if i >= 2:
                    pe.wait_ge(s_v, i - 1)
                for k in range(KC):
                    last = nc.tensor.matmul(bank[i % 2][0:NW, 0:D], HT[:, k, i, :], W[:, k, :], start=k == 0, stop=k == KC - 1)
                last.then_inc(s_m, 1)

        @block.vector
        def _(dve):
            for i in range(WIN):
                dve.wait_ge(s_m, i + 1)
                nc.vector.tensor_tensor(dst[:, i, :], bank[i % 2][0:NW, 0:D], bias[:, :], ALU.add).then_inc(s_v, 1)
            if func == "relu":
                dve.wait_ge(s_v, WIN)
                nc.vector.tensor_scalar(dst[:, :, :], dst[:, :, :], 0.0, None, ALU.max).then_inc(s_r, 1)
            if add is not None:
                dve.wait_ge(s_v, WIN)
                nc.vector.tensor_tensor(add[:, :, :], add[:, :, :], dst[:, :, :], ALU.add).then_inc(s_r, 1)


def load_rows(nc, T, tag, items):
    with ExitStack() as stack, nc.Block() as block:
        s_in = Ctx(nc, stack).sem(f"lr_in_{tag}")

        @block.sync
        def _(sp):
            for dst, src in items:
                sp.dma_start(dst, src).then_inc(s_in, 16)
            sp.wait_ge(s_in, 16 * len(items))


def project_qkv(nc, K, T, HT, QT, Wq, Wkv, bq, bkv):
    with ExitStack() as stack, nc.Block() as block:
        c = Ctx(nc, stack)
        rows = c.sb("pq_rows", [NW, 2, HO])
        bank = [c.ps(f"pq_ps{b}", [P, 512]) for b in range(2)]
        bq_ps = [c.ps(f"pq_q{b}", [P, 512]) for b in range(2)]
        s_kv, s_row, s_q, s_qc = c.sem("pq_kv"), c.sem("pq_row"), c.sem("pq_sq"), c.sem("pq_qc")
        s_st = [c.sem(f"pq_st{b}") for b in range(2)]
        qs = [(h, ck) for h in range(NH) for ck in range(NCHK)]

        @block.tensor
        def _(pe):
            for n in range(max(WIN, len(qs))):
                if n < WIN:
                    if n >= 2:
                        pe.wait_ge(s_row, n - 1)
                    for k in range(KC):
                        last = nc.tensor.matmul(bank[n % 2][0:NW, :], HT[:, k, n, :], Wkv[:, k, :], start=k == 0, stop=k == KC - 1)
                    last.then_inc(s_kv, 1)
                if n < len(qs):
                    h, ck = qs[n]
                    if n >= 2:
                        pe.wait_ge(s_qc, n - 1)
                    for k in range(KC):
                        last = nc.tensor.matmul(bq_ps[n % 2][0:HD, 0:NCK * NW], Wq[:, k, h * HD:(h + 1) * HD],
                                                HT[:, k, ck * NCK:(ck + 1) * NCK, :].rearrange("p a w -> p (a w)"),
                                                start=k == 0, stop=k == KC - 1)
                    last.then_inc(s_q, 1)

        @block.vector
        def _(dve):
            for i in range(WIN):
                dve.wait_ge(s_kv, i + 1)
                if i >= 2:
                    dve.wait_ge(s_st[i % 2], 16 * (i // 2))
                nc.vector.tensor_tensor(rows[:, i % 2, :], bank[i % 2][0:NW, :], bkv[:, :], ALU.add).then_inc(s_row, 1)

        @block.scalar
        def _(act):
            for n, (h, ck) in enumerate(qs):
                act.wait_ge(s_q, n + 1)
                nc.scalar.activation(QT[:, :, h, ck * NCK:(ck + 1) * NCK].rearrange("p w i -> p i w"),
                                     bq_ps[n % 2][0:HD, 0:NCK * NW].rearrange("p (i w) -> p i w", w=NW), ACT.Identity,
                                     bias=bq[:, h:h + 1]).then_inc(s_qc, 1)

        @block.sync
        def _(sp):
            table = T["kv"].rearrange("(w i) d -> w i d", i=WIN)
            for i in range(WIN):
                sp.wait_ge(s_row, i + 1)
                sp.dma_start(table[:, i, :], rows[:, i % 2, :]).then_inc(s_st[i % 2], 16)
            for b in range(2):
                sp.wait_ge(s_st[b], 16 * (WIN // 2))


NTY = 3
AR = HD + NTY


def head_attention(nc, K, T, R, QT, acc):
    with ExitStack() as stack, nc.Block() as block:
        c = Ctx(nc, stack)
        S16 = NH * NH
        DVE_TILES = 2
        NB = 3
        idx_s = [c.sb(f"ha_idx{b}", [P, GROUP], I32) for b in range(NB)]
        kv = [c.sb(f"ha_kv{b}", [P, GROUP, HO]) for b in range(NB)]
        kT = [c.sb(f"ha_kt{q}", [HD, NH, P]) for q in range(2)]
        hot = [c.sb(f"ha_hot{b}", [P, GROUP, WIN], BF16) for b in range(NB)]
        typ = [c.sb(f"ha_typ{b}", [P, GROUP, AR], BF16) for b in range(NB)]
        qw = c.sb("ha_qw", [HD, GROUP, HW])
        none = c.sb("ha_none", [P, AR], BF16)
        M = [c.sb(f"ha_m{q}", [P, S16, WIN]) for q in range(2)]
        s16 = [c.sb(f"ha_s{b}", [P, GROUP, S16]) for b in range(NB)]
        mx = [c.sb(f"ha_mx{b}", [P, GROUP, NH]) for b in range(NB)]
        A = c.sb("ha_a", [P, GROUP, S16, WIN])
        pk = [c.ps(f"ha_pk{q}", [P, 2, P]) for q in range(2)]
        pS = [c.ps(f"ha_ps{t}", [P, 512]) for t in range(GROUP)]
        pg = c.ps("ha_pg", [AR, GROUP, HW])
        sems = lambda n: [c.sem(f"ha_{n}{b}") for b in range(NB)]
        staged, arrived = sems("staged"), [[c.sem(f"ha_arr{b}{t}") for t in range(GROUP)] for b in range(NB)]
        s_kt = c.sem("ha_turned")
        s_kc = c.sem("ha_kcopied")
        s_sc = c.sem("ha_scores")
        s_sel = c.sem("ha_selected")
        s_red = c.sem("ha_reduced")
        s_hot, s_typ, s_mx, s_sub, s_exp = sems("hoted"), sems("typed"), sems("max"), sems("sub"), sems("exp")
        s_sum, s_rec, s_nrm, s_A = sems("sum"), sems("rec"), sems("norm"), sems("As")
        s_turned = sems("group_turned")
        s_gat = [[c.sem(f"ha_gat{b}{t}") for t in range(GROUP)] for b in range(NB)]
        s_acc = c.sem("ha_acc")
        s_z = c.sem("ha_zero")
        s_q = sems("queries")
        s_Ap = sems("As_pool")
        NP = NG // NB
        TB = NB * GROUP

        def spread_weights(eng, b, t):
            return eng.tensor_tensor(A[:, t, :, :], s16[b][:, t, :].unsqueeze(2).to_broadcast([P, S16, WIN]),
                                     hot[b][:, t, :].unsqueeze(1).to_broadcast([P, S16, WIN]), ALU.mult)

        @block.gpsimd
        def _(pool):
            bound = nc.gpsimd.to_reg(N_NODES - 1)

            def fetch(b, i):
                pool.wait_ge(s_turned[b], i)
                nc.gpsimd.tensor_tensor(idx_s[b][:, :], R.index[0][:, bass.ds(i * TB + (b - NB) * GROUP, GROUP)],
                                        K.zero_i[:, :], ALU.add).then_inc(staged[b], 1)
                for t in range(GROUP):
                    pool.wait_ge(K.ready, 1)
                    if t == 0:
                        pool.wait_ge(staged[b], i)
                    pool.wait_ge(s_gat[b][t], i)
                    nc.gpsimd.indirect_dma_start(
                        out=kv[b][:, t, :], out_offset=None, in_=T["kv"][:, :],
                        in_offset=bass.IndirectOffsetOnAxis(ap=idx_s[b][:, t:t + 1].bitcast(U32), axis=0),
                        bounds_check=bound, oob_is_err=False).then_inc(arrived[b][t], 16)

            def spread_out(b, i):
                pool.wait_ge(s_nrm[b], i + 1)
                for t in range(DVE_TILES, GROUP):
                    spread_weights(nc.gpsimd, b, t).then_inc(s_Ap[b], 1)

            for b in range(NB):
                fetch(b, 1)
                if b >= 2:
                    spread_out(b - 2, 0)
            with pool.Fori(2, NP + 1) as i:
                for b in range(NB):
                    fetch(b, i)
                    q, j = earlier(b, i, 2, NB)
                    spread_out(q, j - 1)
            for b in range(NB - 2, NB):
                pool.wait_ge(s_gat[b - 1][GROUP - 1], NP + 1)
                spread_out(b, NP - 1)

        @block.tensor
        def _(pe):
            for b in range(NB):
                pe.sem_inc(s_turned[b], 1)
                for t in range(GROUP):
                    pe.sem_inc(s_gat[b][t], 1)

            def turn(b, i, t):
                n = i * TB + b * GROUP + t
                pe.wait_ge(arrived[b][t], i * 16 + 16)
                pe.wait_ge(s_kc, n + 1)
                for k in range(2):
                    last = nc.tensor.transpose(pk[t % 2][:, k, :], kv[b][:, t, k * P:(k + 1) * P], K.ident[:, :])
                    if k == 0 and t == GROUP - 1:
                        last.then_inc(s_turned[b], 1)
                last.then_inc(s_kt, 1)

            def score(b, i, t):
                n = i * TB + b * GROUP + t
                pe.wait_ge(s_kc, n + 3)
                pe.wait_ge(s_sel, n + 1)
                for g in range(NH):
                    last = nc.tensor.matmul(pS[t][:, g * HW:(g + 1) * HW], kT[t % 2][:, g, :], qw[:, t, :],
                                            start=True, stop=True)
                last.then_inc(s_sc, 1)

            def gather(b, i, t):
                if t < DVE_TILES:
                    pe.wait_ge(s_A[b], i * DVE_TILES + t + 1)
                else:
                    pe.wait_ge(s_Ap[b], i * (GROUP - DVE_TILES) + t - DVE_TILES + 1)
                pe.wait_ge(s_acc, i * TB + (b + 1) * GROUP + 1)
                o = pg[:, t, :]
                at_node = hot[b][:, t, :].unsqueeze(1).to_broadcast([P, NH, WIN])
                nc.tensor.matmul(o, typ[b][:, t, :], at_node, start=True, stop=False)
                for g in range(NH):
                    nc.tensor.matmul(o[0:HD, :], kv[b][:, t, D + g * HD:D + (g + 1) * HD],
                                     A[:, t, g * NH:(g + 1) * NH, :].rearrange("p h n -> p (h n)"),
                                     start=False, stop=False)
                nc.tensor.matmul(o, none[:, :], at_node, start=False, stop=True).then_inc(s_gat[b][t], 1)

            def step(b, i):
                if live(b, i, 2, NB):
                    for t in range(GROUP):
                        gather(*earlier(b, i, 2, NB), t)
                if live(b, i, 0, NB):
                    turn(b, i, 0)
                    pe.wait_ge(s_q[b], i + 1)
                    for t in range(GROUP):
                        if t + 1 < GROUP:
                            turn(b, i, t + 1)
                        score(b, i, t)

            pipeline(pe, step, NB)

        @block.scalar
        def _(act):
            act.sem_inc(s_kc, 2)
            act.sem_inc(s_sc, 2)

            def stage_queries(b, i):
                w = [act.value_load(R.window_i[0:1, bass.ds(i * TB + b * GROUP + t, 1)], min_val=0, max_val=NW - 1)
                     for t in range(GROUP)]
                act.wait_ge(s_sc, i * TB + b * GROUP + 2)
                for t in range(GROUP):
                    last = nc.scalar.copy(qw[:, t, :], QT[:, bass.ds(w[t], 1), :, :].rearrange("p a h n -> p (a h n)"))
                last.then_inc(s_q[b], 1)

            def exps(b, i):
                act.wait_ge(s_sub[b], i + 1)
                nc.scalar.activation(s16[b][:, :, :], s16[b][:, :, :], ACT.Exp, scale=HD ** -0.5).then_inc(s_exp[b], 1)

            def step(b, i):
                for t in range(GROUP):
                    if live(b, i, 0, NB):
                        n = i * TB + b * GROUP + t
                        act.wait_ge(s_kt, n + 1)
                        act.wait_ge(s_sc, n + 1)
                        nc.scalar.copy(kT[t % 2][:, 0::2, :], pk[t % 2][0:HD, :, :])
                        nc.scalar.copy(kT[t % 2][:, 1::2, :], pk[t % 2][HD:P, :, :]).then_inc(s_kc, 1)
                    if t == 1 and live(b, i, 1, NB):
                        exps(*earlier(b, i, 1, NB))
                if live(b, i, -1, NB):
                    stage_queries(*earlier(b, i, -1, NB))

            stage_queries(0, 0)
            pipeline(act, step, NB, ahead=1)

        @block.vector
        def _(dve):
            nc.vector.memset(acc[:, :, :], 0.0).then_inc(s_acc, 1)
            nc.vector.memset(none[:, :], 0.0).then_inc(s_z, 1)
            for b in range(NB):
                nc.vector.memset(typ[b][:, :, :], 0.0).then_inc(s_z, 1)
            dve.sem_inc(s_acc, GROUP)
            dve.sem_inc(s_sel, GROUP)
            dve.wait_ge(s_z, 1 + NB)

            def select(b, i, between, load_windows):
                j0 = i * TB + b * GROUP
                dve.wait_ge(s_gat[b][GROUP - 1], i + 1)
                nc.vector.tensor_tensor(hot[b][:, :, :], R.node[:, bass.ds(j0, GROUP)].unsqueeze(2).to_broadcast([P, GROUP, WIN]),
                                        K.iota[:, :].unsqueeze(1).to_broadcast([P, GROUP, WIN]), ALU.is_equal).then_inc(s_hot[b], 1)
                nc.vector.tensor_tensor(typ[b][:, :, HD:AR], R.type[:, bass.ds(j0, GROUP)].unsqueeze(2).to_broadcast([P, GROUP, NTY]),
                                        K.iota[:, 0:NTY].unsqueeze(1).to_broadcast([P, GROUP, NTY]), ALU.is_equal).then_inc(s_typ[b], 1)
                dve.wait_ge(s_hot[b], i + 1)

                def mask(t):
                    dve.wait_ge(s_sc, j0 + t + 3)
                    if t >= 2:
                        dve.wait_ge(s_red, j0 + t - 1)
                    nc.vector.tensor_tensor(M[t % 2][:, :, :], pS[t][:, 0:S16 * WIN].rearrange("p (q n) -> p q n", n=WIN),
                                            hot[b][:, t, :].unsqueeze(1).to_broadcast([P, S16, WIN]), ALU.mult).then_inc(s_sel, 1)

                def total(t):
                    dve.wait_ge(s_sel, j0 + t + GROUP + 1)
                    nc.vector.tensor_reduce(s16[b][:, t, :], M[t % 2][:, :, :], AX, ALU.add).then_inc(s_red, 1)

                for t in range(0, GROUP, 2):
                    mask(t)
                    mask(t + 1)
                    load_windows(2)
                    total(t)
                    total(t + 1)
                between()
                dve.wait_ge(s_red, j0 + GROUP)
                nc.vector.tensor_reduce(mx[b][:, :, :], s16[b][:, :, :].rearrange("p t (g h) -> p t h g", h=NH), AX, ALU.max).then_inc(s_mx[b], 1)
                between()
                dve.wait_ge(s_mx[b], i + 1)
                q = s16[b][:, :, :].rearrange("p t (g h) -> p t g h", h=NH)
                nc.vector.tensor_tensor(q, q, mx[b][:, :, :].unsqueeze(2).to_broadcast([P, GROUP, NH, NH]), ALU.subtract).then_inc(s_sub[b], 1)

            def weights(b, i, between):
                between()
                dve.wait_ge(s_exp[b], i + 1)
                nc.vector.tensor_reduce(mx[b][:, :, :], s16[b][:, :, :].rearrange("p t (g h) -> p t h g", h=NH), AX, ALU.add).then_inc(s_sum[b], 1)
                between()
                dve.wait_ge(s_sum[b], i + 1)
                nc.vector.reciprocal(mx[b][:, :, :], mx[b][:, :, :]).then_inc(s_rec[b], 1)
                dve.wait_ge(s_rec[b], i + 1)
                q = s16[b][:, :, :].rearrange("p t (g h) -> p t g h", h=NH)
                nc.vector.tensor_tensor(q, q, mx[b][:, :, :].unsqueeze(2).to_broadcast([P, GROUP, NH, NH]), ALU.mult).then_inc(s_nrm[b], 1)
                dve.wait_ge(s_nrm[b], i + 1)

            def add(b, i, t, w):
                n = i * TB + b * GROUP + t
                dve.wait_ge(s_gat[b][GROUP - 1], i + 2)
                dve.wait_ge(s_acc, n + GROUP + 1)
                a = acc[:, bass.ds(w, 1), :]
                nc.vector.tensor_tensor(a, a, pg[:, t:t + 1, :], ALU.add).then_inc(s_acc, 1)

            def step(b, i):
                adds = list(range(GROUP)) if live(b, i, 1, NB) else []
                w = []

                def load_windows(n):
                    if live(b, i, 1, NB):
                        q, j = earlier(b, i, 1, NB)
                        for t in range(len(w), len(w) + n):
                            w.append(dve.value_load(R.window_i[0:1, bass.ds(j * TB + q * GROUP + t, 1)], min_val=0, max_val=NW - 1))

                def between():
                    if adds:
                        t = adds.pop(0)
                        add(*earlier(b, i, 1, NB), t, w[t])

                if live(b, i, 0, NB):
                    select(b, i, between, load_windows)
                    weights(b, i, between)
                else:
                    load_windows(GROUP)
                while adds:
                    between()
                if live(b, i, 0, NB):
                    for t in range(DVE_TILES):
                        spread_weights(nc.vector, b, t).then_inc(s_A[b], 1)

            pipeline(dve, step, NB)
            dve.wait_ge(s_acc, NT + GROUP + 1)


def node_update(nc, K, acc, Wo, H, tag):
    with ExitStack() as stack, nc.Block() as block:
        c = Ctx(nc, stack)
        bank = [c.ps(f"nu_ps{b}_{tag}", [P, 512]) for b in range(2)]
        s_m, s_v = c.sem(f"nu_m_{tag}"), c.sem(f"nu_v_{tag}")

        @block.tensor
        def _(pe):
            for i in range(WIN):
                if i >= 2:
                    pe.wait_ge(s_v, i - 1)
                for h in range(NH):
                    rows = AR if h == 0 else HD
                    last = nc.tensor.matmul(bank[i % 2][0:NW, 0:D], acc[0:rows, :, h * WIN + i], Wo[0:rows, h, :],
                                            start=h == 0, stop=h == NH - 1)
                last.then_inc(s_m, 1)

        @block.vector
        def _(dve):
            for i in range(WIN):
                dve.wait_ge(s_m, i + 1)
                nc.vector.tensor_tensor(H[:, i, :], H[:, i, :], bank[i % 2][0:NW, 0:D], ALU.add).then_inc(s_v, 1)


def edge_type_rows(nc, K, T, l, Wo, tag):
    with ExitStack() as stack, nc.Block() as block:
        c = Ctx(nc, stack)
        E = c.sb("et_e_" + tag, [NTY, D])
        bo = c.sb("et_bo_" + tag, [NTY, D])
        ET = c.sb("et_et_" + tag, [HD, NH, NTY])
        ew = c.sb("et_ew_" + tag, [NTY, D])
        pe_t = c.ps("et_pt_" + tag, [HD, NH, NTY])
        pe_o = c.ps("et_po_" + tag, [NTY, D])
        s_in, s_t, s_c, s_m, s_o, s_w = [c.sem(f"et_{n}_{tag}") for n in ("in", "t", "c", "m", "o", "w")]

        @block.sync
        def _(sp):
            sp.dma_start(E[:, :], T["L1_gnn_Eemb"][l]).then_inc(s_in, 16)
            sp.dma_start(bo[:, :], spread(T["L1_gnn_bo"][l], NTY, D)).then_inc(s_in, 16)
            sp.wait_ge(s_o, 1)
            sp.dma_start(Wo[HD:AR, 0, :], ew[:, :]).then_inc(s_w, 16)
            sp.wait_ge(s_w, 16)

        @block.tensor
        def _(pe):
            pe.wait_ge(s_in, 32)
            for h in range(NH):
                last = nc.tensor.transpose(pe_t[:, h, :], E[:, h * HD:(h + 1) * HD], K.ident[0:NTY, 0:NTY])
            last.then_inc(s_t, 1)
            pe.wait_ge(s_c, 1)
            for h in range(NH):
                last = nc.tensor.matmul(pe_o[:, :], ET[:, h, :], Wo[0:HD, h, :], start=h == 0, stop=h == NH - 1)
            last.then_inc(s_m, 1)

        @block.vector
        def _(dve):
            dve.wait_ge(s_t, 1)
            nc.vector.tensor_copy(ET[:, :, :], pe_t[:, :, :]).then_inc(s_c, 1)
            dve.wait_ge(s_m, 1)
            nc.vector.tensor_tensor(ew[:, :], pe_o[:, :], bo[:, :], ALU.add).then_inc(s_o, 1)


def scale_relu(nc, H, g, b, tag):
    with ExitStack() as stack, nc.Block() as block:
        s_ch = Ctx(nc, stack).sem("sr_ch_" + tag)

        @block.vector
        def _(dve):
            link = chained(dve, s_ch)
            link(nc.vector.tensor_tensor(H[:, :, :], H[:, :, :], g[:, :].unsqueeze(1).to_broadcast([NW, WIN, D]), ALU.mult))
            link(nc.vector.tensor_tensor(H[:, :, :], H[:, :, :], b[:, :].unsqueeze(1).to_broadcast([NW, WIN, D]), ALU.add))
            link(nc.vector.tensor_scalar(H[:, :, :], H[:, :, :], 0.0, None, ALU.max))


def message_layers(nc, K, T, R, H):
    for l in range(3):
        tag = f"l{l}"
        with ExitStack() as stack:
            c = Ctx(nc, stack)
            QT = c.sb("qt_" + tag, [HD, NW, NH, WIN])
            Wo = c.sb("wo_" + tag, [AR, NH, D])
            with ExitStack() as inner:
                ci = Ctx(nc, inner)
                HT = ci.sb("ht_" + tag, [P, KC, WIN, NW])
                Wq = ci.sb("wq_" + tag, [P, KC, D])
                Wkv = ci.sb("wkv_" + tag, [P, KC, HO])
                bq = ci.sb("bq_" + tag, [HD, NH])
                bkv = ci.sb("bkv_" + tag, [NW, HO])
                load_rows(nc, T, tag, [(bkv[:, 0:D], spread(T["L1_gnn_bk"][l], NW, D)), (bkv[:, D:HO], spread(T["L1_gnn_bv"][l], NW, D)),
                                       (bq[:, :], T["L1_gnn_bq"][l].rearrange("(h d) -> d h", h=NH))])
                load_transposed(nc, K, T, ci, tag, [(T["L1_gnn_Wq"][l], Wq, P), (T["L1_gnn_Wk"][l], Wkv[:, :, 0:D], P),
                                                    (T["L1_gnn_Wv"][l], Wkv[:, :, D:HO], P), (T["L1_gnn_Wo"][l], Wo, HD)])
                edge_type_rows(nc, K, T, l, Wo, tag)
                transpose_nodes(nc, K, H, HT, tag)
                project_qkv(nc, K, T, HT, QT, Wq, Wkv, bq, bkv)
            acc = c.sb("acc_" + tag, [AR, NW, HW])
            head_attention(nc, K, T, R, QT, acc)
            node_update(nc, K, acc, Wo, H, tag)
        layernorm(nc, K, H, H, tag)
        with ExitStack() as stack:
            c = Ctx(nc, stack)
            g, b = c.sb("ln_gain_" + tag, [NW, D]), c.sb("ln_bias_" + tag, [NW, D])
            load_rows(nc, T, tag + "b", [(g[:, :], spread(T["L1_gnn_ln_g"][l], NW, D)), (b[:, :], spread(T["L1_gnn_ln_b"][l], NW, D))])
            scale_relu(nc, H, g, b, tag)


NE = 4
EH1, EH2 = 128, 64


def expert_gates(nc, K, T, YT, R):
    with ExitStack() as stack, nc.Block() as block:
        c = Ctx(nc, stack)
        gW, gb = c.sb("eg_w", [P, KC, NE]), c.sb("eg_b", [NW, NE])
        G, cmp = c.sb("eg_g", [NW, WIN, NE]), c.sb("eg_cmp", [NW, WIN, NE])
        rank, red = c.sb("eg_rank", [NW, WIN, NE]), c.sb("eg_red", [NW, WIN])
        pg = c.ps("eg_ps", [NW, WIN, NE])
        s_in, s_m, s_ch, s_e, s_x = [c.sem("eg_s" + n) for n in ("in", "m", "ch", "e", "x")]
        wide = red[:, :].unsqueeze(2).to_broadcast([NW, WIN, NE])

        @block.sync
        def _(sp):
            sp.dma_start(gW[:, :, :], T["L1_ffn_gW"].rearrange("(k p) e -> p k e", p=P)).then_inc(s_in, 16)
            sp.dma_start(gb[:, :], spread(T["L1_ffn_gb"], NW, NE)).then_inc(s_in, 16)

        @block.tensor
        def _(pe):
            pe.wait_ge(s_in, 32)
            for i in range(WIN):
                for k in range(KC):
                    last = nc.tensor.matmul(pg[:, i, :], YT[:, k, i, :], gW[:, k, :], start=k == 0, stop=k == KC - 1)
            last.then_inc(s_m, 1)

        @block.vector
        def _(dve):
            link = chained(dve, s_ch)
            dve.wait_ge(s_in, 32)
            dve.wait_ge(s_m, 1)
            link(nc.vector.tensor_tensor(G[:, :, :], pg[:, :, :], gb[:, :].unsqueeze(1).to_broadcast([NW, WIN, NE]), ALU.add))
            link(nc.vector.tensor_reduce(red[:, :], G[:, :, :], AX, ALU.max))
            nc.vector.tensor_tensor(G[:, :, :], G[:, :, :], wide, ALU.subtract).then_inc(s_x, 1)
            dve.wait_ge(s_e, 1)
            link(nc.vector.tensor_reduce(red[:, :], G[:, :, :], AX, ALU.add))
            link(nc.vector.reciprocal(red[:, :], red[:, :]))
            link(nc.vector.tensor_tensor(G[:, :, :], G[:, :, :], wide, ALU.mult))
            for e in range(NE):
                own = G[:, :, e:e + 1]
                if e:
                    link(nc.vector.tensor_tensor(cmp[:, :, 0:e], G[:, :, 0:e], own.to_broadcast([NW, WIN, e]), ALU.is_ge))
                link(nc.vector.tensor_tensor(cmp[:, :, e:NE], G[:, :, e:NE], own.to_broadcast([NW, WIN, NE - e]), ALU.is_gt))
                link(nc.vector.tensor_reduce(rank[:, :, e], cmp[:, :, :], AX, ALU.add))
            link(nc.vector.tensor_scalar(rank[:, :, :], rank[:, :, :], 2.0, None, ALU.is_lt))
            link(nc.vector.tensor_reduce(red[:, :], G[:, :, :], AX, ALU.max))
            nc.vector.tensor_tensor(G[:, :, :], G[:, :, :], wide, ALU.subtract).then_inc(s_x, 1)
            dve.wait_ge(s_e, 2)
            link(nc.vector.tensor_tensor(G[:, :, :], G[:, :, :], rank[:, :, :], ALU.mult))
            link(nc.vector.tensor_reduce(red[:, :], G[:, :, :], AX, ALU.add))
            link(nc.vector.reciprocal(red[:, :], red[:, :]))
            link(nc.vector.tensor_tensor(R.share[:, :, :], G[:, :, :], wide, ALU.mult))

        @block.scalar
        def _(act):
            for n in range(2):
                act.wait_ge(s_x, n + 1)
                nc.scalar.activation(G[:, :, :], G[:, :, :], ACT.Exp).then_inc(s_e, 1)


def expert_ffn(nc, K, T, X, YT, R):
    with ExitStack() as stack, nc.Block() as block:
        c = Ctx(nc, stack)
        sW1, sW2, sW3 = c.sb("ef_s1", [P, KC, D]), c.sb("ef_s2", [P, KC, P]), c.sb("ef_s3", [P, D])
        sb1, sb2, sb3 = c.sb("ef_sb1", [P, KC]), c.sb("ef_sb2", [P, 1]), c.sb("ef_sb3", [NW, D])
        eW1, eW2 = c.sb("ef_e1", [P, NE, KC, EH1]), c.sb("ef_e2", [P, NE, EH2])
        eW3 = c.sb("ef_e3", [EH2 + 1, NE, D])
        eb1, eb2 = c.sb("ef_eb1", [P, NE]), c.sb("ef_eb2", [EH2, NE])
        NN = NCK * NW
        h1 = [c.sb(f"ef_h1{b}", [P, KC + NE, NN]) for b in range(2)]
        h2 = [c.sb(f"ef_h2{b}", [P, NN]) for b in range(2)]
        e2 = [c.sb(f"ef_g2{b}", [EH2 + 1, NE, NN]) for b in range(2)]
        pu = [c.ps(f"ef_pu{b}", [P, 512]) for b in range(4)]
        po = [c.ps(f"ef_po{b}", [P, 512]) for b in range(3)]
        s_in, s_u, s_a, s_o, s_x, s_one, s_b = [c.sem("ef_s" + n) for n in ("in", "u", "a", "o", "x", "one", "b")]
        s_1, s_2 = c.sem("ef_l1"), c.sem("ef_l2")
        loads = [(sW1[:, :, :], T["L1_ffn_sW1"].rearrange("(k p) n -> p k n", p=P)),
                 (sW2[:, :, :], T["L1_ffn_sW2"].rearrange("(k p) n -> p k n", p=P)), (sW3[:, :], T["L1_ffn_sW3"]),
                 (sb1[:, :], T["L1_ffn_sb1"].rearrange("(k p) -> p k", p=P)), (sb2[:, :], T["L1_ffn_sb2"].unsqueeze(1)),
                 (sb3[:, :], spread(T["L1_ffn_sb3"], NW, D)),
                 (eW2[:, :, :], T["L1_ffn_eW2"].rearrange("e p n -> p e n")),
                 (eW3[0:EH2, :, :], T["L1_ffn_eW3"].rearrange("e p n -> p e n")),
                 (eW3[EH2:EH2 + 1, :, :], T["L1_ffn_eb3"].unsqueeze(0)),
                 (eb1[:, :], T["L1_ffn_eb1"].rearrange("e p -> p e")), (eb2[:, :], T["L1_ffn_eb2"].rearrange("e p -> p e"))]
        loads += [(eW1[:, e, :, :], T["L1_ffn_eW1"][e].rearrange("(k p) n -> p k n", p=P)) for e in range(NE)]
        L1, L2 = KC + NE, 1 + NE
        NU = L1 + L2

        @block.sync
        def _(sp):
            for dst, src in loads:
                sp.dma_start(dst, src).then_inc(s_in, 16)
            sp.wait_ge(s_in, 16 * len(loads))

        @block.tensor
        def _(pe):
            pe.wait_ge(s_in, 16 * len(loads))
            pe.wait_ge(s_one, 2)

            def unit(ck, u):
                n = ck * NU + u
                if n >= 4:
                    pe.wait_ge(s_a, n - 3)
                bank = pu[n % 4]
                cols = YT[:, :, ck * NCK:(ck + 1) * NCK, :].rearrange("p k a w -> p k (a w)")
                if u < L1:
                    for k in range(KC):
                        w = sW1[:, k, u * P:(u + 1) * P] if u < KC else eW1[:, u - KC, k, :]
                        last = nc.tensor.matmul(bank[:, 0:NN], w, cols[:, k, :], start=k == 0, stop=k == KC - 1)
                elif u == L1:
                    pe.wait_ge(s_a, ck * NU + L1)
                    for k in range(KC):
                        last = nc.tensor.matmul(bank[:, 0:NN], sW2[:, k, :], h1[ck % 2][:, k, :], start=k == 0, stop=k == KC - 1)
                else:
                    e = u - L1 - 1
                    last = nc.tensor.matmul(bank[0:EH2, 0:NN], eW2[:, e, :], h1[ck % 2][:, KC + e, :], start=True, stop=True)
                last.then_inc(s_u, 1)

            def outputs(ck):
                pe.wait_ge(s_a, (ck + 1) * NU)
                for a in range(NCK):
                    for v in range(1 + NE):
                        n = (ck * NCK + a) * (1 + NE) + v
                        if n >= 3:
                            pe.wait_ge(s_x, n - 2)
                        part = slice(a * NW, (a + 1) * NW)
                        o = po[n % 3][0:NW, 0:D]
                        if v == 0:
                            nc.tensor.matmul(o, h2[ck % 2][:, part], sW3[:, :], start=True, stop=True).then_inc(s_o, 1)
                        else:
                            nc.tensor.matmul(o, e2[ck % 2][:, v - 1, part], eW3[:, v - 1, :], start=True, stop=True).then_inc(s_o, 1)

            for ck in range(NCHK):
                for u in range(NU):
                    unit(ck, u)
                if ck:
                    outputs(ck - 1)
            outputs(NCHK - 1)

        @block.scalar
        def _(act):
            act.wait_ge(s_in, 16 * len(loads))
            for ck in range(NCHK):
                for u in range(NU):
                    n = ck * NU + u
                    act.wait_ge(s_u, n + 1)
                    if u == 0 and ck >= 2:
                        act.wait_ge(s_o, (ck - 1) * NCK * (1 + NE))
                    if u < L1:
                        dst, src = h1[ck % 2][:, u, :], pu[n % 4][:, 0:NN]
                        bias = sb1[:, u:u + 1] if u < KC else eb1[:, u - KC:u - KC + 1]
                    elif u == L1:
                        dst, src, bias = h2[ck % 2][:, :], pu[n % 4][:, 0:NN], sb2[:, :]
                    else:
                        e = u - L1 - 1
                        dst, src, bias = e2[ck % 2][0:EH2, e, :], pu[n % 4][0:EH2, 0:NN], eb2[:, e:e + 1]
                    nc.scalar.activation(dst, src, ACT.Relu, bias=bias).then_inc(s_a, 1)

        @block.gpsimd
        def _(pool):
            for b in range(2):
                nc.gpsimd.memset(e2[b][EH2:EH2 + 1, :, :], 1.0).then_inc(s_one, 1)

        @block.vector
        def _(dve):
            dve.wait_ge(s_in, 16 * len(loads))
            nc.vector.tensor_tensor(X[:, :, :], X[:, :, :], sb3[:, :].unsqueeze(1).to_broadcast([NW, WIN, D]), ALU.add).then_inc(s_b, 1)
            dve.wait_ge(s_b, 1)
            for i in range(WIN):
                for v in range(1 + NE):
                    n = i * (1 + NE) + v
                    dve.wait_ge(s_o, n + 1)
                    if n:
                        dve.wait_ge(s_x, n)
                    if v == 0:
                        nc.vector.tensor_tensor(X[:, i, :], X[:, i, :], po[n % 3][0:NW, 0:D], ALU.add).then_inc(s_x, 1)
                    else:
                        nc.vector.scalar_tensor_tensor(X[:, i, :], po[n % 3][0:NW, 0:D], R.share[:, i, v - 1:v], X[:, i, :],
                                                       ALU.mult, ALU.add).then_inc(s_x, 1)


def node_rows(ap):
    return ap.rearrange("(w i) d -> w i d", i=WIN)


def build(nc, T, out):
    Ctx.used.clear()
    with ExitStack() as stack:
        stack.enter_context(nc.allow_non_contiguous_dma(reason="biases of a few hundred elements, one per partition"))
        c = Ctx(nc, stack)
        K = Bag()
        K.ident = c.sb("identity", [P, P])
        K.ones = c.sb("ones", [P, P])
        K.before = c.sb("before", [P, P])
        K.iota = c.sb("iota_window", [P, WIN], BF16)
        K.part = c.sb("iota_partition", [P, 1])
        K.tile_no = c.sb("iota_tile", [P, NT])
        K.zero_i = c.sb("zero_i", [P, GROUP], I32)
        K.ready = c.sem("constants_ready")
        X = c.sb("x", [NW, WIN, D])
        constants(nc, K)

        load_rows(nc, T, "x", [(X[:, :, :], node_rows(T["x"]))])
        with ExitStack() as st:
            c1 = Ctx(nc, st)
            Y, YT = c1.sb("y0", [NW, WIN, D]), c1.sb("yt0", [P, KC, WIN, NW])
            layernorm(nc, K, X, Y, "a")
            transpose_nodes(nc, K, Y, YT, "a")
            relation_features(nc, K, T, YT)
        with ExitStack() as st:
            c1 = Ctx(nc, st)
            R = Bag()
            R.window, R.window_i = c1.sb("win0", [P, NT]), c1.sb("wini0", [1, NT], I32)
            R.index = [c1.sb(f"idx0{f}", [P, NT], I32) for f in range(2)]
            R.node = c1.sb("node0", [P, NT], BF16)
            sort_edges(nc, K, T, "dst", [[("src", NREL), ("edge_type_8", 1)], [("dst", NREL), ("edge_type_8", 1)]],
                       "slots0", "bucket0", "s0", R)
            R.ev, R.negmax = c1.sb("ev", [P, NT, NH]), c1.sb("negmax", [HW, NT])
            edge_logits(nc, K, T, R)
            relation_attention(nc, K, T, R, X)

        with ExitStack() as st:
            c1 = Ctx(nc, st)
            R = Bag()
            Y, YT, R.gate = c1.sb("y1", [NW, WIN, D]), c1.sb("yt1", [P, KC, WIN, NW]), c1.sb("gate", [NW, WIN])
            layernorm(nc, K, X, Y, "b")
            token_weights(nc, K, T, Y, R)
            transpose_nodes(nc, K, Y, YT, "b")
            routed_ffn(nc, K, T, X, Y, YT, R)

        with ExitStack() as st:
            c1 = Ctx(nc, st)
            Y, YT = c1.sb("y2", [NW, WIN, D]), c1.sb("yt2", [P, KC, WIN, NW])
            WinT, b_in = c1.sb("win_t", [P, KC, D]), c1.sb("b_in", [NW, D])
            layernorm(nc, K, X, Y, "c")
            s_sum, s_park = c1.sem("residual"), c1.sem("parked")
            with nc.Block() as block:
                @block.vector
                def _(dve):
                    nc.vector.tensor_tensor(X[:, :, :], X[:, :, :], Y[:, :, :], ALU.add).then_inc(s_sum, 1)

                @block.sync
                def _(sp):
                    sp.wait_ge(s_sum, 1)
                    sp.dma_start(node_rows(T["park"]), X[:, :, :]).then_inc(s_park, 16)
                    sp.wait_ge(s_park, 16)
            load_rows(nc, T, "win", [(b_in[:, :], spread(T["L1_gnn_b_in"], NW, D))])
            load_transposed(nc, K, T, c1, "win", [(T["L1_gnn_Win"], WinT, P)])
            transpose_nodes(nc, K, Y, YT, "c")
            node_linear(nc, K, YT, WinT, b_in, X, "win")
        H = X
        with ExitStack() as st:
            c1 = Ctx(nc, st)
            R = Bag()
            R.window_i, R.node, R.type = c1.sb("wini1", [1, NT], I32), c1.sb("node1", [P, NT], BF16), c1.sb("type1", [P, NT], BF16)
            R.index = [c1.sb("idx10", [P, NT], I32), R.type]
            with ExitStack() as st2:
                R.window = Ctx(nc, st2).sb("win1", [P, NT])
                sort_edges(nc, K, T, "src", [[("dst", 1)], [("edge_type_3", 1)]], "slots1", "bucket1", "s1", R)
            message_layers(nc, K, T, R, H)
        with ExitStack() as st:
            c1 = Ctx(nc, st)
            HT, B = c1.sb("ht_adj", [P, KC, WIN, NW]), c1.sb("adj", [NW, WIN, D])
            W1T, W2T = c1.sb("w1_t", [P, KC, D]), c1.sb("w2_t", [P, KC, D])
            b1, b2 = c1.sb("b1_adj", [NW, D]), c1.sb("b2_adj", [NW, D])
            load_rows(nc, T, "adj", [(b1[:, :], spread(T["L1_gnn_b1"], NW, D)), (b2[:, :], spread(T["L1_gnn_b2"], NW, D))])
            load_transposed(nc, K, T, c1, "adj", [(T["L1_gnn_W1"], W1T, P), (T["L1_gnn_W2"], W2T, P)])
            transpose_nodes(nc, K, H, HT, "adj1")
            node_linear(nc, K, HT, W1T, b1, B, "adj1", func="relu")
            load_rows(nc, T, "park", [(X[:, :, :], node_rows(T["park"]))])
            transpose_nodes(nc, K, B, HT, "adj2")
            node_linear(nc, K, HT, W2T, b2, B, "adj2", add=X)

        with ExitStack() as st:
            c1 = Ctx(nc, st)
            R = Bag()
            Y, YT, R.share = c1.sb("y3", [NW, WIN, D]), c1.sb("yt3", [P, KC, WIN, NW]), c1.sb("share", [NW, WIN, NE])
            layernorm(nc, K, X, Y, "d")
            transpose_nodes(nc, K, Y, YT, "d")
            expert_gates(nc, K, T, YT, R)
            expert_ffn(nc, K, T, X, YT, R)
        stored = c.sem("output_stored")
        with nc.Block() as block:
            @block.sync
            def _(sp):
                sp.dma_start(node_rows(out), X[:, :, :]).then_inc(stored, 16)
                sp.wait_ge(stored, 16)


SCRATCH = [("feat", (N_NODES * NREL, D), F32), ("logit0", (N_NODES * NREL, NH), F32), ("logit1", (N_NODES * NREL, NH), F32),
           ("bucket0", (N_EDGES,), BF16), ("bucket1", (N_EDGES,), BF16), ("slots0", (P * NT, 4), F32), ("slots1", (P * NT, 4), F32),
           ("order", (N_NODES,), F32), ("park", (N_NODES, D), F32), ("kv", (N_NODES, 2 * D), F32)]


def kernel(**inputs):
    import numpy as _np
    import concourse.bacc as _bacc
    from concourse import mybir as _mybir
    from concourse.bass_utils import run_bass_kernel_spmd as _run
    nc = _bacc.Bacc("TRN2", target_bir_lowering=False, num_devices=1)
    arrays, T = {}, {}
    for name, value in inputs.items():
        a = _np.ascontiguousarray(value)
        arrays[f"in_{name}"] = a
        T[name] = nc.dram_tensor(f"in_{name}", a.shape, _mybir.dt.from_np(a.dtype), kind="ExternalInput").ap()
    for name, shape, dt in SCRATCH:
        T[name] = nc.dram_tensor(f"scratch_{name}", shape, dt).ap()
    out = nc.dram_tensor("out_x", (N_NODES, D), F32, kind="ExternalOutput").ap()
    build(nc, T, out)
    r = _run(nc, [arrays], core_ids=[0])
    return r.results[0]["out_x"]
```

```python
import concourse.bass as bass
from concourse import mybir
from contextlib import ExitStack

F32 = mybir.dt.float32
BF16 = mybir.dt.bfloat16
I32 = mybir.dt.int32
U32 = mybir.dt.uint32
ALU = mybir.AluOpType
ACT = mybir.ActivationFunctionType
AX = mybir.AxisListType.X

P = 128
N_NODES, D = 3750, 256
N_EDGES = 60000
KC = D // P
NH, HD = 4, 64
NREL = 8
WIN = 30
NW = N_NODES // WIN
HW = NH * WIN
GROUP = 4
NT = -(-((N_EDGES + (P - 1) * NW) // P) // (6 * GROUP)) * 6 * GROUP
NG = NT // GROUP
SLICE = 120
NSL = N_EDGES // SLICE
SB = 4
SK = NSL // SB
CH = 20
NCH = NSL // CH
ROUND = 12582912.0
NEG = -1.0e30
FLOOR = -1.0e20
EPS = 1e-5
FROW = NREL * D


class Ctx:

    def __init__(self, nc, stack):
        self.nc, self.stack, self.sems = nc, stack, []

    used = {}

    def own(self, name):
        n = self.used[name] = self.used.get(name, 0) + 1
        return name if n == 1 else f"{name}_{n}"

    def sb(self, name, shape, dt=F32):
        return self.stack.enter_context(self.nc.sbuf_tensor(self.own(name), shape, dt))

    def ps(self, name, shape):
        bank = self.stack.enter_context(self.nc.psum_tensor(self.own(name), [P, 512], F32))
        n = 1
        for m in shape[1:]:
            n *= m
        view = bank[0:shape[0], 0:n]
        return view if len(shape) == 2 else view.rearrange("p (a b) -> p a b", b=shape[2])

    def sem(self, name):
        if not self.sems:
            self.stack.callback(self.clear)
        self.sems.append(self.nc.alloc_semaphore(self.own(name)))
        return self.sems[-1]

    def clear(self):
        self.nc.clear_and_free_semaphores(self.sems)
        self.nc.all_engine_barrier()

    def block(self):
        return self.stack.enter_context(self.nc.Block())


def chained(eng, sem):
    count = [0]

    def link(ins):
        count[0] += 1
        ins.then_inc(sem, 1)
        eng.wait_ge(sem, count[0])

    return link


def spread(ap, parts, n):
    return ap.unsqueeze(0).to_broadcast([parts, n])


class Bag:
    pass


def constants(nc, K):
    with ExitStack() as stack:
        c = Ctx(nc, stack)
        s_fill, s_made, s_conv = c.sem("const_filled"), c.sem("const_made"), c.sem("const_converted")
        iota_i = c.sb("iota_i", [P, WIN], I32)
        part_i = c.sb("part_i", [P, 1], I32)
        tile_i = c.sb("tile_i", [P, NT], I32)
        block = c.block()

        @block.gpsimd
        def _(pool):
            nc.gpsimd.memset(K.ident[:, :], 1.0).then_inc(s_fill, 1)
            nc.gpsimd.memset(K.ones[:, :], 1.0).then_inc(s_fill, 1)
            nc.gpsimd.memset(K.before[:, :], 1.0).then_inc(s_fill, 1)
            nc.gpsimd.memset(K.zeros_i[:, :], 0).then_inc(s_fill, 1)
            nc.gpsimd.memset(K.zeros[:, :], 0.0).then_inc(s_fill, 1)
            pool.wait_ge(s_fill, 5)
            nc.gpsimd.affine_select(out=K.ident[:, :], in_=K.ident[:, :], compare_op=ALU.is_equal, fill=0.0,
                                    base=0, pattern=[[-1, P]], channel_multiplier=1).then_inc(s_made, 1)
            nc.gpsimd.affine_select(out=K.before[:, :], in_=K.before[:, :], compare_op=ALU.is_gt, fill=0.0,
                                    base=0, pattern=[[1, P]], channel_multiplier=-1).then_inc(s_made, 1)
            nc.gpsimd.iota(iota_i[:, :], pattern=[[1, WIN]], base=0, channel_multiplier=0).then_inc(s_made, 1)
            nc.gpsimd.iota(part_i[:, :], pattern=[[1, 1]], base=0, channel_multiplier=1).then_inc(s_made, 1)
            nc.gpsimd.iota(tile_i[:, :], pattern=[[1, NT]], base=0, channel_multiplier=0).then_inc(s_made, 1)

        @block.vector
        def _(dve):
            dve.wait_ge(s_made, 5)
            nc.vector.tensor_copy(K.iota[:, :], iota_i[:, :]).then_inc(s_conv, 1)
            nc.vector.tensor_copy(K.part[:, :], part_i[:, :]).then_inc(s_conv, 1)
            nc.vector.tensor_copy(K.tile_no[:, :], tile_i[:, :]).then_inc(K.ready, 1)


def layernorm(nc, K, X, Y, tag):
    with ExitStack() as stack:
        c = Ctx(nc, stack)
        stats = c.sb("ln_stats_" + tag, [NW, WIN, 6])
        mv = c.sb("ln_mv_" + tag, [NW, WIN, 2])
        std = c.sb("ln_std_" + tag, [NW, WIN])
        s_stats, s_mv, s_var = c.sem("ln_stats_" + tag), c.sem("ln_mv_" + tag), c.sem("ln_var_" + tag)
        s_std, s_rstd, s_out = c.sem("ln_std_" + tag), c.sem("ln_rstd_" + tag), c.sem("ln_out_" + tag)
        block = c.block()

        @block.vector
        def _(dve):
            with dve.Fori(0, WIN) as i:
                nc.vector.bn_stats(stats[:, bass.ds(i, 1), :].rearrange("p a s -> p (a s)"),
                                   X[:, bass.ds(i, 1), :].rearrange("p a d -> p (a d)")).then_inc(s_stats, 1)
            dve.wait_ge(s_stats, WIN)
            for i in range(WIN):
                nc.vector.bn_aggr(mv[:, i, :], stats[:, i, :]).then_inc(s_mv, 1)
            dve.wait_ge(s_mv, WIN)
            nc.vector.tensor_scalar(mv[:, :, 1], mv[:, :, 1], EPS, None, ALU.add).then_inc(s_var, 1)
            dve.wait_ge(s_std, 1)
            nc.vector.reciprocal(mv[:, :, 1], std[:, :]).then_inc(s_rstd, 1)
            dve.wait_ge(s_rstd, 1)
            for i in range(WIN):
                nc.vector.tensor_scalar(Y[:, i, :], X[:, i, :], mv[:, i, 0:1], mv[:, i, 1:2],
                                        ALU.subtract, ALU.mult).then_inc(s_out, 1)

        @block.scalar
        def _(act):
            act.wait_ge(s_var, 1)
            nc.scalar.activation(std[:, :], mv[:, :, 1], ACT.Sqrt).then_inc(s_std, 1)


def transpose_nodes(nc, K, Y, YT, tag):
    with ExitStack() as stack:
        c = Ctx(nc, stack)
        pt = [c.ps(f"tn_ps{b}_" + tag, [P, 2, P]) for b in range(2)]
        s_t, s_free = c.sem("tn_transposed_" + tag), c.sem("tn_bank_free_" + tag)
        block = c.block()

        @block.tensor
        def _(pe):
            for i in range(WIN):
                pe.wait_ge(s_free, i + 1)
                for k in range(KC):
                    last = nc.tensor.transpose(pt[i % 2][:, k, 0:NW], Y[:, i, k * P:(k + 1) * P], K.ident[0:NW, 0:NW])
                last.then_inc(s_t, 1)

        @block.scalar
        def _(act):
            act.sem_inc(s_free, 2)
            with act.Fori(0, WIN // 2) as j:
                for b in range(2):
                    act.wait_ge(s_t, j * 2 + b + 1)
                    nc.scalar.activation(YT[:, :, bass.ds(j * 2 + b, 1), :].rearrange("p k a w -> p k (a w)"),
                                         pt[b][:, :, 0:NW], ACT.Copy).then_inc(s_free, 1)


def relation_features(nc, K, T, YT, S, passes):
    with ExitStack() as stack:
        c = Ctx(nc, stack)
        NQ = FROW // 512
        W = c.sb("rf_w", [P, KC, FROW])
        prod = c.sb("rf_prod", [P, FROW])
        attn = [c.sb(f"rf_attn{a}", [P, FROW]) for a in range(2)]
        WA = c.sb("rf_wa", [P, KC, 2, NREL * NH])
        stage = c.sb("rf_stage", [NW, 2, FROW])
        logits = c.sb("rf_logits", [NW, 2, WIN, NREL * NH])
        bank = [c.ps(f"rf_ps{q}", [P, 512]) for q in range(NQ)]
        bank_l = [c.ps(f"rf_psl{b}", [P, 2, NREL * NH]) for b in range(2)]
        s_w, s_wa, s_prod = c.sem("rf_weights"), c.sem("rf_wa_parts"), c.sem("rf_product")
        full = [c.sem(f"rf_full{q}") for q in range(NQ)]
        copied = [c.sem(f"rf_copied{q}") for q in range(NQ)]
        full_l = [c.sem(f"rf_full_l{b}") for b in range(2)]
        copied_l = [c.sem(f"rf_copied_l{b}") for b in range(2)]
        stored = [c.sem(f"rf_stored{b}") for b in range(2)]
        s_lst = c.sem("rf_logits_stored")
        block = c.block()

        @block.sync
        def _(sp):
            for a, name in enumerate(("L0_gnn_attn_l", "L0_gnn_attn_r")):
                sp.dma_start(attn[a][:, :], spread(T[name].rearrange("r h d -> (r h d)"), P, FROW)).then_inc(stored[a], 16)
            for r in range(NREL):
                for h in range(NH):
                    q = r * NH + h
                    sp.dma_start(W[:, :, q * HD:(q + 1) * HD],
                                 T["L0_gnn_conv_weights"][r, h].rearrange("(k p) d -> p k d", p=P)).then_inc(s_w, 16)
            table = T["feat"].rearrange("(w i r) d -> w i (r d)", i=WIN, r=NREL)
            with sp.Fori(0, WIN // 2) as j:
                for b in range(2):
                    for q in range(NQ):
                        sp.wait_ge(copied[q], j * 2 + b + 2)
                    sp.dma_start(table[:, bass.ds(j * 2 + b, 1), :], stage[:, b:b + 1, :]).then_inc(stored[b], 16)
            for b in range(2):
                sp.wait_ge(copied_l[b], WIN // 2 + 1)
            for a in range(2):
                sp.dma_start(T[f"logit{a}"].rearrange("(w q) h -> w (q h)", w=NW),
                             logits[:, a, :, :].rearrange("p i q -> p (i q)")).then_inc(s_lst, 16)
            sp.wait_ge(s_lst, 32)
            for b in range(2):
                sp.wait_ge(stored[b], 16 + 16 * (WIN // 2))

        def copy_rows(eng, op, q, j, b):
            eng.wait_ge(full[q], j * 2 + b + 1)
            eng.wait_ge(stored[b], j * 16 + 16)
            op(stage[:, b, q * 512:(q + 1) * 512], bank[q][0:NW, :]).then_inc(copied[q], 1)

        @block.gpsimd
        def _(pool):
            scatter_edges(nc, pool, K, T, c, S, passes)

        @block.vector
        def _(dve):
            dve.wait_ge(s_w, 16 * NREL * NH)
            for a in range(2):
                dve.wait_ge(stored[a], 16)
            n = 0
            for k in range(KC):
                for a in range(2):
                    if n:
                        dve.wait_ge(s_wa, n)
                    n += 1
                    nc.vector.tensor_tensor(prod[:, :], W[:, k, :], attn[a][:, :], ALU.mult).then_inc(s_prod, 1)
                    dve.wait_ge(s_prod, n)
                    nc.vector.tensor_reduce(WA[:, k, a, :], prod[:, :].rearrange("p (q d) -> p q d", d=HD),
                                            AX, ALU.add).then_inc(s_wa, 1)
            dve.sem_inc(copied[0], 1)
            dve.sem_inc(copied[1], 1)
            for b in range(2):
                dve.sem_inc(copied_l[b], 1)
            with dve.Fori(0, WIN // 2) as j:
                for b in range(2):
                    for q in (0, 1):
                        copy_rows(dve, nc.vector.tensor_copy, q, j, b)
                    dve.wait_ge(full_l[b], j + 1)
                    nc.vector.tensor_copy(logits[:, :, bass.ds(j * 2 + b, 1), :].rearrange("p a i q -> p a (i q)"),
                                          bank_l[b][0:NW, :, :]).then_inc(copied_l[b], 1)

        @block.scalar
        def _(act):
            act.sem_inc(copied[2], 1)
            act.sem_inc(copied[3], 1)
            with act.Fori(0, WIN // 2) as j:
                for b in range(2):
                    for q in (2, 3):
                        copy_rows(act, nc.scalar.copy, q, j, b)

        @block.tensor
        def _(pe):
            pe.wait_ge(s_w, 16 * NREL * NH)
            pe.wait_ge(s_wa, 2 * KC)
            for i in range(WIN):
                for q in range(NQ):
                    pe.wait_ge(copied[q], i + 1)
                    for k in range(KC):
                        last = nc.tensor.matmul(bank[q][0:NW, :], YT[:, k, i, :], W[:, k, q * 512:(q + 1) * 512],
                                                start=k == 0, stop=k == KC - 1)
                    last.then_inc(full[q], 1)
                pe.wait_ge(copied_l[i % 2], i // 2 + 1)
                for k in range(KC):
                    last = nc.tensor.matmul(bank_l[i % 2][0:NW, :, :].rearrange("p a q -> p (a q)"), YT[:, k, i, :],
                                            WA[:, k, :, :].rearrange("p a q -> p (a q)"), start=k == 0, stop=k == KC - 1)
                last.then_inc(full_l[i % 2], 1)


def sort_edges(nc, K, T, key, fields, slots, bucket, tag, R, S, beside=None):
    nf = len(fields)
    names = sorted({n for terms in fields for n, _ in terms} | {key})
    with ExitStack() as stack:
        c = Ctx(nc, stack)
        raw = {n: c.sb(f"so_raw_{n}_" + tag, [SK, SB, SLICE], I32) for n in names}
        val = {n: c.sb(f"so_val_{n}_" + tag, [SK, SB, SLICE]) for n in names}
        bk = c.sb("so_bucket_" + tag, [SK, SB, SLICE])
        bkh = c.sb("so_bucket_bf_" + tag, [SK, SB, SLICE], BF16)
        F = [c.sb(f"so_field{f}_" + tag, [SK, SB, SLICE]) for f in range(nf + 1)]
        empty = c.sb("so_empty_" + tag, [P, NT, 4])
        keys = [c.sb(f"so_keys{b}_" + tag, [NW, CH * SLICE], BF16) for b in range(2)]
        hot = [c.sb(f"so_hot{b}_" + tag, [NW, CH * SLICE], BF16) for b in range(2)]
        scan = [c.sb(f"so_scan{b}_" + tag, [NW, CH * SLICE]) for b in range(2)]
        hit = [c.sb(f"so_hit{b}_" + tag, [NW, CH * SLICE]) for b in range(2)]
        count = c.sb("so_count_" + tag, [NW, NCH])
        total = c.sb("so_total_" + tag, [NW, 1])
        tiles = c.sb("so_tiles_" + tag, [NW, 1])
        first = c.sb("so_first_" + tag, [NW, 1])
        carry = c.sb("so_carry_" + tag, [NW, 1])
        reach = c.sb("so_reach_" + tag, [NW, NT])
        place = c.sb("so_place_" + tag, [SLICE, NSL])
        tile = c.sb("so_tile_" + tag, [SLICE, NSL])
        addr = c.sb("so_addr_" + tag, [SLICE, NSL])
        window = c.sb("so_window_" + tag, [P, NT])
        pay, addr_i = S.pay, S.addr
        pt = [c.ps(f"so_pt{q}_" + tag, [P, 512]) for q in range(2)]
        ppos = c.ps("so_ppos_" + tag, [P, 512])
        pw = [c.ps(f"so_pw{q}_" + tag, [P, 512]) for q in range(2)]
        pf = c.ps("so_pf_" + tag, [P, 8])
        sem = lambda n: c.sem("so_" + n + "_" + tag)
        s_ld, s_ch, s_bk, s_bks, s_tr, s_pay = sem("loaded"), sem("chain"), sem("bucket"), sem("bucket_stored"), sem("transposed"), sem("pay")
        s_kin = [sem(f"keys_in{b}") for b in range(2)]
        s_cnt, s_first, s_wb, s_win = sem("counted"), sem("first"), sem("window_of_tile"), sem("win")
        s_hot, s_scan, s_hit, s_hfree = sem("hot"), sem("scanned"), sem("hit"), sem("hit_free")
        s_empty, s_estored, s_ch2, s_ch3 = sem("empty"), sem("empty_stored"), sem("chain2"), sem("chain3")

        with nc.Block() as block:
            @block.sync
            def _(sp):
                for n in names:
                    sp.dma_start(raw[n][:, :, :], T[n].rearrange("(b k p) -> k b p", b=SB, p=SLICE)).then_inc(s_ld, 16)
                sp.wait_ge(s_bk, 1)
                sp.dma_start(T[bucket].rearrange("(b k p) -> k b p", b=SB, p=SLICE), bkh[:, :, :]).then_inc(s_bks, 16)
                sp.wait_ge(s_empty, 2)
                sp.dma_start(T[slots].rearrange("(s j) q -> s (j q)", s=P),
                             empty[:, :, :].rearrange("p j q -> p (j q)")).then_inc(s_estored, 16)
                sp.wait_ge(s_bks, 16)
                sp.wait_ge(s_estored, 16)

            @block.gpsimd
            def _(pool):
                nc.gpsimd.memset(empty[:, :, :], 0.0).then_inc(s_empty, 1)
                pool.wait_ge(s_empty, 1)
                nc.gpsimd.memset(empty[:, :, 2:3], -1.0).then_inc(s_empty, 1)

            @block.vector
            def _(dve):
                link = chained(dve, s_ch)
                dve.wait_ge(s_ld, 16 * len(names))
                for n in names:
                    link(nc.vector.tensor_copy(val[n][:, :, :], raw[n][:, :, :]))
                link(nc.vector.tensor_scalar(bk[:, :, :], val[key][:, :, :], -(WIN - 1) / 2, 1.0 / WIN, ALU.add, ALU.mult))
                link(nc.vector.tensor_scalar(bk[:, :, :], bk[:, :, :], ROUND, None, ALU.add))
                link(nc.vector.tensor_scalar(bk[:, :, :], bk[:, :, :], -ROUND, None, ALU.add))
                nc.vector.tensor_copy(bkh[:, :, :], bk[:, :, :]).then_inc(s_bk, 1)
                for f, terms in enumerate(fields):
                    n0, m0 = terms[0]
                    link(nc.vector.tensor_scalar(F[f][:, :, :], val[n0][:, :, :], float(m0), None, ALU.mult))
                    for n1, m1 in terms[1:]:
                        link(nc.vector.scalar_tensor_tensor(F[f][:, :, :], val[n1][:, :, :], float(m1), F[f][:, :, :],
                                                            ALU.mult, ALU.add))
                link(nc.vector.scalar_tensor_tensor(F[nf][:, :, :], bk[:, :, :], -float(WIN), val[key][:, :, :],
                                                    ALU.mult, ALU.add))
                nc.vector.memset(pay[:, :, 3:4], 0.0).then_inc(s_pay, 1)
                for f in range(nf + 1):
                    dve.wait_ge(s_tr, f + 1)
                    nc.vector.tensor_copy(pay[:, :, f:f + 1].rearrange("p s a -> p (s a)"),
                                          pt[f % 2][0:SLICE, 0:NSL]).then_inc(s_pay, 1)

            @block.tensor
            def _(pe):
                pe.wait_ge(s_ch, len(names) + 3 + sum(len(t) for t in fields) + 1)
                for f in range(nf + 1):
                    if f >= 2:
                        pe.wait_ge(s_pay, f)
                    for b in range(SB):
                        last = nc.tensor.transpose(pt[f % 2][0:SLICE, b * SK:(b + 1) * SK], F[f][:, b, :],
                                                   K.ident[0:SK, 0:SK])
                    last.then_inc(s_tr, 1)

        keys_of = lambda ch: T[bucket][bass.ds(ch * CH * SLICE, CH * SLICE)].unsqueeze(0).to_broadcast([NW, CH * SLICE])
        with nc.Block() as block:
            if beside:
                @block.gpsimd
                def _(pool):
                    scatter_edges(nc, pool, K, T, c, beside[0], beside[1])

            @block.sync
            def _(sp):
                for ch in range(NCH):
                    b = ch % 2
                    if ch >= 2:
                        sp.wait_ge(s_cnt, ch - 1)
                    sp.dma_start(keys[b][:, :], keys_of(ch)).then_inc(s_kin[b], 16)

            @block.vector
            def _(dve):
                for ch in range(NCH):
                    b = ch % 2
                    dve.wait_ge(s_kin[b], 16 * (ch // 2 + 1))
                    if ch >= 2:
                        dve.wait_ge(s_cnt, ch - 1)
                    nc.vector.tensor_scalar(hot[b][:, :], keys[b][:, :], K.part[0:NW, :], 0.0, ALU.is_equal, ALU.add,
                                            accum_out=count[:, ch:ch + 1]).then_inc(s_cnt, 1)
                dve.wait_ge(s_cnt, NCH)
                link = chained(dve, s_ch2)
                link(nc.vector.tensor_reduce(total[:, :], count[:, :], AX, ALU.add))
                link(nc.vector.tensor_scalar(tiles[:, :], total[:, :], 63.25, 1.0 / P, ALU.add, ALU.mult))
                link(nc.vector.tensor_scalar(tiles[:, :], tiles[:, :], ROUND, None, ALU.add))
                link(nc.vector.tensor_scalar(tiles[:, :], tiles[:, :], -ROUND, None, ALU.add))
                dve.wait_ge(s_first, 1)
                link(nc.vector.tensor_copy(first[:, :], pf[0:NW, 0:1]))
                link(nc.vector.tensor_scalar(carry[:, :], first[:, :], float(P), None, ALU.mult))
                link(nc.vector.tensor_scalar(reach[:, :], K.tile_no[0:NW, :], first[:, :], None, ALU.is_ge))
                for q in range(2):
                    dve.wait_ge(s_wb, q + 1)
                    nc.vector.tensor_scalar(window[:, q * (NT // 2):(q + 1) * (NT // 2)], pw[q][:, 0:NT // 2], -1.0, None,
                                            ALU.add).then_inc(s_win, 1)
                dve.wait_ge(s_win, 2)
                nc.vector.tensor_copy(R.window_i[:, :], window[0:1, :]).then_inc(s_win, 1)
                nc.vector.memset(R.begins[:, 0:1], 0.0).then_inc(s_win, 1)
                nc.vector.tensor_tensor(R.begins[:, 1:NT], window[0:HW, 1:NT], window[0:HW, 0:NT - 1], ALU.not_equal).then_inc(s_win, 1)

            @block.tensor
            def _(pe):
                pe.wait_ge(s_ch2, 4)
                nc.tensor.matmul(pf[0:NW, 0:1], K.before[0:NW, 0:NW], tiles[:, :], start=True, stop=True).then_inc(s_first, 1)
                pe.wait_ge(s_ch2, 7)
                for q in range(2):
                    nc.tensor.matmul(pw[q][:, 0:NT // 2], K.ones[0:NW, :], reach[:, q * (NT // 2):(q + 1) * (NT // 2)],
                                     start=True, stop=True).then_inc(s_wb, 1)

        with nc.Block() as block:
            if beside:
                @block.gpsimd
                def _(pool):
                    scatter_edges(nc, pool, K, T, c, beside[0], beside[2])

            @block.sync
            def _(sp):
                for ch in range(NCH):
                    b = ch % 2
                    if ch >= 2:
                        sp.wait_ge(s_hot, ch - 1)
                    sp.dma_start(keys[b][:, :], keys_of(ch)).then_inc(s_kin[b], 16)

            @block.vector
            def _(dve):
                for ch in range(NCH):
                    b = ch % 2
                    dve.wait_ge(s_kin[b], 16 * ((NCH + 1 - b) // 2 + ch // 2 + 1))
                    if ch >= 2:
                        dve.wait_ge(s_hit, ch - 1)
                    nc.vector.tensor_scalar(hot[b][:, :], keys[b][:, :], K.part[0:NW, :], None, ALU.is_equal).then_inc(s_hot, 1)
                    dve.wait_ge(s_hot, ch + 1)
                    if ch:
                        dve.wait_ge(s_scan, ch)
                    nc.vector.tensor_tensor_scan(scan[b][:, :], hot[b][:, :], hot[b][:, :],
                                                 scan[1 - b][:, CH * SLICE - 1:CH * SLICE] if ch else carry[:, :],
                                                 ALU.add, ALU.max).then_inc(s_scan, 1)
                    dve.wait_ge(s_scan, ch + 1)
                    if ch >= 2:
                        dve.wait_ge(s_hfree, ch - 1)
                    nc.vector.tensor_tensor(hit[b][:, :], scan[b][:, :], hot[b][:, :], ALU.mult).then_inc(s_hit, 1)
                link = chained(dve, s_ch3)
                dve.wait_ge(s_hfree, NCH)
                link(nc.vector.tensor_scalar(place[:, :], ppos[0:SLICE, 0:NSL], -1.0, None, ALU.add))
                link(nc.vector.tensor_scalar(tile[:, :], place[:, :], -(P - 1) / 2, 1.0 / P, ALU.add, ALU.mult))
                link(nc.vector.tensor_scalar(tile[:, :], tile[:, :], ROUND, None, ALU.add))
                link(nc.vector.tensor_scalar(tile[:, :], tile[:, :], -ROUND, None, ALU.add))
                link(nc.vector.scalar_tensor_tensor(addr[:, :], tile[:, :], -float(P), place[:, :], ALU.mult, ALU.add))
                link(nc.vector.scalar_tensor_tensor(addr[:, :], addr[:, :], float(NT), tile[:, :], ALU.mult, ALU.add))
                link(nc.vector.tensor_copy(addr_i[:, :], addr[:, :]))

            @block.tensor
            def _(pe):
                for ch in range(NCH):
                    pe.wait_ge(s_hit, ch + 1)
                    for q in range(CH):
                        last = nc.tensor.matmul(ppos[0:SLICE, ch * CH + q:ch * CH + q + 1],
                                                hit[ch % 2][:, q * SLICE:(q + 1) * SLICE], K.ones[0:NW, 0:1], start=True, stop=True)
                    last.then_inc(s_hfree, 1)


class Scatter:
    NS = 10
    PASSES = NSL // (2 * NS)

    def __init__(self, c, slots, tag):
        self.slots, self.tag, self.done = slots, tag, 0
        self.pay = c.sb("sc_pay_" + tag, [SLICE, NSL, 4])
        self.addr = c.sb("sc_addr_" + tag, [SLICE, NSL], I32)
        self.idx_s = c.sb("sc_idx_stage_" + tag, [SLICE, 2, self.NS], I32)
        self.pay_s = c.sb("sc_pay_stage_" + tag, [SLICE, 2, self.NS, 4])


def scatter_edges(nc, pool, K, T, c, S, passes):
    NS, lo, tag = S.NS, S.done, f"{S.tag}_{S.done}"
    S.done += passes
    s_i, s_p, s_sc = [[c.sem(f"sc_{n}{b}_{tag}") for b in range(2)] for n in ("idx", "pay", "stored")]
    bound = nc.gpsimd.to_reg(P * NT - 1)

    def half_pass(b, i):
        k0 = i * (2 * NS) + (2 * lo + b - 2) * NS
        nc.gpsimd.tensor_tensor(S.idx_s[:, b, :], S.addr[:, bass.ds(k0, NS)], K.zeros_i[0:SLICE, 0:NS], ALU.add).then_inc(s_i[b], 1)
        nc.gpsimd.tensor_tensor(S.pay_s[:, b, :, :], S.pay[:, bass.ds(k0, NS), :],
                                K.zeros[0:SLICE, 0:NS].unsqueeze(2).to_broadcast([SLICE, NS, 4]), ALU.add).then_inc(s_p[b], 1)
        pool.wait_ge(K.ready, 1)
        pool.wait_ge(s_i[b], i)
        pool.wait_ge(s_p[b], i)
        for q in range(NS):
            nc.gpsimd.indirect_dma_start(
                out=T[S.slots][:, :], out_offset=bass.IndirectOffsetOnAxis(ap=S.idx_s[:, b, q:q + 1].bitcast(U32), axis=0),
                in_=S.pay_s[:, b, q, :], in_offset=None, bounds_check=bound, oob_is_err=False).then_inc(s_sc[b], 16)

    half_pass(0, 1)
    half_pass(1, 1)
    with pool.Fori(2, passes + 1) as i:
        for b in range(2):
            pool.wait_ge(s_sc[b], i * (16 * NS) - 16 * NS)
            half_pass(b, i)
    for b in range(2):
        pool.wait_ge(s_sc[b], 16 * NS * passes)


def finish_scatter(nc, K, T, S):
    if S.done < S.PASSES:
        with ExitStack() as stack:
            c = Ctx(nc, stack)
            with nc.Block() as block:
                @block.gpsimd
                def _(pool):
                    scatter_edges(nc, pool, K, T, c, S, S.PASSES - S.done)


def load_slots(nc, K, T, S, R, tag):
    with ExitStack() as stack:
        c = Ctx(nc, stack)
        got = c.sb("so_slots_" + tag, [P, NT, 4])
        s_got, s_done = c.sem("so_slots_loaded_" + tag), c.sem("so_done_" + tag)
        with nc.Block() as block:
            @block.sync
            def _(sp):
                sp.dma_start(got[:, :, :].rearrange("p j q -> p (j q)"), T[S.slots].rearrange("(s j) q -> s (j q)", s=P)).then_inc(s_got, 16)

            @block.scalar
            def _(act):
                act.wait_ge(s_got, 16)
                for f, into in enumerate([R.index, R.type, R.node]):
                    nc.scalar.copy(into[:, :], got[:, :, f]).then_inc(s_done, 1)


def earlier(b, i, k, n=2):
    return (b - k) % n, i + (b - k) // n


def live(b, i, k, n=2):
    return not isinstance(i, int) or 0 <= n * i + b - k < NG


def windows_of(nc, eng, R, j0):
    _, w = nc.values_load_multi_w_load_instructions(R.window_i[0:1, bass.ds(j0, GROUP)], engines=[eng.engine], min_val=0, max_val=NW - 1,
                                                    skip_runtime_bounds_check_because="the sort writes window numbers, 0 to NW - 1")
    return w


def pipeline(eng, step, n=2, ahead=0):
    def one_pass(i):
        for b in range(n):
            step(b, i)

    passes, peeled = NG // n, -(-3 // n)
    for i in range(peeled):
        one_pass(i)
    with eng.Fori(peeled, passes - ahead) as i:
        one_pass(i)
    for i in range(passes - ahead, passes + peeled):
        one_pass(i)


def edge_logits(nc, K, T, R):
    with ExitStack() as stack:
        c = Ctx(nc, stack)
        RH = NREL * NH
        ER = c.sb("el_er", [WIN, NW, RH])
        idx_s = [c.sb(f"el_idx{b}", [P, GROUP], I32) for b in range(2)]
        part = [c.sb(f"el_part{b}", [P, GROUP, NH]) for b in range(2)]
        hot = [c.sb(f"el_hot{b}", [P, GROUP, WIN]) for b in range(2)]
        typ = [c.sb(f"el_typ{b}", [P, GROUP, NREL]) for b in range(2)]
        hotT = [c.sb(f"el_hot_t{b}", [WIN, GROUP, P]) for b in range(2)]
        own = [c.sb(f"el_own{b}", [P, GROUP, RH]) for b in range(2)]
        er = [c.sb(f"el_er_own{b}", [P, GROUP, NH]) for b in range(2)]
        miss = [c.sb(f"el_miss{b}", [P, GROUP, WIN]) for b in range(2)]
        Xm = [c.sb(f"el_x{b}", [P, GROUP, NH, WIN]) for b in range(2)]
        tmax = c.sb("el_tmax", [HW, NT])
        reset = [c.sb(f"el_reset{d}", [HW, NT]) for d in range(2)]
        run = c.sb("el_run", [HW, NT])
        bank_h = [c.ps(f"el_ph{b}", [WIN, GROUP, P]) for b in range(2)]
        bank_l = [c.ps(f"el_pl{b}", [P, GROUP, RH]) for b in range(2)]
        bank_x = [c.ps(f"el_px{b}", [HW, GROUP, P]) for b in range(2)]
        sems = lambda n: [c.sem(f"el_{n}{b}") for b in range(2)]
        s_er, s_ch = c.sem("el_er_loaded"), c.sem("el_chain")
        staged, arrived = sems("staged"), sems("arrived")
        s_hot, s_typ = sems("hot"), sems("typ")
        s_miss, s_er_own, s_sum, s_x = sems("miss"), sems("er_own"), sems("sum"), sems("xs")
        added, s_turned, s_copied, s_looked, s_xt, s_red = sems("added"), sems("turned"), sems("copied"), sems("looked"), sems("xt"), sems("red")
        s_free = sems("own_read")
        with nc.Block() as block:
            @block.sync
            def _(sp):
                sp.dma_start(ER[:, :, :], T["logit1"].rearrange("(w i r) h -> i w (r h)", i=WIN, r=NREL)).then_inc(s_er, 16)
                sp.wait_ge(s_er, 16)

            @block.gpsimd
            def _(pool):
                bound = nc.gpsimd.to_reg(N_NODES * NREL - 1)
                with pool.Fori(1, NG // 2 + 1) as i:
                    for b in range(2):
                        pool.wait_ge(added[b], i)
                        nc.gpsimd.tensor_tensor(idx_s[b][:, :], R.index[:, bass.ds(i * (2 * GROUP) + (b - 2) * GROUP, GROUP)],
                                                K.zero_i[:, :], ALU.add).then_inc(staged[b], 1)
                        pool.wait_ge(K.ready, 1)
                        pool.wait_ge(staged[b], i)
                        for t in range(GROUP):
                            nc.gpsimd.indirect_dma_start(
                                out=part[b][:, t, :], out_offset=None, in_=T["logit0"][:, :],
                                in_offset=bass.IndirectOffsetOnAxis(ap=idx_s[b][:, t:t + 1].bitcast(U32), axis=0),
                                bounds_check=bound, oob_is_err=False).then_inc(arrived[b], 16)

            @block.vector
            def _(dve):
                for b in range(2):
                    dve.sem_inc(added[b], 1)
                    dve.sem_inc(s_free[b], 1)
                    dve.sem_inc(s_red[b], 1)

                def one_hots(b, i):
                    j0 = i * (2 * GROUP) + b * GROUP
                    dve.wait_ge(s_turned[b], i + 1)
                    nc.vector.tensor_tensor(hot[b][:, :, :], R.node[:, bass.ds(j0, GROUP)].unsqueeze(2).to_broadcast([P, GROUP, WIN]),
                                            K.iota[:, :].unsqueeze(1).to_broadcast([P, GROUP, WIN]), ALU.is_equal).then_inc(s_hot[b], 1)
                    nc.vector.tensor_tensor(typ[b][:, :, :], R.type[:, bass.ds(j0, GROUP)].unsqueeze(2).to_broadcast([P, GROUP, NREL]),
                                            K.iota[:, 0:NREL].unsqueeze(1).to_broadcast([P, GROUP, NREL]), ALU.is_equal).then_inc(s_typ[b], 1)

                def logits(b, i, between):
                    ev = R.ev[:, bass.ds(i * (2 * GROUP) + b * GROUP, GROUP), :]
                    dve.wait_ge(s_looked[b], i + 2)
                    dve.wait_ge(s_typ[b], i + 1)
                    nc.vector.tensor_tensor(own[b][:, :, :].rearrange("p t (r h) -> p t r h", h=NH),
                                            bank_l[b][:, :, :].rearrange("p t (r h) -> p t r h", h=NH),
                                            typ[b][:, :, :].unsqueeze(3).to_broadcast([P, GROUP, NREL, NH]), ALU.mult).then_inc(s_free[b], 1)
                    nc.vector.tensor_scalar(miss[b][:, :, :], hot[b][:, :, :], -1.0, -NEG, ALU.add, ALU.mult).then_inc(s_miss[b], 1)
                    dve.wait_ge(s_free[b], i + 2)
                    nc.vector.tensor_reduce(er[b][:, :, :], own[b][:, :, :].rearrange("p t (r h) -> p t h r", h=NH), AX, ALU.add).then_inc(s_er_own[b], 1)
                    between()
                    dve.wait_ge(arrived[b], i * (16 * GROUP) + 16 * GROUP)
                    dve.wait_ge(s_er_own[b], i + 1)
                    nc.vector.tensor_tensor(er[b][:, :, :], er[b][:, :, :], part[b][:, :, :], ALU.add).then_inc(added[b], 1)
                    dve.wait_ge(added[b], i + 2)
                    nc.vector.scalar_tensor_tensor(ev, er[b][:, :, :], 0.2, er[b][:, :, :], ALU.mult, ALU.max).then_inc(s_sum[b], 1)
                    dve.wait_ge(s_sum[b], i + 1)
                    dve.wait_ge(s_miss[b], i + 1)
                    dve.wait_ge(s_xt[b], i + 1)
                    nc.vector.tensor_tensor(Xm[b][:, :, :, :], miss[b][:, :, :].unsqueeze(2).to_broadcast([P, GROUP, NH, WIN]),
                                            ev.unsqueeze(3).to_broadcast([P, GROUP, NH, WIN]), ALU.add).then_inc(s_x[b], 1)

                def tile_maxima(b, i):
                    dve.wait_ge(s_xt[b], i + 2)
                    nc.vector.tensor_reduce(tmax[:, bass.ds(i * (2 * GROUP) + b * GROUP, GROUP)], bank_x[b][:, :, :],
                                            AX, ALU.max).then_inc(s_red[b], 1)

                def step(b, i):
                    def between():
                        if live(b, i, 2):
                            tile_maxima(*earlier(b, i, 2))

                    if live(b, i, 0):
                        one_hots(b, i)
                    if live(b, i, 1):
                        logits(*earlier(b, i, 1), between)
                    else:
                        between()

                pipeline(dve, step)
                for b in range(2):
                    dve.wait_ge(s_red[b], NG // 2 + 1)
                link = chained(dve, s_ch)
                link(nc.vector.memset(reset[1][:, :], 0.0))
                link(nc.vector.tensor_copy(reset[0][:, :], R.begins[:, :]))
                link(nc.vector.tensor_copy(reset[1][:, 0:NT - 1], reset[0][:, 1:NT]))
                for d in range(2):
                    link(nc.vector.tensor_scalar(reset[d][:, :], reset[d][:, :], NEG, None, ALU.mult))
                link(nc.vector.tensor_tensor_scan(run[:, :], reset[0][:, :], tmax[:, :], NEG, ALU.add, ALU.max))
                link(nc.vector.tensor_tensor_scan(tmax[:, ::-1], reset[1][:, ::-1], run[:, ::-1], NEG, ALU.add, ALU.max))
                link(nc.vector.tensor_scalar(R.negmax[:, :], tmax[:, :], FLOOR, -1.0, ALU.max, ALU.mult))

            @block.tensor
            def _(pe):
                for b in range(2):
                    pe.sem_inc(s_turned[b], 1)
                    pe.sem_inc(s_looked[b], 1)
                    pe.sem_inc(s_xt[b], 1)

                def turn_hot(b, i):
                    pe.wait_ge(s_hot[b], i + 1)
                    pe.wait_ge(s_copied[b], i + 1)
                    for t in range(GROUP):
                        last = nc.tensor.transpose(bank_h[b][:, t, :], hot[b][:, t, :], K.ident[:, :])
                    last.then_inc(s_turned[b], 1)

                def look_up(b, i, w):
                    pe.wait_ge(s_copied[b], i + 2)
                    pe.wait_ge(s_free[b], i + 1)
                    for t in range(GROUP):
                        last = nc.tensor.matmul(bank_l[b][:, t, :], hotT[b][:, t, :],
                                                ER[:, bass.ds(w[t], 1), :].rearrange("i a q -> i (a q)"), start=True, stop=True)
                    last.then_inc(s_looked[b], 1)

                def turn_logits(b, i):
                    pe.wait_ge(s_x[b], i + 1)
                    pe.wait_ge(s_red[b], i + 1)
                    for t in range(GROUP):
                        last = nc.tensor.transpose(bank_x[b][:, t, :], Xm[b][:, t, :, :].rearrange("p h n -> p (h n)"), K.ident[:, :])
                    last.then_inc(s_xt[b], 1)

                def step(b, i):
                    if live(b, i, 1):
                        q, j = earlier(b, i, 1)
                        w = windows_of(nc, nc.tensor, R, j * (2 * GROUP) + q * GROUP)
                        look_up(q, j, w)
                    if live(b, i, 2):
                        turn_logits(*earlier(b, i, 2))
                    if live(b, i, 0):
                        turn_hot(b, i)

                pe.wait_ge(s_er, 16)
                pipeline(pe, step)

            @block.scalar
            def _(act):
                for b in range(2):
                    act.sem_inc(s_copied[b], 1)
                with act.Fori(0, NG // 2) as i:
                    for b in range(2):
                        act.wait_ge(s_turned[b], i + 2)
                        act.wait_ge(s_looked[b], i + 1)
                        nc.scalar.copy(hotT[b][:, :, :], bank_h[b][:, :, :]).then_inc(s_copied[b], 1)


def masked_logits(nc, dve, K, R, i, b, miss, Xm, s_m1, s_m2, s_x, turned):
    j0 = i * (2 * GROUP) + b * GROUP
    nc.vector.tensor_tensor(miss[b][:, :, :], R.node[:, bass.ds(j0, GROUP)].unsqueeze(2).to_broadcast([P, GROUP, WIN]),
                            K.iota[:, :].unsqueeze(1).to_broadcast([P, GROUP, WIN]), ALU.not_equal).then_inc(s_m1[b], 1)
    dve.wait_ge(s_m1[b], i + 1)
    nc.vector.tensor_scalar(miss[b][:, :, :], miss[b][:, :, :], NEG, None, ALU.mult).then_inc(s_m2[b], 1)
    dve.wait_ge(s_m2[b], i + 1)
    dve.wait_ge(turned[b], i + 1)
    nc.vector.tensor_tensor(Xm[b][:, :, :, :], miss[b][:, :, :].unsqueeze(2).to_broadcast([P, GROUP, NH, WIN]),
                            R.ev[:, bass.ds(j0, GROUP), :].unsqueeze(3).to_broadcast([P, GROUP, NH, WIN]),
                            ALU.add).then_inc(s_x[b], 1)


def relation_attention(nc, K, T, R, X):
    with ExitStack() as stack:
        c = Ctx(nc, stack)
        acc = c.sb("ra_acc", [HD, NW, 2 * HW])
        idx_s = [c.sb(f"ra_idx{b}", [P, GROUP], I32) for b in range(2)]
        feat = [c.sb(f"ra_feat{b}", [P, GROUP, D]) for b in range(2)]
        miss = [c.sb(f"ra_miss{b}", [P, GROUP, WIN]) for b in range(2)]
        Xm = [c.sb(f"ra_x{b}", [P, GROUP, NH, WIN]) for b in range(2)]
        prob = [c.sb(f"ra_prob{b}", [HW, GROUP, P]) for b in range(2)]
        A = [c.sb(f"ra_a{b}", [P, GROUP, HW]) for b in range(2)]
        bias = c.sb("ra_bias", [NW, D])
        sems = lambda n: [c.sem(f"ra_{n}{b}") for b in range(2)]
        staged, arrived = sems("staged"), [[c.sem(f"ra_arrived{b}{t}") for t in range(GROUP)] for b in range(2)]
        s_m1, s_m2, s_x, s_t = sems("m1"), sems("m2"), sems("x"), sems("t")
        s_exp = sems("exp")
        s_a, s_ac = sems("a"), sems("ac")
        s_gat = [[c.sem(f"ra_gat{b}{t}") for t in range(GROUP)] for b in range(2)]
        s_acc, s_bias, s_ch = c.sem("ra_acc"), c.sem("ra_bias"), c.sem("ra_ch")
        NP = NG // 2
        with ExitStack() as banks, nc.Block() as block:
            cb = Ctx(nc, banks)
            pt = [cb.ps(f"ra_pt{b}", [HW, GROUP, P]) for b in range(2)]
            pa = [cb.ps(f"ra_pa{b}", [P, 512]) for b in range(2)]
            pg = [[cb.ps(f"ra_pg{b}{q}", [HD, 2, 2 * HW]) for q in range(2)] for b in range(2)]

            @block.sync
            def _(sp):
                sp.dma_start(bias[:, :], spread(T["L0_gnn_h_bias"], NW, D)).then_inc(s_bias, 16)
                sp.wait_ge(s_bias, 16)

            @block.gpsimd
            def _(pool):
                bound = nc.gpsimd.to_reg(N_NODES * NREL - 1)

                def fetch(b, i):
                    nc.gpsimd.tensor_tensor(idx_s[b][:, :], R.index[:, bass.ds(i * (2 * GROUP) + (b - 2) * GROUP, GROUP)],
                                            K.zero_i[:, :], ALU.add).then_inc(staged[b], 1)
                    for t in range(GROUP):
                        pool.wait_ge(K.ready, 1)
                        if t == 0:
                            pool.wait_ge(staged[b], i)
                        pool.wait_ge(s_gat[b][t], i)
                        nc.gpsimd.indirect_dma_start(
                            out=feat[b][:, t, :], out_offset=None, in_=T["feat"][:, :],
                            in_offset=bass.IndirectOffsetOnAxis(ap=idx_s[b][:, t:t + 1].bitcast(U32), axis=0),
                            bounds_check=bound, oob_is_err=False).then_inc(arrived[b][t], 16)

                fetch(0, 1)
                fetch(1, 1)
                with pool.Fori(2, NP + 1) as i:
                    for b in range(2):
                        for t in range(GROUP):
                            pool.wait_ge(arrived[b][t], i * 16 - 16)
                        fetch(b, i)

            @block.tensor
            def _(pe):
                def turn(b, i):
                    pe.wait_ge(s_x[b], i + 1)
                    pe.wait_ge(s_exp[b], i + 1)
                    for t in range(GROUP):
                        last = nc.tensor.transpose(pt[b][:, t, :], Xm[b][:, t, :, :].rearrange("p h n -> p (h n)"), K.ident[:, :])
                    last.then_inc(s_t[b], 1)

                def back(b, i):
                    pe.wait_ge(s_exp[b], i + 2)
                    pe.wait_ge(s_ac[b], i + 1)
                    for t in range(GROUP):
                        last = nc.tensor.matmul(pa[b][:, t * HW:(t + 1) * HW], prob[b][:, t, :], K.ident[0:HW, 0:HW],
                                                start=True, stop=True)
                    last.then_inc(s_a[b], 1)

                def gather(b, i):
                    pe.wait_ge(s_ac[b], i + 2)
                    pe.wait_ge(s_acc, i * (2 * GROUP) + b * GROUP + 1)
                    for t in range(GROUP):
                        pe.wait_ge(arrived[b][t], i * 16 + 16)
                        o = pg[b][t // 2][:, t % 2, :]
                        for h in range(NH):
                            nc.tensor.matmul(o[:, h * WIN:(h + 1) * WIN], feat[b][:, t, h * HD:(h + 1) * HD],
                                             A[b][:, t, h * WIN:(h + 1) * WIN], start=True, stop=True)
                        nc.tensor.matmul(o[:, HW:2 * HW], K.ones[:, 0:HD], A[b][:, t, :], start=True, stop=True).then_inc(s_gat[b][t], 1)

                def step(b, i):
                    if live(b, i, 0):
                        turn(b, i)
                    if live(b, i, 1):
                        back(*earlier(b, i, 1))
                    if live(b, i, 2):
                        gather(*earlier(b, i, 2))

                for b in range(2):
                    pe.sem_inc(s_t[b], 1)
                    for t in range(GROUP):
                        pe.sem_inc(s_gat[b][t], 1)
                pipeline(pe, step)

            @block.scalar
            def _(act):
                for b in range(2):
                    act.sem_inc(s_exp[b], 1)
                    act.sem_inc(s_ac[b], 1)

                def exps(b, i):
                    act.wait_ge(s_t[b], i + 2)
                    for t in range(GROUP):
                        last = nc.scalar.activation(prob[b][:, t, :], pt[b][:, t, :], ACT.Exp,
                                                    bias=R.negmax[:, bass.ds(i * (2 * GROUP) + b * GROUP + t, 1)])
                    last.then_inc(s_exp[b], 1)

                def copy_a(b, i):
                    act.wait_ge(s_a[b], i + 1)
                    act.wait_ge(s_gat[b][GROUP - 1], i + 1)
                    nc.scalar.copy(A[b][:, :, :].rearrange("p t q -> p (t q)"), pa[b][:, 0:GROUP * HW]).then_inc(s_ac[b], 1)

                def step(b, i):
                    if live(b, i, 1):
                        copy_a(*earlier(b, i, 1))
                    if live(b, i, 0):
                        exps(b, i)

                pipeline(act, step)

            @block.vector
            def _(dve):
                nc.vector.memset(acc[:, :, :], 0.0).then_inc(s_acc, 1)
                dve.sem_inc(s_acc, GROUP)

                def windows(b, i):
                    return windows_of(nc, nc.vector, R, i * (2 * GROUP) + b * GROUP)

                def add(b, i, t, w):
                    dve.wait_ge(s_gat[b][t | 1], i + 2)
                    n = i * (2 * GROUP) + b * GROUP + t
                    dve.wait_ge(s_acc, n + GROUP + 1)
                    a = acc[:, bass.ds(w, 1), :]
                    nc.vector.tensor_tensor(a, a, pg[b][t // 2][:, t % 2:t % 2 + 1, :], ALU.add).then_inc(s_acc, 1)

                def mask(b, i):
                    masked_logits(nc, dve, K, R, i, b, miss, Xm, s_m1, s_m2, s_x, s_t)

                def step(b, i):
                    if live(b, i, -1):
                        mask(*earlier(b, i, -1))
                    if live(b, i, 3):
                        w = windows(*earlier(b, i, 3))
                        for t in range(GROUP):
                            add(*earlier(b, i, 3), t, w[t])

                mask(0, 0)
                pipeline(dve, step, ahead=1)
                dve.wait_ge(s_acc, NT + GROUP + 1)
                link = chained(dve, s_ch)
                link(nc.vector.tensor_scalar(acc[:, :, HW:2 * HW], acc[:, :, HW:2 * HW], 1e-30, None, ALU.max))
                link(nc.vector.reciprocal(acc[:, :, HW:2 * HW], acc[:, :, HW:2 * HW]))
                link(nc.vector.tensor_tensor(acc[:, :, 0:HW], acc[:, :, 0:HW], acc[:, :, HW:2 * HW], ALU.mult))

        with ExitStack() as banks, nc.Block() as block:
            cb = Ctx(nc, banks)
            pb = [cb.ps(f"ra_pb{b}", [NW, D]) for b in range(2)]
            s_tb, s_add, s_b = cb.sem("ra_tb"), cb.sem("ra_add"), cb.sem("ra_b")

            @block.tensor
            def _(pe):
                for i in range(WIN):
                    if i >= 2:
                        pe.wait_ge(s_add, i - 1)
                    for h in range(NH):
                        last = nc.tensor.transpose(pb[i % 2][:, h * HD:(h + 1) * HD], acc[:, :, h * WIN + i], K.ident[0:HD, 0:HD])
                    last.then_inc(s_tb, 1)

            @block.vector
            def _(dve):
                nc.vector.tensor_tensor(X[:, :, :], X[:, :, :], bias[:, :].unsqueeze(1).to_broadcast([NW, WIN, D]),
                                        ALU.add).then_inc(s_b, 1)
                dve.wait_ge(s_b, 1)
                for i in range(WIN):
                    dve.wait_ge(s_tb, i + 1)
                    nc.vector.tensor_tensor(X[:, i, :], X[:, i, :], pb[i % 2][:, :], ALU.add).then_inc(s_add, 1)


N_SEL = N_NODES // 2 - 1
HID = 1024
NCK = 3
NCHK = WIN // NCK


def token_weights(nc, K, T, Y, R, S, passes):
    with ExitStack() as stack:
        c = Ctx(nc, stack)
        wr = c.sb("tw_wr", [NW, D])
        br = c.sb("tw_br", [NW, 1])
        prod = c.sb("tw_prod", [NW, WIN, D])
        w = c.sb("tw_w", [NW, WIN])
        every = c.sb("tw_every", [NW, N_NODES])
        larger = c.sb("tw_larger", [NW, 2, N_NODES], BF16)
        above = c.sb("tw_above", [NW, WIN])
        inside = c.sb("tw_inside", [NW, WIN])
        cand = c.sb("tw_cand", [NW, WIN])
        peak = c.sb("tw_peak", [NW, 1])
        peakT = c.sb("tw_peakT", [1, P])
        top = c.sb("tw_top", [1, 1])
        edge = c.sb("tw_edge", [NW, 1])
        tie = c.sb("tw_tie", [NW, WIN])
        order = c.sb("tw_order", [NW, WIN])
        ties = c.sb("tw_ties", [NW, 1])
        before = c.sb("tw_before", [NW, 1])
        room = c.sb("tw_room", [NW, 1])
        p1, p2, p3 = c.ps("tw_p1", [P, 512]), c.ps("tw_p2", [P, 512]), c.ps("tw_p3", [P, 512])
        s_in, s_ch, s_w, s_ws, s_all = c.sem("tw_in"), c.sem("tw_ch"), c.sem("tw_ws"), c.sem("tw_stored"), c.sem("tw_all")
        s_gt, s_peak, s_pt, s_top, s_edge, s_ties, s_bef = [c.sem("tw_s" + n) for n in ("gt", "peak", "pt", "top", "edge", "ties", "bef")]
        with nc.Block() as block:
            @block.sync
            def _(sp):
                sp.dma_start(wr[:, :], spread(T["L0_ffn_wr"].rearrange("d a -> (d a)"), NW, D)).then_inc(s_in, 16)
                sp.dma_start(br[:, :], spread(T["L0_ffn_br"], NW, 1)).then_inc(s_in, 16)
                sp.wait_ge(s_w, 1)
                sp.dma_start(T["order"].rearrange("(w i) -> w i", i=WIN), w[:, :]).then_inc(s_ws, 16)
                sp.wait_ge(s_ws, 16)
                sp.dma_start(every[:, :], spread(T["order"], NW, N_NODES)).then_inc(s_all, 16)

            @block.gpsimd
            def _(pool):
                scatter_edges(nc, pool, K, T, c, S, passes)

            @block.vector
            def _(dve):
                link = chained(dve, s_ch)
                dve.wait_ge(s_in, 32)
                link(nc.vector.tensor_tensor(prod[:, :, :], Y[:, :, :], wr[:, :].unsqueeze(1).to_broadcast([NW, WIN, D]), ALU.mult))
                link(nc.vector.tensor_reduce(w[:, :], prod[:, :, :], AX, ALU.add))
                nc.vector.tensor_scalar(w[:, :], w[:, :], br[:, :], None, ALU.add).then_inc(s_w, 1)
                dve.wait_ge(s_w, 1)
                dve.wait_ge(s_all, 16)
                for i in range(WIN):
                    if i >= 2:
                        dve.wait_ge(s_gt, i - 1)
                    nc.vector.tensor_scalar(larger[:, i % 2, :], every[:, :], w[:, i:i + 1], 0.0, ALU.is_gt, ALU.add,
                                            accum_out=above[:, i:i + 1]).then_inc(s_gt, 1)
                dve.wait_ge(s_gt, WIN)
                link(nc.vector.tensor_scalar(inside[:, :], above[:, :], float(N_SEL), None, ALU.is_lt))
                link(nc.vector.tensor_scalar(cand[:, :], above[:, :], 1.0, None, ALU.add))
                link(nc.vector.tensor_tensor(cand[:, :], cand[:, :], inside[:, :], ALU.mult))
                nc.vector.tensor_reduce(peak[:, :], cand[:, :], AX, ALU.max).then_inc(s_peak, 1)
                dve.wait_ge(s_pt, 1)
                link(nc.vector.tensor_copy(peakT[:, 0:NW], p1[0:1, 0:NW]))
                nc.vector.tensor_reduce(top[:, :], peakT[:, 0:NW], AX, ALU.max).then_inc(s_top, 1)
                dve.wait_ge(s_edge, 1)
                link(nc.vector.tensor_scalar(edge[:, :], p2[0:NW, 0:1], -1.0, None, ALU.add))
                link(nc.vector.tensor_scalar(tie[:, :], above[:, :], edge[:, :], None, ALU.is_equal))
                nc.vector.tensor_reduce(ties[:, :], tie[:, :], AX, ALU.add).then_inc(s_ties, 1)
                dve.wait_ge(s_bef, 1)
                link(nc.vector.tensor_copy(before[:, :], p3[0:NW, 0:1]))
                link(nc.vector.tensor_tensor_scan(order[:, :], tie[:, :], tie[:, :], before[:, :], ALU.add, ALU.max))
                link(nc.vector.tensor_scalar(room[:, :], edge[:, :], -1.0, float(N_SEL), ALU.mult, ALU.add))
                link(nc.vector.tensor_scalar(order[:, :], order[:, :], room[:, :], None, ALU.is_le))
                link(nc.vector.tensor_tensor(order[:, :], order[:, :], tie[:, :], ALU.mult))
                link(nc.vector.tensor_scalar(inside[:, :], above[:, :], edge[:, :], None, ALU.is_lt))
                link(nc.vector.tensor_tensor(inside[:, :], inside[:, :], order[:, :], ALU.add))
                link(nc.vector.tensor_tensor(R.gate[:, :], inside[:, :], w[:, :], ALU.mult))

            @block.tensor
            def _(pe):
                pe.wait_ge(s_peak, 1)
                nc.tensor.transpose(p1[0:1, 0:NW], peak[:, :], K.ident[0:NW, 0:NW]).then_inc(s_pt, 1)
                pe.wait_ge(s_top, 1)
                nc.tensor.matmul(p2[0:NW, 0:1], K.ones[0:1, 0:NW], top[:, :], start=True, stop=True).then_inc(s_edge, 1)
                pe.wait_ge(s_ties, 1)
                nc.tensor.matmul(p3[0:NW, 0:1], K.before[0:NW, 0:NW], ties[:, :], start=True, stop=True).then_inc(s_bef, 1)


def routed_ffn(nc, K, T, X, Y, YT, R, S, passes):
    with ExitStack() as stack:
        c = Ctx(nc, stack)
        NH1 = HID // P
        w1 = c.sb("rt_w1", [P, KC, HID])
        w2 = c.sb("rt_w2", [P, NH1, D])
        b1 = c.sb("rt_b1", [P, NH1])
        b2 = c.sb("rt_b2", [NW, D])
        H = [c.sb(f"rt_h{b}", [P, NH1, NCK * NW]) for b in range(2)]
        y = [c.sb(f"rt_y{b}", [NW, D]) for b in range(2)]
        pu = [c.ps(f"rt_pu{b}", [P, 512]) for b in range(3)]
        pd = [c.ps(f"rt_pd{b}", [P, 512]) for b in range(2)]
        s_in, s_u, s_h, s_d, s_y, s_x, s_res = [c.sem("rt_s" + n) for n in ("in", "u", "h", "d", "y", "x", "res")]
        with nc.Block() as block:
            @block.sync
            def _(sp):
                sp.dma_start(w1[:, :, :], T["L0_ffn_w1"].rearrange("(k p) n -> p k n", p=P)).then_inc(s_in, 16)
                sp.dma_start(w2[:, :, :], T["L0_ffn_w2"].rearrange("(k p) n -> p k n", p=P)).then_inc(s_in, 16)
                sp.dma_start(b1[:, :], T["L0_ffn_b1"].rearrange("(k p) -> p k", p=P)).then_inc(s_in, 16)
                sp.dma_start(b2[:, :], spread(T["L0_ffn_b2"], NW, D)).then_inc(s_in, 16)

            @block.gpsimd
            def _(pool):
                scatter_edges(nc, pool, K, T, c, S, passes)

            @block.tensor
            def _(pe):
                pe.wait_ge(s_in, 64)

                def up(ck):
                    for m in range(NH1):
                        n = ck * NH1 + m
                        if n >= 3:
                            pe.wait_ge(s_h, n - 2)
                        for k in range(KC):
                            last = nc.tensor.matmul(pu[n % 3][:, 0:NCK * NW], w1[:, k, m * P:(m + 1) * P],
                                                    YT[:, k, ck * NCK:(ck + 1) * NCK, :].rearrange("p a w -> p (a w)"),
                                                    start=k == 0, stop=k == KC - 1)
                        last.then_inc(s_u, 1)

                def down(ck):
                    pe.wait_ge(s_h, (ck + 1) * NH1)
                    for a in range(NCK):
                        i = ck * NCK + a
                        if i >= 2:
                            pe.wait_ge(s_y, i - 1)
                        for m in range(NH1):
                            last = nc.tensor.matmul(pd[i % 2][0:NW, 0:D], H[ck % 2][:, m, a * NW:(a + 1) * NW], w2[:, m, :],
                                                    start=m == 0, stop=m == NH1 - 1)
                        last.then_inc(s_d, 1)

                up(0)
                for ck in range(1, NCHK):
                    up(ck)
                    down(ck - 1)
                down(NCHK - 1)

            @block.scalar
            def _(act):
                act.wait_ge(s_in, 64)
                for n in range(NCHK * NH1):
                    ck, m = divmod(n, NH1)
                    act.wait_ge(s_u, n + 1)
                    if m == 0 and ck >= 2:
                        act.wait_ge(s_d, (ck - 1) * NCK)
                    nc.scalar.activation(H[ck % 2][:, m, :], pu[n % 3][:, 0:NCK * NW], ACT.Gelu_apprx_tanh,
                                         bias=b1[:, m:m + 1]).then_inc(s_h, 1)

            @block.vector
            def _(dve):
                dve.wait_ge(s_in, 64)
                nc.vector.tensor_tensor(X[:, :, :], X[:, :, :], Y[:, :, :], ALU.add).then_inc(s_res, 1)
                dve.wait_ge(s_res, 1)
                for i in range(WIN):
                    dve.wait_ge(s_d, i + 1)
                    if i >= 2:
                        dve.wait_ge(s_x, i - 1)
                    nc.vector.tensor_tensor(y[i % 2][:, :], pd[i % 2][0:NW, 0:D], b2[:, :], ALU.add).then_inc(s_y, 1)
                    dve.wait_ge(s_y, i + 1)
                    nc.vector.scalar_tensor_tensor(X[:, i, :], y[i % 2][:, :], R.gate[:, i:i + 1], X[:, i, :],
                                                   ALU.mult, ALU.add).then_inc(s_x, 1)


HO = 2 * D


def load_transposed(nc, K, T, c, tag, items):
    with ExitStack() as stack, nc.Block() as block:
        s = Ctx(nc, stack)
        raw = [s.sb(f"lt_raw{q}_{tag}", [P, KC, D]) for q in range(len(items))]
        bank = [s.ps(f"lt_ps{b}_{tag}", [P, P]) for b in range(2)]
        s_in, s_t, s_c = s.sem(f"lt_in_{tag}"), s.sem(f"lt_t_{tag}"), s.sem(f"lt_c_{tag}")
        pieces = [(q, k, o) for q, (_, _, wide) in enumerate(items) for k in range(D // wide) for o in range(KC)]

        @block.sync
        def _(sp):
            for q, (src, _, _) in enumerate(items):
                sp.dma_start(raw[q][:, :, :], src.rearrange("(o p) n -> p o n", p=P)).then_inc(s_in, 16)

        @block.tensor
        def _(pe):
            pe.wait_ge(s_in, 16 * len(items))
            for n, (q, k, o) in enumerate(pieces):
                wide = items[q][2]
                if n >= 2:
                    pe.wait_ge(s_c, n - 1)
                nc.tensor.transpose(bank[n % 2][0:wide, :], raw[q][:, o, k * wide:(k + 1) * wide], K.ident[:, :]).then_inc(s_t, 1)

        @block.vector
        def _(dve):
            for n, (q, k, o) in enumerate(pieces):
                _, dst, wide = items[q]
                dve.wait_ge(s_t, n + 1)
                nc.vector.tensor_copy(dst[0:wide, k, o * P:(o + 1) * P], bank[n % 2][0:wide, :]).then_inc(s_c, 1)


def node_linear(nc, K, HT, W, bias, dst, tag, func=None, add=None):
    with ExitStack() as stack, nc.Block() as block:
        c = Ctx(nc, stack)
        bank = [c.ps(f"nl_ps{b}_{tag}", [P, 512]) for b in range(2)]
        s_m, s_v, s_r = c.sem(f"nl_m_{tag}"), c.sem(f"nl_v_{tag}"), c.sem(f"nl_r_{tag}")

        @block.tensor
        def _(pe):
            for i in range(WIN):
                if i >= 2:
                    pe.wait_ge(s_v, i - 1)
                for k in range(KC):
                    last = nc.tensor.matmul(bank[i % 2][0:NW, 0:D], HT[:, k, i, :], W[:, k, :], start=k == 0, stop=k == KC - 1)
                last.then_inc(s_m, 1)

        @block.vector
        def _(dve):
            for i in range(WIN):
                dve.wait_ge(s_m, i + 1)
                nc.vector.tensor_tensor(dst[:, i, :], bank[i % 2][0:NW, 0:D], bias[:, :], ALU.add).then_inc(s_v, 1)
            if func == "relu":
                dve.wait_ge(s_v, WIN)
                nc.vector.tensor_scalar(dst[:, :, :], dst[:, :, :], 0.0, None, ALU.max).then_inc(s_r, 1)
            if add is not None:
                dve.wait_ge(s_v, WIN)
                nc.vector.tensor_tensor(add[:, :, :], add[:, :, :], dst[:, :, :], ALU.add).then_inc(s_r, 1)


def load_rows(nc, T, tag, items):
    with ExitStack() as stack, nc.Block() as block:
        s_in = Ctx(nc, stack).sem(f"lr_in_{tag}")

        @block.sync
        def _(sp):
            for dst, src in items:
                sp.dma_start(dst, src).then_inc(s_in, 16)
            sp.wait_ge(s_in, 16 * len(items))


def project_qkv(nc, K, T, HT, QT, Wq, Wkv, bq, bkv):
    with ExitStack() as stack, nc.Block() as block:
        c = Ctx(nc, stack)
        rows = c.sb("pq_rows", [NW, 2, HO])
        bank = [c.ps(f"pq_ps{b}", [P, 512]) for b in range(2)]
        bq_ps = [c.ps(f"pq_q{b}", [P, 512]) for b in range(2)]
        s_kv, s_row, s_q, s_qc = c.sem("pq_kv"), c.sem("pq_row"), c.sem("pq_sq"), c.sem("pq_qc")
        s_st = [c.sem(f"pq_st{b}") for b in range(2)]
        qs = [(h, ck) for h in range(NH) for ck in range(NCHK)]

        @block.tensor
        def _(pe):
            for n in range(max(WIN, len(qs))):
                if n < WIN:
                    if n >= 2:
                        pe.wait_ge(s_row, n - 1)
                    for k in range(KC):
                        last = nc.tensor.matmul(bank[n % 2][0:NW, :], HT[:, k, n, :], Wkv[:, k, :], start=k == 0, stop=k == KC - 1)
                    last.then_inc(s_kv, 1)
                if n < len(qs):
                    h, ck = qs[n]
                    if n >= 2:
                        pe.wait_ge(s_qc, n - 1)
                    for k in range(KC):
                        last = nc.tensor.matmul(bq_ps[n % 2][0:HD, 0:NCK * NW], Wq[:, k, h * HD:(h + 1) * HD],
                                                HT[:, k, ck * NCK:(ck + 1) * NCK, :].rearrange("p a w -> p (a w)"),
                                                start=k == 0, stop=k == KC - 1)
                    last.then_inc(s_q, 1)

        @block.vector
        def _(dve):
            for i in range(WIN):
                dve.wait_ge(s_kv, i + 1)
                if i >= 2:
                    dve.wait_ge(s_st[i % 2], 16 * (i // 2))
                nc.vector.tensor_tensor(rows[:, i % 2, :], bank[i % 2][0:NW, :], bkv[:, :], ALU.add).then_inc(s_row, 1)

        @block.scalar
        def _(act):
            for n, (h, ck) in enumerate(qs):
                act.wait_ge(s_q, n + 1)
                nc.scalar.activation(QT[:, :, h, ck * NCK:(ck + 1) * NCK].rearrange("p w i -> p i w"),
                                     bq_ps[n % 2][0:HD, 0:NCK * NW].rearrange("p (i w) -> p i w", w=NW), ACT.Identity,
                                     bias=bq[:, h:h + 1]).then_inc(s_qc, 1)

        @block.sync
        def _(sp):
            table = T["kv"].rearrange("(w i) d -> w i d", i=WIN)
            for i in range(WIN):
                sp.wait_ge(s_row, i + 1)
                sp.dma_start(table[:, i, :], rows[:, i % 2, :]).then_inc(s_st[i % 2], 16)
            for b in range(2):
                sp.wait_ge(s_st[b], 16 * (WIN // 2))


NTY = 3
AR = HD + NTY


def head_attention(nc, K, T, R, QT, acc):
    with ExitStack() as stack, nc.Block() as block:
        c = Ctx(nc, stack)
        S16 = NH * NH
        DVE_TILES = 2
        NB = 3
        idx_s = [c.sb(f"ha_idx{b}", [P, GROUP], I32) for b in range(NB)]
        kv = [c.sb(f"ha_kv{b}", [P, GROUP, HO]) for b in range(NB)]
        kT = [c.sb(f"ha_kt{q}", [HD, NH, P]) for q in range(2)]
        hot = [c.sb(f"ha_hot{b}", [P, GROUP, WIN], BF16) for b in range(NB)]
        typ = [c.sb(f"ha_typ{b}", [P, GROUP, AR], BF16) for b in range(NB)]
        qw = c.sb("ha_qw", [HD, GROUP, HW])
        none = c.sb("ha_none", [P, AR], BF16)
        M = [c.sb(f"ha_m{q}", [P, S16, WIN]) for q in range(2)]
        s16 = [c.sb(f"ha_s{b}", [P, GROUP, S16]) for b in range(NB)]
        mx = [c.sb(f"ha_mx{b}", [P, GROUP, NH]) for b in range(NB)]
        A = c.sb("ha_a", [P, GROUP, S16, WIN])
        pk = [c.ps(f"ha_pk{q}", [P, 2, P]) for q in range(2)]
        pS = [c.ps(f"ha_ps{t}", [P, 512]) for t in range(GROUP)]
        pg = c.ps("ha_pg", [AR, GROUP, HW])
        sems = lambda n: [c.sem(f"ha_{n}{b}") for b in range(NB)]
        staged, arrived = sems("staged"), [[c.sem(f"ha_arr{b}{t}") for t in range(GROUP)] for b in range(NB)]
        s_kt = c.sem("ha_turned")
        s_kc = c.sem("ha_kcopied")
        s_sc = c.sem("ha_scores")
        s_sel = c.sem("ha_selected")
        s_red = c.sem("ha_reduced")
        s_hot, s_typ, s_mx, s_sub, s_exp = sems("hoted"), sems("typed"), sems("max"), sems("sub"), sems("exp")
        s_sum, s_rec, s_nrm, s_A = sems("sum"), sems("rec"), sems("norm"), sems("As")
        s_turned = sems("group_turned")
        s_gat = [[c.sem(f"ha_gat{b}{t}") for t in range(GROUP)] for b in range(NB)]
        s_acc = c.sem("ha_acc")
        s_z = c.sem("ha_zero")
        s_q = sems("queries")
        s_Ap = sems("As_pool")
        NP = NG // NB
        TB = NB * GROUP

        def spread_weights(eng, b, t):
            return eng.tensor_tensor(A[:, t, :, :], s16[b][:, t, :].unsqueeze(2).to_broadcast([P, S16, WIN]),
                                     hot[b][:, t, :].unsqueeze(1).to_broadcast([P, S16, WIN]), ALU.mult)

        @block.gpsimd
        def _(pool):
            bound = nc.gpsimd.to_reg(N_NODES - 1)

            def fetch(b, i):
                pool.wait_ge(s_turned[b], i)
                nc.gpsimd.tensor_tensor(idx_s[b][:, :], R.index[:, bass.ds(i * TB + (b - NB) * GROUP, GROUP)],
                                        K.zero_i[:, :], ALU.add).then_inc(staged[b], 1)
                for t in range(GROUP):
                    pool.wait_ge(K.ready, 1)
                    if t == 0:
                        pool.wait_ge(staged[b], i)
                    pool.wait_ge(s_gat[b][t], i)
                    nc.gpsimd.indirect_dma_start(
                        out=kv[b][:, t, :], out_offset=None, in_=T["kv"][:, :],
                        in_offset=bass.IndirectOffsetOnAxis(ap=idx_s[b][:, t:t + 1].bitcast(U32), axis=0),
                        bounds_check=bound, oob_is_err=False).then_inc(arrived[b][t], 16)

            def spread_out(b, i):
                pool.wait_ge(s_nrm[b], i + 1)
                for t in range(DVE_TILES, GROUP):
                    spread_weights(nc.gpsimd, b, t).then_inc(s_Ap[b], 1)

            for b in range(NB):
                fetch(b, 1)
                if b >= 2:
                    spread_out(b - 2, 0)
            with pool.Fori(2, NP + 1) as i:
                for b in range(NB):
                    fetch(b, i)
                    q, j = earlier(b, i, 2, NB)
                    spread_out(q, j - 1)
            for b in range(NB - 2, NB):
                pool.wait_ge(s_gat[b - 1][GROUP - 1], NP + 1)
                spread_out(b, NP - 1)

        @block.tensor
        def _(pe):
            for b in range(NB):
                pe.sem_inc(s_turned[b], 1)
                for t in range(GROUP):
                    pe.sem_inc(s_gat[b][t], 1)

            def turn(b, i, t):
                n = i * TB + b * GROUP + t
                pe.wait_ge(arrived[b][t], i * 16 + 16)
                pe.wait_ge(s_kc, n + 1)
                for k in range(2):
                    last = nc.tensor.transpose(pk[t % 2][:, k, :], kv[b][:, t, k * P:(k + 1) * P], K.ident[:, :])
                    if k == 0 and t == GROUP - 1:
                        last.then_inc(s_turned[b], 1)
                last.then_inc(s_kt, 1)

            def score(b, i, t):
                n = i * TB + b * GROUP + t
                pe.wait_ge(s_kc, n + 3)
                pe.wait_ge(s_sel, n + 1)
                for g in range(NH):
                    last = nc.tensor.matmul(pS[t][:, g * HW:(g + 1) * HW], kT[t % 2][:, g, :], qw[:, t, :],
                                            start=True, stop=True)
                last.then_inc(s_sc, 1)

            def gather(b, i, t):
                if t < DVE_TILES:
                    pe.wait_ge(s_A[b], i * DVE_TILES + t + 1)
                else:
                    pe.wait_ge(s_Ap[b], i * (GROUP - DVE_TILES) + t - DVE_TILES + 1)
                pe.wait_ge(s_acc, i * TB + (b + 1) * GROUP + 1)
                o = pg[:, t, :]
                at_node = hot[b][:, t, :].unsqueeze(1).to_broadcast([P, NH, WIN])
                nc.tensor.matmul(o, typ[b][:, t, :], at_node, start=True, stop=False)
                for g in range(NH):
                    nc.tensor.matmul(o[0:HD, :], kv[b][:, t, D + g * HD:D + (g + 1) * HD],
                                     A[:, t, g * NH:(g + 1) * NH, :].rearrange("p h n -> p (h n)"),
                                     start=False, stop=False)
                nc.tensor.matmul(o, none[:, :], at_node, start=False, stop=True).then_inc(s_gat[b][t], 1)

            def step(b, i):
                if live(b, i, 2, NB):
                    for t in range(GROUP):
                        gather(*earlier(b, i, 2, NB), t)
                if live(b, i, 0, NB):
                    turn(b, i, 0)
                    pe.wait_ge(s_q[b], i + 1)
                    for t in range(GROUP):
                        if t + 1 < GROUP:
                            turn(b, i, t + 1)
                        score(b, i, t)

            pipeline(pe, step, NB)

        @block.scalar
        def _(act):
            act.sem_inc(s_kc, 2)
            act.sem_inc(s_sc, 2)

            def stage_queries(b, i):
                w = windows_of(nc, nc.scalar, R, i * TB + b * GROUP)
                act.wait_ge(s_sc, i * TB + b * GROUP + 2)
                for t in range(GROUP):
                    last = nc.scalar.copy(qw[:, t, :], QT[:, bass.ds(w[t], 1), :, :].rearrange("p a h n -> p (a h n)"))
                last.then_inc(s_q[b], 1)

            def exps(b, i):
                act.wait_ge(s_sub[b], i + 1)
                nc.scalar.activation(s16[b][:, :, :], s16[b][:, :, :], ACT.Exp, scale=HD ** -0.5).then_inc(s_exp[b], 1)

            def step(b, i):
                for t in range(GROUP):
                    if live(b, i, 0, NB):
                        n = i * TB + b * GROUP + t
                        act.wait_ge(s_kt, n + 1)
                        act.wait_ge(s_sc, n + 1)
                        nc.scalar.copy(kT[t % 2][:, 0::2, :], pk[t % 2][0:HD, :, :])
                        nc.scalar.copy(kT[t % 2][:, 1::2, :], pk[t % 2][HD:P, :, :]).then_inc(s_kc, 1)
                    if t == 1 and live(b, i, 1, NB):
                        exps(*earlier(b, i, 1, NB))
                if live(b, i, -1, NB):
                    stage_queries(*earlier(b, i, -1, NB))

            stage_queries(0, 0)
            pipeline(act, step, NB, ahead=1)

        @block.vector
        def _(dve):
            nc.vector.memset(acc[:, :, :], 0.0).then_inc(s_acc, 1)
            nc.vector.memset(none[:, :], 0.0).then_inc(s_z, 1)
            for b in range(NB):
                nc.vector.memset(typ[b][:, :, :], 0.0).then_inc(s_z, 1)
            dve.sem_inc(s_acc, GROUP)
            dve.sem_inc(s_sel, GROUP)
            dve.wait_ge(s_z, 1 + NB)

            def select(b, i, between, load_windows):
                j0 = i * TB + b * GROUP
                dve.wait_ge(s_gat[b][GROUP - 1], i + 1)
                nc.vector.tensor_tensor(hot[b][:, :, :], R.node[:, bass.ds(j0, GROUP)].unsqueeze(2).to_broadcast([P, GROUP, WIN]),
                                        K.iota[:, :].unsqueeze(1).to_broadcast([P, GROUP, WIN]), ALU.is_equal).then_inc(s_hot[b], 1)
                nc.vector.tensor_tensor(typ[b][:, :, HD:AR], R.type[:, bass.ds(j0, GROUP)].unsqueeze(2).to_broadcast([P, GROUP, NTY]),
                                        K.iota[:, 0:NTY].unsqueeze(1).to_broadcast([P, GROUP, NTY]), ALU.is_equal).then_inc(s_typ[b], 1)
                dve.wait_ge(s_hot[b], i + 1)

                def mask(t):
                    dve.wait_ge(s_sc, j0 + t + 3)
                    if t >= 2:
                        dve.wait_ge(s_red, j0 + t - 1)
                    nc.vector.tensor_tensor(M[t % 2][:, :, :], pS[t][:, 0:S16 * WIN].rearrange("p (q n) -> p q n", n=WIN),
                                            hot[b][:, t, :].unsqueeze(1).to_broadcast([P, S16, WIN]), ALU.mult).then_inc(s_sel, 1)

                def total(t):
                    dve.wait_ge(s_sel, j0 + t + GROUP + 1)
                    nc.vector.tensor_reduce(s16[b][:, t, :], M[t % 2][:, :, :], AX, ALU.add).then_inc(s_red, 1)

                for t in range(0, GROUP, 2):
                    mask(t)
                    mask(t + 1)
                    if t == 0:
                        load_windows()
                    total(t)
                    total(t + 1)
                between()
                dve.wait_ge(s_red, j0 + GROUP)
                nc.vector.tensor_reduce(mx[b][:, :, :], s16[b][:, :, :].rearrange("p t (g h) -> p t h g", h=NH), AX, ALU.max).then_inc(s_mx[b], 1)
                between()
                dve.wait_ge(s_mx[b], i + 1)
                q = s16[b][:, :, :].rearrange("p t (g h) -> p t g h", h=NH)
                nc.vector.tensor_tensor(q, q, mx[b][:, :, :].unsqueeze(2).to_broadcast([P, GROUP, NH, NH]), ALU.subtract).then_inc(s_sub[b], 1)

            def weights(b, i, between):
                between()
                dve.wait_ge(s_exp[b], i + 1)
                nc.vector.tensor_reduce(mx[b][:, :, :], s16[b][:, :, :].rearrange("p t (g h) -> p t h g", h=NH), AX, ALU.add).then_inc(s_sum[b], 1)
                between()
                dve.wait_ge(s_sum[b], i + 1)
                nc.vector.reciprocal(mx[b][:, :, :], mx[b][:, :, :]).then_inc(s_rec[b], 1)
                dve.wait_ge(s_rec[b], i + 1)
                q = s16[b][:, :, :].rearrange("p t (g h) -> p t g h", h=NH)
                nc.vector.tensor_tensor(q, q, mx[b][:, :, :].unsqueeze(2).to_broadcast([P, GROUP, NH, NH]), ALU.mult).then_inc(s_nrm[b], 1)
                dve.wait_ge(s_nrm[b], i + 1)

            def add(b, i, t, w):
                n = i * TB + b * GROUP + t
                dve.wait_ge(s_gat[b][GROUP - 1], i + 2)
                dve.wait_ge(s_acc, n + GROUP + 1)
                a = acc[:, bass.ds(w, 1), :]
                nc.vector.tensor_tensor(a, a, pg[:, t:t + 1, :], ALU.add).then_inc(s_acc, 1)

            def step(b, i):
                adds = list(range(GROUP)) if live(b, i, 1, NB) else []
                w = []

                def load_windows():
                    if live(b, i, 1, NB):
                        q, j = earlier(b, i, 1, NB)
                        w.extend(windows_of(nc, nc.vector, R, j * TB + q * GROUP))

                def between():
                    if adds:
                        t = adds.pop(0)
                        add(*earlier(b, i, 1, NB), t, w[t])

                if live(b, i, 0, NB):
                    select(b, i, between, load_windows)
                    weights(b, i, between)
                else:
                    load_windows()
                while adds:
                    between()
                if live(b, i, 0, NB):
                    for t in range(DVE_TILES):
                        spread_weights(nc.vector, b, t).then_inc(s_A[b], 1)

            pipeline(dve, step, NB)
            dve.wait_ge(s_acc, NT + GROUP + 1)


def node_update(nc, K, acc, Wo, H, tag):
    with ExitStack() as stack, nc.Block() as block:
        c = Ctx(nc, stack)
        bank = [c.ps(f"nu_ps{b}_{tag}", [P, 512]) for b in range(2)]
        s_m, s_v = c.sem(f"nu_m_{tag}"), c.sem(f"nu_v_{tag}")

        @block.tensor
        def _(pe):
            for i in range(WIN):
                if i >= 2:
                    pe.wait_ge(s_v, i - 1)
                for h in range(NH):
                    rows = AR if h == 0 else HD
                    last = nc.tensor.matmul(bank[i % 2][0:NW, 0:D], acc[0:rows, :, h * WIN + i], Wo[0:rows, h, :],
                                            start=h == 0, stop=h == NH - 1)
                last.then_inc(s_m, 1)

        @block.vector
        def _(dve):
            for i in range(WIN):
                dve.wait_ge(s_m, i + 1)
                nc.vector.tensor_tensor(H[:, i, :], H[:, i, :], bank[i % 2][0:NW, 0:D], ALU.add).then_inc(s_v, 1)


def edge_type_rows(nc, K, T, l, Wo, tag):
    with ExitStack() as stack, nc.Block() as block:
        c = Ctx(nc, stack)
        E = c.sb("et_e_" + tag, [NTY, D])
        bo = c.sb("et_bo_" + tag, [NTY, D])
        ET = c.sb("et_et_" + tag, [HD, NH, NTY])
        ew = c.sb("et_ew_" + tag, [NTY, D])
        pe_t = c.ps("et_pt_" + tag, [HD, NH, NTY])
        pe_o = c.ps("et_po_" + tag, [NTY, D])
        s_in, s_t, s_c, s_m, s_o, s_w = [c.sem(f"et_{n}_{tag}") for n in ("in", "t", "c", "m", "o", "w")]

        @block.sync
        def _(sp):
            sp.dma_start(E[:, :], T["L1_gnn_Eemb"][l]).then_inc(s_in, 16)
            sp.dma_start(bo[:, :], spread(T["L1_gnn_bo"][l], NTY, D)).then_inc(s_in, 16)
            sp.wait_ge(s_o, 1)
            sp.dma_start(Wo[HD:AR, 0, :], ew[:, :]).then_inc(s_w, 16)
            sp.wait_ge(s_w, 16)

        @block.tensor
        def _(pe):
            pe.wait_ge(s_in, 32)
            for h in range(NH):
                last = nc.tensor.transpose(pe_t[:, h, :], E[:, h * HD:(h + 1) * HD], K.ident[0:NTY, 0:NTY])
            last.then_inc(s_t, 1)
            pe.wait_ge(s_c, 1)
            for h in range(NH):
                last = nc.tensor.matmul(pe_o[:, :], ET[:, h, :], Wo[0:HD, h, :], start=h == 0, stop=h == NH - 1)
            last.then_inc(s_m, 1)

        @block.vector
        def _(dve):
            dve.wait_ge(s_t, 1)
            nc.vector.tensor_copy(ET[:, :, :], pe_t[:, :, :]).then_inc(s_c, 1)
            dve.wait_ge(s_m, 1)
            nc.vector.tensor_tensor(ew[:, :], pe_o[:, :], bo[:, :], ALU.add).then_inc(s_o, 1)


def scale_relu(nc, H, g, b, tag):
    with ExitStack() as stack, nc.Block() as block:
        s_ch = Ctx(nc, stack).sem("sr_ch_" + tag)

        @block.vector
        def _(dve):
            link = chained(dve, s_ch)
            link(nc.vector.tensor_tensor(H[:, :, :], H[:, :, :], g[:, :].unsqueeze(1).to_broadcast([NW, WIN, D]), ALU.mult))
            link(nc.vector.tensor_tensor(H[:, :, :], H[:, :, :], b[:, :].unsqueeze(1).to_broadcast([NW, WIN, D]), ALU.add))
            link(nc.vector.tensor_scalar(H[:, :, :], H[:, :, :], 0.0, None, ALU.max))


def message_layers(nc, K, T, R, H):
    for l in range(3):
        tag = f"l{l}"
        with ExitStack() as stack:
            c = Ctx(nc, stack)
            QT = c.sb("qt_" + tag, [HD, NW, NH, WIN])
            Wo = c.sb("wo_" + tag, [AR, NH, D])
            with ExitStack() as inner:
                ci = Ctx(nc, inner)
                HT = ci.sb("ht_" + tag, [P, KC, WIN, NW])
                Wq = ci.sb("wq_" + tag, [P, KC, D])
                Wkv = ci.sb("wkv_" + tag, [P, KC, HO])
                bq = ci.sb("bq_" + tag, [HD, NH])
                bkv = ci.sb("bkv_" + tag, [NW, HO])
                load_rows(nc, T, tag, [(bkv[:, 0:D], spread(T["L1_gnn_bk"][l], NW, D)), (bkv[:, D:HO], spread(T["L1_gnn_bv"][l], NW, D)),
                                       (bq[:, :], T["L1_gnn_bq"][l].rearrange("(h d) -> d h", h=NH))])
                load_transposed(nc, K, T, ci, tag, [(T["L1_gnn_Wq"][l], Wq, P), (T["L1_gnn_Wk"][l], Wkv[:, :, 0:D], P),
                                                    (T["L1_gnn_Wv"][l], Wkv[:, :, D:HO], P), (T["L1_gnn_Wo"][l], Wo, HD)])
                edge_type_rows(nc, K, T, l, Wo, tag)
                transpose_nodes(nc, K, H, HT, tag)
                project_qkv(nc, K, T, HT, QT, Wq, Wkv, bq, bkv)
            acc = c.sb("acc_" + tag, [AR, NW, HW])
            head_attention(nc, K, T, R, QT, acc)
            node_update(nc, K, acc, Wo, H, tag)
        layernorm(nc, K, H, H, tag)
        with ExitStack() as stack:
            c = Ctx(nc, stack)
            g, b = c.sb("ln_gain_" + tag, [NW, D]), c.sb("ln_bias_" + tag, [NW, D])
            load_rows(nc, T, tag + "b", [(g[:, :], spread(T["L1_gnn_ln_g"][l], NW, D)), (b[:, :], spread(T["L1_gnn_ln_b"][l], NW, D))])
            scale_relu(nc, H, g, b, tag)


NE = 4
EH1, EH2 = 128, 64


def expert_gates(nc, K, T, YT, R):
    with ExitStack() as stack, nc.Block() as block:
        c = Ctx(nc, stack)
        gW, gb = c.sb("eg_w", [P, KC, NE]), c.sb("eg_b", [NW, NE])
        G, cmp = c.sb("eg_g", [NW, WIN, NE]), c.sb("eg_cmp", [NW, WIN, NE])
        rank, red = c.sb("eg_rank", [NW, WIN, NE]), c.sb("eg_red", [NW, WIN])
        pg = c.ps("eg_ps", [NW, WIN, NE])
        s_in, s_m, s_ch, s_e, s_x = [c.sem("eg_s" + n) for n in ("in", "m", "ch", "e", "x")]
        wide = red[:, :].unsqueeze(2).to_broadcast([NW, WIN, NE])

        @block.sync
        def _(sp):
            sp.dma_start(gW[:, :, :], T["L1_ffn_gW"].rearrange("(k p) e -> p k e", p=P)).then_inc(s_in, 16)
            sp.dma_start(gb[:, :], spread(T["L1_ffn_gb"], NW, NE)).then_inc(s_in, 16)

        @block.tensor
        def _(pe):
            pe.wait_ge(s_in, 32)
            for i in range(WIN):
                for k in range(KC):
                    last = nc.tensor.matmul(pg[:, i, :], YT[:, k, i, :], gW[:, k, :], start=k == 0, stop=k == KC - 1)
            last.then_inc(s_m, 1)

        @block.vector
        def _(dve):
            link = chained(dve, s_ch)
            dve.wait_ge(s_in, 32)
            dve.wait_ge(s_m, 1)
            link(nc.vector.tensor_tensor(G[:, :, :], pg[:, :, :], gb[:, :].unsqueeze(1).to_broadcast([NW, WIN, NE]), ALU.add))
            link(nc.vector.tensor_reduce(red[:, :], G[:, :, :], AX, ALU.max))
            nc.vector.tensor_tensor(G[:, :, :], G[:, :, :], wide, ALU.subtract).then_inc(s_x, 1)
            dve.wait_ge(s_e, 1)
            link(nc.vector.tensor_reduce(red[:, :], G[:, :, :], AX, ALU.add))
            link(nc.vector.reciprocal(red[:, :], red[:, :]))
            link(nc.vector.tensor_tensor(G[:, :, :], G[:, :, :], wide, ALU.mult))
            for e in range(NE):
                own = G[:, :, e:e + 1]
                if e:
                    link(nc.vector.tensor_tensor(cmp[:, :, 0:e], G[:, :, 0:e], own.to_broadcast([NW, WIN, e]), ALU.is_ge))
                link(nc.vector.tensor_tensor(cmp[:, :, e:NE], G[:, :, e:NE], own.to_broadcast([NW, WIN, NE - e]), ALU.is_gt))
                link(nc.vector.tensor_reduce(rank[:, :, e], cmp[:, :, :], AX, ALU.add))
            link(nc.vector.tensor_scalar(rank[:, :, :], rank[:, :, :], 2.0, None, ALU.is_lt))
            link(nc.vector.tensor_reduce(red[:, :], G[:, :, :], AX, ALU.max))
            nc.vector.tensor_tensor(G[:, :, :], G[:, :, :], wide, ALU.subtract).then_inc(s_x, 1)
            dve.wait_ge(s_e, 2)
            link(nc.vector.tensor_tensor(G[:, :, :], G[:, :, :], rank[:, :, :], ALU.mult))
            link(nc.vector.tensor_reduce(red[:, :], G[:, :, :], AX, ALU.add))
            link(nc.vector.reciprocal(red[:, :], red[:, :]))
            link(nc.vector.tensor_tensor(R.share[:, :, :], G[:, :, :], wide, ALU.mult))

        @block.scalar
        def _(act):
            for n in range(2):
                act.wait_ge(s_x, n + 1)
                nc.scalar.activation(G[:, :, :], G[:, :, :], ACT.Exp).then_inc(s_e, 1)


def expert_ffn(nc, K, T, X, YT, R):
    with ExitStack() as stack, nc.Block() as block:
        c = Ctx(nc, stack)
        sW1, sW2, sW3 = c.sb("ef_s1", [P, KC, D]), c.sb("ef_s2", [P, KC, P]), c.sb("ef_s3", [P, D])
        sb1, sb2, sb3 = c.sb("ef_sb1", [P, KC]), c.sb("ef_sb2", [P, 1]), c.sb("ef_sb3", [NW, D])
        eW1, eW2 = c.sb("ef_e1", [P, NE, KC, EH1]), c.sb("ef_e2", [P, NE, EH2])
        eW3 = c.sb("ef_e3", [EH2 + 1, NE, D])
        eb1, eb2 = c.sb("ef_eb1", [P, NE]), c.sb("ef_eb2", [EH2, NE])
        NN = NCK * NW
        h1 = [c.sb(f"ef_h1{b}", [P, KC + NE, NN]) for b in range(2)]
        h2 = [c.sb(f"ef_h2{b}", [P, NN]) for b in range(2)]
        e2 = [c.sb(f"ef_g2{b}", [EH2 + 1, NE, NN]) for b in range(2)]
        pu = [c.ps(f"ef_pu{b}", [P, 512]) for b in range(4)]
        po = [c.ps(f"ef_po{b}", [P, 512]) for b in range(3)]
        s_in, s_u, s_a, s_o, s_x, s_one, s_b = [c.sem("ef_s" + n) for n in ("in", "u", "a", "o", "x", "one", "b")]
        loads = [(sW1[:, :, :], T["L1_ffn_sW1"].rearrange("(k p) n -> p k n", p=P)),
                 (sW2[:, :, :], T["L1_ffn_sW2"].rearrange("(k p) n -> p k n", p=P)), (sW3[:, :], T["L1_ffn_sW3"]),
                 (sb1[:, :], T["L1_ffn_sb1"].rearrange("(k p) -> p k", p=P)), (sb2[:, :], T["L1_ffn_sb2"].unsqueeze(1)),
                 (sb3[:, :], spread(T["L1_ffn_sb3"], NW, D)),
                 (eW2[:, :, :], T["L1_ffn_eW2"].rearrange("e p n -> p e n")),
                 (eW3[0:EH2, :, :], T["L1_ffn_eW3"].rearrange("e p n -> p e n")),
                 (eW3[EH2:EH2 + 1, :, :], T["L1_ffn_eb3"].unsqueeze(0)),
                 (eb1[:, :], T["L1_ffn_eb1"].rearrange("e p -> p e")), (eb2[:, :], T["L1_ffn_eb2"].rearrange("e p -> p e"))]
        loads += [(eW1[:, e, :, :], T["L1_ffn_eW1"][e].rearrange("(k p) n -> p k n", p=P)) for e in range(NE)]
        L1, L2 = KC + NE, 1 + NE
        NU = L1 + L2

        @block.sync
        def _(sp):
            for dst, src in loads:
                sp.dma_start(dst, src).then_inc(s_in, 16)
            sp.wait_ge(s_in, 16 * len(loads))

        @block.tensor
        def _(pe):
            pe.wait_ge(s_in, 16 * len(loads))
            pe.wait_ge(s_one, 2)

            def unit(ck, u):
                n = ck * NU + u
                if n >= 4:
                    pe.wait_ge(s_a, n - 3)
                bank = pu[n % 4]
                cols = YT[:, :, ck * NCK:(ck + 1) * NCK, :].rearrange("p k a w -> p k (a w)")
                if u < L1:
                    for k in range(KC):
                        w = sW1[:, k, u * P:(u + 1) * P] if u < KC else eW1[:, u - KC, k, :]
                        last = nc.tensor.matmul(bank[:, 0:NN], w, cols[:, k, :], start=k == 0, stop=k == KC - 1)
                elif u == L1:
                    pe.wait_ge(s_a, ck * NU + L1)
                    for k in range(KC):
                        last = nc.tensor.matmul(bank[:, 0:NN], sW2[:, k, :], h1[ck % 2][:, k, :], start=k == 0, stop=k == KC - 1)
                else:
                    e = u - L1 - 1
                    last = nc.tensor.matmul(bank[0:EH2, 0:NN], eW2[:, e, :], h1[ck % 2][:, KC + e, :], start=True, stop=True)
                last.then_inc(s_u, 1)

            def outputs(ck):
                pe.wait_ge(s_a, (ck + 1) * NU)
                for a in range(NCK):
                    for v in range(1 + NE):
                        n = (ck * NCK + a) * (1 + NE) + v
                        if n >= 3:
                            pe.wait_ge(s_x, n - 2)
                        part = slice(a * NW, (a + 1) * NW)
                        o = po[n % 3][0:NW, 0:D]
                        if v == 0:
                            nc.tensor.matmul(o, h2[ck % 2][:, part], sW3[:, :], start=True, stop=True).then_inc(s_o, 1)
                        else:
                            nc.tensor.matmul(o, e2[ck % 2][:, v - 1, part], eW3[:, v - 1, :], start=True, stop=True).then_inc(s_o, 1)

            for ck in range(NCHK):
                for u in range(NU):
                    unit(ck, u)
                if ck:
                    outputs(ck - 1)
            outputs(NCHK - 1)

        @block.scalar
        def _(act):
            act.wait_ge(s_in, 16 * len(loads))
            for ck in range(NCHK):
                for u in range(NU):
                    n = ck * NU + u
                    act.wait_ge(s_u, n + 1)
                    if u == 0 and ck >= 2:
                        act.wait_ge(s_o, (ck - 1) * NCK * (1 + NE))
                    if u < L1:
                        dst, src = h1[ck % 2][:, u, :], pu[n % 4][:, 0:NN]
                        bias = sb1[:, u:u + 1] if u < KC else eb1[:, u - KC:u - KC + 1]
                    elif u == L1:
                        dst, src, bias = h2[ck % 2][:, :], pu[n % 4][:, 0:NN], sb2[:, :]
                    else:
                        e = u - L1 - 1
                        dst, src, bias = e2[ck % 2][0:EH2, e, :], pu[n % 4][0:EH2, 0:NN], eb2[:, e:e + 1]
                    nc.scalar.activation(dst, src, ACT.Relu, bias=bias).then_inc(s_a, 1)

        @block.gpsimd
        def _(pool):
            for b in range(2):
                nc.gpsimd.memset(e2[b][EH2:EH2 + 1, :, :], 1.0).then_inc(s_one, 1)

        @block.vector
        def _(dve):
            dve.wait_ge(s_in, 16 * len(loads))
            nc.vector.tensor_tensor(X[:, :, :], X[:, :, :], sb3[:, :].unsqueeze(1).to_broadcast([NW, WIN, D]), ALU.add).then_inc(s_b, 1)
            dve.wait_ge(s_b, 1)
            for i in range(WIN):
                for v in range(1 + NE):
                    n = i * (1 + NE) + v
                    dve.wait_ge(s_o, n + 1)
                    if n:
                        dve.wait_ge(s_x, n)
                    if v == 0:
                        nc.vector.tensor_tensor(X[:, i, :], X[:, i, :], po[n % 3][0:NW, 0:D], ALU.add).then_inc(s_x, 1)
                    else:
                        nc.vector.scalar_tensor_tensor(X[:, i, :], po[n % 3][0:NW, 0:D], R.share[:, i, v - 1:v], X[:, i, :],
                                                       ALU.mult, ALU.add).then_inc(s_x, 1)


def node_rows(ap):
    return ap.rearrange("(w i) d -> w i d", i=WIN)


def build(nc, T, out):
    Ctx.used.clear()
    with ExitStack() as stack:
        stack.enter_context(nc.allow_non_contiguous_dma(reason="biases of a few hundred elements, one per partition"))
        c = Ctx(nc, stack)
        K = Bag()
        K.ident = c.sb("identity", [P, P])
        K.ones = c.sb("ones", [P, P])
        K.before = c.sb("before", [P, P])
        K.iota = c.sb("iota_window", [P, WIN], BF16)
        K.part = c.sb("iota_partition", [P, 1])
        K.tile_no = c.sb("iota_tile", [P, NT])
        K.zeros_i = c.sb("zeros_i", [P, Scatter.NS], I32)
        K.zeros = c.sb("zeros", [P, Scatter.NS])
        K.zero_i = K.zeros_i[:, 0:GROUP]
        K.ready = c.sem("constants_ready")
        X = c.sb("x", [NW, WIN, D])
        constants(nc, K)

        R1 = Bag()
        R1.window_i = c.sb("wini1", [1, NT], I32)
        later = stack.enter_context(ExitStack())
        S1 = Scatter(Ctx(nc, later), "slots1", "s1")

        load_rows(nc, T, "x", [(X[:, :, :], node_rows(T["x"]))])
        with ExitStack() as st:
            c1 = Ctx(nc, st)
            R = Bag()
            R.window_i, R.begins = c1.sb("wini0", [1, NT], I32), c1.sb("begins0", [HW, NT])
            R.node, R.type, R.index = c1.sb("node0", [P, NT], BF16), c1.sb("type0", [P, NT], BF16), c1.sb("idx0", [P, NT], I32)
            with ExitStack() as inner:
                c2 = Ctx(nc, inner)
                S = Scatter(c2, "slots0", "s0")
                sort_edges(nc, K, T, "dst", [[("src", NREL), ("edge_type_8", 1)], [("edge_type_8", 1)]], "slots0", "bucket0", "s0", R, S)
                with ExitStack() as nodes:
                    c3 = Ctx(nc, nodes)
                    Y, YT = c3.sb("y0", [NW, WIN, D]), c3.sb("yt0", [P, KC, WIN, NW])
                    layernorm(nc, K, X, Y, "a")
                    transpose_nodes(nc, K, Y, YT, "a")
                    relation_features(nc, K, T, YT, S, 12)
                R1.begins = c2.sb("begins1", [HW, NT])
                sort_edges(nc, K, T, "src", [[("dst", 1)], [("edge_type_3", 1)]], "slots1", "bucket1", "s1", R1, S1, beside=(S, 3, 8))
                finish_scatter(nc, K, T, S)
                load_slots(nc, K, T, S, R, "s0")
            R.ev, R.negmax = c1.sb("ev", [P, NT, NH]), c1.sb("negmax", [HW, NT])
            edge_logits(nc, K, T, R)
            relation_attention(nc, K, T, R, X)

        with ExitStack() as st:
            c1 = Ctx(nc, st)
            R = Bag()
            Y, YT, R.gate = c1.sb("y1", [NW, WIN, D]), c1.sb("yt1", [P, KC, WIN, NW]), c1.sb("gate", [NW, WIN])
            layernorm(nc, K, X, Y, "b")
            token_weights(nc, K, T, Y, R, S1, 6)
            transpose_nodes(nc, K, Y, YT, "b")
            routed_ffn(nc, K, T, X, Y, YT, R, S1, 10)
        finish_scatter(nc, K, T, S1)
        later.close()
        R1.node, R1.type, R1.index = c.sb("node1", [P, NT], BF16), c.sb("type1", [P, NT], BF16), c.sb("idx1", [P, NT], I32)
        load_slots(nc, K, T, S1, R1, "s1")

        with ExitStack() as st:
            c1 = Ctx(nc, st)
            Y, YT = c1.sb("y2", [NW, WIN, D]), c1.sb("yt2", [P, KC, WIN, NW])
            WinT, b_in = c1.sb("win_t", [P, KC, D]), c1.sb("b_in", [NW, D])
            layernorm(nc, K, X, Y, "c")
            s_sum, s_park = c1.sem("residual"), c1.sem("parked")
            with nc.Block() as block:
                @block.vector
                def _(dve):
                    nc.vector.tensor_tensor(X[:, :, :], X[:, :, :], Y[:, :, :], ALU.add).then_inc(s_sum, 1)

                @block.sync
                def _(sp):
                    sp.wait_ge(s_sum, 1)
                    sp.dma_start(node_rows(T["park"]), X[:, :, :]).then_inc(s_park, 16)
                    sp.wait_ge(s_park, 16)
            load_rows(nc, T, "win", [(b_in[:, :], spread(T["L1_gnn_b_in"], NW, D))])
            load_transposed(nc, K, T, c1, "win", [(T["L1_gnn_Win"], WinT, P)])
            transpose_nodes(nc, K, Y, YT, "c")
            node_linear(nc, K, YT, WinT, b_in, X, "win")
        H = X
        message_layers(nc, K, T, R1, H)
        with ExitStack() as st:
            c1 = Ctx(nc, st)
            HT, B = c1.sb("ht_adj", [P, KC, WIN, NW]), c1.sb("adj", [NW, WIN, D])
            W1T, W2T = c1.sb("w1_t", [P, KC, D]), c1.sb("w2_t", [P, KC, D])
            b1, b2 = c1.sb("b1_adj", [NW, D]), c1.sb("b2_adj", [NW, D])
            load_rows(nc, T, "adj", [(b1[:, :], spread(T["L1_gnn_b1"], NW, D)), (b2[:, :], spread(T["L1_gnn_b2"], NW, D))])
            load_transposed(nc, K, T, c1, "adj", [(T["L1_gnn_W1"], W1T, P), (T["L1_gnn_W2"], W2T, P)])
            transpose_nodes(nc, K, H, HT, "adj1")
            node_linear(nc, K, HT, W1T, b1, B, "adj1", func="relu")
            load_rows(nc, T, "park", [(X[:, :, :], node_rows(T["park"]))])
            transpose_nodes(nc, K, B, HT, "adj2")
            node_linear(nc, K, HT, W2T, b2, B, "adj2", add=X)

        with ExitStack() as st:
            c1 = Ctx(nc, st)
            R = Bag()
            Y, YT, R.share = c1.sb("y3", [NW, WIN, D]), c1.sb("yt3", [P, KC, WIN, NW]), c1.sb("share", [NW, WIN, NE])
            layernorm(nc, K, X, Y, "d")
            transpose_nodes(nc, K, Y, YT, "d")
            expert_gates(nc, K, T, YT, R)
            expert_ffn(nc, K, T, X, YT, R)
        stored = c.sem("output_stored")
        with nc.Block() as block:
            @block.sync
            def _(sp):
                sp.dma_start(node_rows(out), X[:, :, :]).then_inc(stored, 16)
                sp.wait_ge(stored, 16)


SCRATCH = [("feat", (N_NODES * NREL, D), F32), ("logit0", (N_NODES * NREL, NH), F32), ("logit1", (N_NODES * NREL, NH), F32),
           ("bucket0", (N_EDGES,), BF16), ("bucket1", (N_EDGES,), BF16), ("slots0", (P * NT, 4), F32), ("slots1", (P * NT, 4), F32),
           ("order", (N_NODES,), F32), ("park", (N_NODES, D), F32), ("kv", (N_NODES, 2 * D), F32)]


def kernel(**inputs):
    import numpy as _np
    import concourse.bacc as _bacc
    from concourse import mybir as _mybir
    from concourse.bass_utils import run_bass_kernel_spmd as _run
    nc = _bacc.Bacc("TRN2", target_bir_lowering=False, num_devices=1)
    arrays, T = {}, {}
    for name, value in inputs.items():
        a = _np.ascontiguousarray(value)
        arrays[f"in_{name}"] = a
        T[name] = nc.dram_tensor(f"in_{name}", a.shape, _mybir.dt.from_np(a.dtype), kind="ExternalInput").ap()
    for name, shape, dt in SCRATCH:
        T[name] = nc.dram_tensor(f"scratch_{name}", shape, dt).ap()
    out = nc.dram_tensor("out_x", (N_NODES, D), F32, kind="ExternalOutput").ap()
    build(nc, T, out)
    r = _run(nc, [arrays], core_ids=[0])
    return r.results[0]["out_x"]
```
